# Optimizing a Trainium2 kernel written in Bass

```python
import numpy as np
import jax
import jax.numpy as jnp

def _softmax(x, axis=-1):
    return jax.nn.softmax(x, axis=axis)

def _gelu(x):
    return jax.nn.gelu(x, approximate=True)

def _silu(x):
    return jax.nn.silu(x)

def _sigmoid(x):
    return jax.nn.sigmoid(x)

def _layernorm(x, axis=-1, eps=1e-05):
    m = jnp.mean(x, axis=axis, keepdims=True)
    v = jnp.var(x, axis=axis, keepdims=True)
    return (x - m) / jnp.sqrt(v + eps)

def _scatter_add(tgt, idx, src, axis=0):
    return tgt.at[idx].add(src)

def _segment_sum(src, seg, n):
    return jax.ops.segment_sum(src, seg, n)
kernel_name = 'mk_hybrid_d1_jaxref_r8_ca2995'

def setup_inputs(seed: int=0):
    np.random.seed(seed)
    _w = jnp.asarray

    def _L0_attn_a_setup():
        import jax, jax.numpy as jnp
        import numpy as np
        B, S, E = (8, 128, 128)
        H = 16
        D = E // H

        def _split_heads(t, b, s):
            return t.reshape(b, s, H, D).transpose(0, 2, 1, 3)
        key = jax.random.key(seed)
        ks = jax.random.split(key, 5)
        scale = 1.0 / np.sqrt(E)
        return {'x': jax.random.normal(ks[0], (B, S, E), dtype=jnp.float32), 'Wq': jax.random.normal(ks[1], (E, E), dtype=jnp.float32) * scale, 'Wk': jax.random.normal(ks[2], (E, E), dtype=jnp.float32) * scale, 'Wv': jax.random.normal(ks[3], (E, E), dtype=jnp.float32) * scale, 'Wo': jax.random.normal(ks[4], (E, E), dtype=jnp.float32) * scale}
    _L0_attn_a_in = _L0_attn_a_setup()

    def _L0_attn_b_setup():
        import jax, jax.numpy as jnp
        import numpy as np
        DIM = 128
        H = 16
        DH = DIM // H
        K = 4
        B = 8
        N = 256
        EPS = 1e-06

        def _depthwise_conv_silu(x, w, n):
            pad = K // 2
            y = jax.lax.conv_general_dilated(x.transpose(0, 2, 1), w, window_strides=(1,), padding=[(pad, pad)], dimension_numbers=('NCH', 'OIH', 'NCH'), feature_group_count=x.shape[-1])
            y = y[..., :n]
            return jax.nn.silu(y).transpose(0, 2, 1)

        def _l2norm(x):
            return x / (jnp.linalg.norm(x, axis=-1, keepdims=True) + EPS)

        def _forward(x, Wq, bq, Wk, bk, Wv, bv, Wa, ba, Wb, bb, conv_q, conv_k, conv_v, Wo, bo):
            b_, n_, c_ = x.shape
            q = _l2norm(_depthwise_conv_silu(jax.nn.silu(x @ Wq.T + bq), conv_q, n_))
            k = _l2norm(_depthwise_conv_silu(jax.nn.silu(x @ Wk.T + bk), conv_k, n_))
            v = _depthwise_conv_silu(jax.nn.silu(x @ Wv.T + bv), conv_v, n_)
            a = jax.nn.sigmoid(x @ Wa.T + ba)
            bgate = jax.nn.sigmoid(x @ Wb.T + bb)
            q = q.reshape(b_, n_, H, DH).transpose(1, 0, 2, 3)
            k = k.reshape(b_, n_, H, DH).transpose(1, 0, 2, 3)
            v = v.reshape(b_, n_, H, DH).transpose(1, 0, 2, 3)
            a = a.transpose(1, 0, 2)
            bgate = bgate.transpose(1, 0, 2)
            S0 = jnp.zeros((b_, H, DH, DH), x.dtype)

            def step(S, inp):
                qt, kt, vt, at, bt = inp
                at = at[..., None, None]
                bt = bt[..., None, None]
                Sk = jnp.einsum('bhde,bhe->bhd', S, kt)
                outer_Sk_k = Sk[..., :, None] * kt[..., None, :]
                outer_v_k = vt[..., :, None] * kt[..., None, :]
                S_new = at * S - at * bt * outer_Sk_k + bt * outer_v_k
                ot = jnp.einsum('bhd,bhde->bhe', qt, S_new)
                return (S_new, ot)
            _, O = jax.lax.scan(step, S0, (q, k, v, a, bgate))
            O = O.transpose(1, 0, 2, 3).reshape(b_, n_, c_)
            return O @ Wo.T + bo
        key = jax.random.key(seed)
        ks = jax.random.split(key, 16)
        s = 1.0 / np.sqrt(DIM)
        d = dict(x=jax.random.normal(ks[0], (B, N, DIM), jnp.float32), Wq=jax.random.normal(ks[1], (DIM, DIM), jnp.float32) * s, bq=jnp.zeros((DIM,), jnp.float32), Wk=jax.random.normal(ks[2], (DIM, DIM), jnp.float32) * s, bk=jnp.zeros((DIM,), jnp.float32), Wv=jax.random.normal(ks[3], (DIM, DIM), jnp.float32) * s, bv=jnp.zeros((DIM,), jnp.float32), Wa=jax.random.normal(ks[4], (H, DIM), jnp.float32) * s, ba=jnp.zeros((H,), jnp.float32), Wb=jax.random.normal(ks[5], (H, DIM), jnp.float32) * s, bb=jnp.zeros((H,), jnp.float32), conv_q=jax.random.normal(ks[6], (DIM, 1, K), jnp.float32) * 0.5, conv_k=jax.random.normal(ks[7], (DIM, 1, K), jnp.float32) * 0.5, conv_v=jax.random.normal(ks[8], (DIM, 1, K), jnp.float32) * 0.5, Wo=jax.random.normal(ks[9], (DIM, DIM), jnp.float32) * s, bo=jnp.zeros((DIM,), jnp.float32))
        return d
    _L0_attn_b_in = _L0_attn_b_setup()

    def _L0_ffn_setup():
        import jax, jax.numpy as jnp
        import numpy as np
        NUM_EXPERTS = 8
        TOP_K = 2
        key = jax.random.key(seed)
        k1, k2, k3, k4, k5 = jax.random.split(key, 5)
        B, S, H, F, E = (4, 128, 128, 256, NUM_EXPERTS)
        return {'hidden_states': jax.random.normal(k1, (B, S, H), dtype=jnp.float32), 'gate_w': jax.random.normal(k2, (H, E), dtype=jnp.float32) * 0.02, 'w1': jax.random.normal(k3, (E, H, F), dtype=jnp.float32) * 0.02, 'w2': jax.random.normal(k4, (E, F, H), dtype=jnp.float32) * 0.02, 'w3': jax.random.normal(k5, (E, H, F), dtype=jnp.float32) * 0.02}
    _L0_ffn_in = _L0_ffn_setup()
    _d = {'L0_attn_a_x': _L0_attn_a_in['x'], 'L0_attn_a_Wq': _L0_attn_a_in['Wq'], 'L0_attn_a_Wk': _L0_attn_a_in['Wk'], 'L0_attn_a_Wv': _L0_attn_a_in['Wv'], 'L0_attn_a_Wo': _L0_attn_a_in['Wo'], 'L0_attn_b_Wq': _L0_attn_b_in['Wq'], 'L0_attn_b_bq': _L0_attn_b_in['bq'], 'L0_attn_b_Wk': _L0_attn_b_in['Wk'], 'L0_attn_b_bk': _L0_attn_b_in['bk'], 'L0_attn_b_Wv': _L0_attn_b_in['Wv'], 'L0_attn_b_bv': _L0_attn_b_in['bv'], 'L0_attn_b_Wa': _L0_attn_b_in['Wa'], 'L0_attn_b_ba': _L0_attn_b_in['ba'], 'L0_attn_b_Wb': _L0_attn_b_in['Wb'], 'L0_attn_b_bb': _L0_attn_b_in['bb'], 'L0_attn_b_conv_q': _L0_attn_b_in['conv_q'], 'L0_attn_b_conv_k': _L0_attn_b_in['conv_k'], 'L0_attn_b_conv_v': _L0_attn_b_in['conv_v'], 'L0_attn_b_Wo': _L0_attn_b_in['Wo'], 'L0_attn_b_bo': _L0_attn_b_in['bo'], 'L0_ffn_gate_w': _L0_ffn_in['gate_w'], 'L0_ffn_w1': _L0_ffn_in['w1'], 'L0_ffn_w2': _L0_ffn_in['w2'], 'L0_ffn_w3': _L0_ffn_in['w3']}
    _x0 = _d['L0_attn_a_x']
    _d['L0_attn_a_x'] = jax.random.normal(jax.random.fold_in(jax.random.key(seed), 1), (4, 1024, 128), dtype=_x0.dtype)
    del _x0
    return _d

def reference(L0_attn_a_x, L0_attn_a_Wq, L0_attn_a_Wk, L0_attn_a_Wv, L0_attn_a_Wo, L0_attn_b_Wq, L0_attn_b_bq, L0_attn_b_Wk, L0_attn_b_bk, L0_attn_b_Wv, L0_attn_b_bv, L0_attn_b_Wa, L0_attn_b_ba, L0_attn_b_Wb, L0_attn_b_bb, L0_attn_b_conv_q, L0_attn_b_conv_k, L0_attn_b_conv_v, L0_attn_b_Wo, L0_attn_b_bo, L0_ffn_gate_w, L0_ffn_w1, L0_ffn_w2, L0_ffn_w3):

    def _L0_attn_a_ref(x, Wq, Wk, Wv, Wo):
        import jax, jax.numpy as jnp
        import numpy as np
        B, S, E = (8, 128, 128)
        H = 16
        D = E // H

        def _split_heads(t, b, s):
            return t.reshape(b, s, H, D).transpose(0, 2, 1, 3)
        b, s, e = x.shape
        q = _split_heads(x @ Wq.T, b, s)
        k = _split_heads(x @ Wk.T, b, s)
        v = _split_heads(x @ Wv.T, b, s)
        d = q.shape[-1]
        q_c = q - q.mean(axis=-1, keepdims=True)
        k_c = k - k.mean(axis=-1, keepdims=True)
        cov = jnp.einsum('bhqd,bhkd->bhqk', q_c, k_c) / d
        q_var = (q_c * q_c).sum(axis=-1, keepdims=True) / (d - 1)
        k_var = (k_c * k_c).sum(axis=-1, keepdims=True) / (d - 1)
        var = jnp.einsum('bhqo,bhko->bhqk', q_var, k_var) / d
        attn = jax.nn.softmax(cov + var, axis=-1)
        out = jnp.einsum('bhqk,bhkd->bhqd', attn, v)
        out = out.transpose(0, 2, 1, 3).reshape(b, s, e)
        return out @ Wo.T

    def _L0_attn_b_ref(x, Wq, bq, Wk, bk, Wv, bv, Wa, ba, Wb, bb, conv_q, conv_k, conv_v, Wo, bo):
        import jax, jax.numpy as jnp
        import numpy as np
        DIM = 128
        H = 16
        DH = DIM // H
        K = 4
        B = 8
        N = 256
        EPS = 1e-06

        def _depthwise_conv_silu(x, w, n):
            pad = K // 2
            y = jax.lax.conv_general_dilated(x.transpose(0, 2, 1), w, window_strides=(1,), padding=[(pad, pad)], dimension_numbers=('NCH', 'OIH', 'NCH'), feature_group_count=x.shape[-1])
            y = y[..., :n]
            return jax.nn.silu(y).transpose(0, 2, 1)

        def _l2norm(x):
            return x / (jnp.linalg.norm(x, axis=-1, keepdims=True) + EPS)

        def _forward(x, Wq, bq, Wk, bk, Wv, bv, Wa, ba, Wb, bb, conv_q, conv_k, conv_v, Wo, bo):
            b_, n_, c_ = x.shape
            q = _l2norm(_depthwise_conv_silu(jax.nn.silu(x @ Wq.T + bq), conv_q, n_))
            k = _l2norm(_depthwise_conv_silu(jax.nn.silu(x @ Wk.T + bk), conv_k, n_))
            v = _depthwise_conv_silu(jax.nn.silu(x @ Wv.T + bv), conv_v, n_)
            a = jax.nn.sigmoid(x @ Wa.T + ba)
            bgate = jax.nn.sigmoid(x @ Wb.T + bb)
            q = q.reshape(b_, n_, H, DH).transpose(1, 0, 2, 3)
            k = k.reshape(b_, n_, H, DH).transpose(1, 0, 2, 3)
            v = v.reshape(b_, n_, H, DH).transpose(1, 0, 2, 3)
            a = a.transpose(1, 0, 2)
            bgate = bgate.transpose(1, 0, 2)
            S0 = jnp.zeros((b_, H, DH, DH), x.dtype)

            def step(S, inp):
                qt, kt, vt, at, bt = inp
                at = at[..., None, None]
                bt = bt[..., None, None]
                Sk = jnp.einsum('bhde,bhe->bhd', S, kt)
                outer_Sk_k = Sk[..., :, None] * kt[..., None, :]
                outer_v_k = vt[..., :, None] * kt[..., None, :]
                S_new = at * S - at * bt * outer_Sk_k + bt * outer_v_k
                ot = jnp.einsum('bhd,bhde->bhe', qt, S_new)
                return (S_new, ot)
            _, O = jax.lax.scan(step, S0, (q, k, v, a, bgate))
            O = O.transpose(1, 0, 2, 3).reshape(b_, n_, c_)
            return O @ Wo.T + bo
        return _forward(x, Wq, bq, Wk, bk, Wv, bv, Wa, ba, Wb, bb, conv_q, conv_k, conv_v, Wo, bo)

    def _L0_ffn_ref(hidden_states, gate_w, w1, w2, w3):
        import jax, jax.numpy as jnp
        import numpy as np
        NUM_EXPERTS = 8
        TOP_K = 2
        "Mixtral MoE block: router softmax -> top-2 -> SwiGLU expert FFN -> weighted combine.\n\n            Same math as Gmm (sort + grouped GEMM + scatter): each token passes through its\n            top-k experts' FFNs (silu(x@w1) * (x@w3)) @ w2, then the outputs are combined\n            with the renormalized top-k routing weights.\n            "
        B, S, H = hidden_states.shape
        E = w1.shape[0]
        x = hidden_states.reshape(-1, H)
        m = x.shape[0]
        router_logits = x @ gate_w
        probs = jax.nn.softmax(router_logits, axis=-1)
        top_w, top_i = jax.lax.top_k(probs, TOP_K)
        top_w = top_w / jnp.sum(top_w, axis=-1, keepdims=True)
        route = jnp.zeros((m, E), dtype=x.dtype)
        route = route.at[jnp.arange(m)[:, None], top_i].set(top_w)
        out = jnp.zeros_like(x)
        for e in range(E):
            h = jax.nn.silu(x @ w1[e]) * (x @ w3[e])
            out = out + route[:, e:e + 1] * (h @ w2[e])
        return out.reshape(B, S, H)
    x = L0_attn_a_x
    x = x + _L0_attn_a_ref(_layernorm(x, axis=-1), L0_attn_a_Wq, L0_attn_a_Wk, L0_attn_a_Wv, L0_attn_a_Wo)
    x = x + _L0_ffn_ref(_layernorm(x, axis=-1), L0_ffn_gate_w, L0_ffn_w1, L0_ffn_w2, L0_ffn_w3)
    x = x + _L0_attn_b_ref(_layernorm(x, axis=-1), L0_attn_b_Wq, L0_attn_b_bq, L0_attn_b_Wk, L0_attn_b_bk, L0_attn_b_Wv, L0_attn_b_bv, L0_attn_b_Wa, L0_attn_b_ba, L0_attn_b_Wb, L0_attn_b_bb, L0_attn_b_conv_q, L0_attn_b_conv_k, L0_attn_b_conv_v, L0_attn_b_Wo, L0_attn_b_bo)
    x = x + _L0_ffn_ref(_layernorm(x, axis=-1), L0_ffn_gate_w, L0_ffn_w1, L0_ffn_w2, L0_ffn_w3)
    return x

_drawn_inputs = setup_inputs


def setup_inputs(seed=0):
    import zlib

    import numpy as np

    out = dict(_drawn_inputs(seed))
    spreads = {'L0_attn_b_bq': (0.0, 0.8),
     'L0_attn_b_bk': (0.0, 0.8),
     'L0_attn_b_bv': (0.0, 0.8),
     'L0_attn_b_ba': (0.0, 0.8),
     'L0_attn_b_bb': (0.0, 0.8),
     'L0_attn_b_bo': (0.0, 0.36)}
    factors = {'L0_attn_b_Wq': 8.0,
     'L0_attn_b_Wk': 8.0,
     'L0_attn_b_Wv': 8.0,
     'L0_attn_b_Wa': 8.0,
     'L0_attn_b_Wb': 8.0,
     'L0_attn_b_conv_q': 8.0,
     'L0_attn_b_conv_k': 8.0,
     'L0_attn_b_conv_v': 8.0,
     'L0_attn_b_Wo': 8.0,
     'L0_ffn_gate_w': 5.683,
     'L0_ffn_w1': 4.95,
     'L0_ffn_w2': 4.93,
     'L0_ffn_w3': 4.926}
    for name, (base, spread) in spreads.items():
        noise = np.random.default_rng([zlib.crc32(name.encode()), seed]).standard_normal(out[name].shape)
        drawn = base * np.exp(spread * noise) if base else spread * noise
        out[name] = jnp.asarray(drawn.astype(out[name].dtype))
    for name, factor in factors.items():
        out[name] = (out[name] * factor).astype(out[name].dtype)
    return out
```

```python
from contextlib import ExitStack

import concourse.bass as bass
from concourse import mybir

F32 = mybir.dt.float32
BF16 = mybir.dt.bfloat16
ALU = mybir.AluOpType
ACT = mybir.ActivationFunctionType
AX = mybir.AxisListType

P = 128
H = 16
D = P // H
B = 4
S = 1024
N = B * S
NT = N // P
TB = S // P
CH = 512
NC_ = N // CH
CT = CH // P
LN_EPS = 1e-5
L2_EPS = 1e-6

NPART = 3
K1 = D + 1
R_ALL = NPART * NPART * K1
R_MAX = 96
R_END = R_MAX + NPART
GH = 4
NQ = H // GH
E, F = 8, 256
VW = D + 1


class Count:

    def __init__(self, eng, sem, start=0):
        self.eng, self.sem, self.n = eng, sem, start

    def done(self, ins):
        ins.then_inc(self.sem, 1)
        self.n = self.n + 1
        self.eng.wait_ge(self.sem, self.n)


def wait_used(eng, sem, value):
    if not (isinstance(value, int) and value <= 0):
        eng.wait_ge(sem, value)


def repeat(eng, n, body):
    body(0)
    with eng.Fori(1, n) as i:
        body(i)


class Mem:

    def __init__(self, nc, ctx, phase):
        self.nc, self.ctx, self.phase, self.used = nc, ctx, phase, []

    def sb(self, name, shape, dt=F32):
        return self.ctx.enter_context(self.nc.sbuf_tensor(f"{self.phase}_{name}", shape, dt))

    def ps(self, name, shape, dt=F32):
        return self.ctx.enter_context(self.nc.psum_tensor(f"{self.phase}_{name}", shape, dt))

    def sem(self, name):
        s = self.ctx.enter_context(self.nc.semaphore(f"{self.phase}_{name}"))
        self.used.append(s)
        return s

    def sems(self, name, n):
        return [self.sem(f"{name}{i}") for i in range(n)]

    def block(self):
        self.ctx.callback(self.clear)
        return self.ctx.enter_context(self.nc.Block())

    def clear(self):
        numbers = sorted(s.num for s in self.used)
        with self.nc.Block() as block:
            @block.sync
            def _(sp):
                first = last = numbers[0]
                for n in numbers[1:] + [-1]:
                    if n == last + 1:
                        last = n
                        continue
                    sp.sem_clear(range(first, last + 1))
                    first = last = n


def load_and_turn_weights(nc, g, ins):
    with ExitStack() as ctx:
        m = Mem(nc, ctx, "w")
        names = ["a_Wq", "a_Wk", "a_Wv", "a_Wo", "b_Wq", "b_Wk", "b_Wv", "b_Wo"]
        raw = m.sb("raw", [P, len(names), P])
        gates = m.sb("gates", [48, P])
        headsum = m.sb("headsum", [P, 2, H])
        headmean = m.sb("headmean", [P, 2, H])
        turned_ps = [m.ps(f"turned{i}", [P, CH]) for i in range(2)]
        gates_ps = m.ps("gates_ps", [P, CH])
        s_w = m.sem("w_loaded")
        s_x = m.sem("x_loaded")
        s_small = m.sem("small_loaded")
        s_id0 = m.sem("ident_cleared")
        s_id = m.sem("ident_ready")
        s_sel = m.sem("selectors")
        s_turned = m.sem("turned")
        s_gates = m.sem("gates_cleared")
        s_chain = m.sem("chain")

        block = m.block()

        @block.sync
        def _(sp):
            for i, n in enumerate(names):
                sp.dma_start(raw[:, i, :], ins[n]).then_inc(s_w, 16)
            xd = ins["a_x"].rearrange("b (t p) c -> p (b t) c", p=P)
            for i in range(4):
                sp.dma_start(g.x[:, i * TB:(i + 1) * TB, :], xd[:, i * TB:(i + 1) * TB, :]).then_inc(s_x, 16)
            for i, n in enumerate(["b_bq", "b_bk", "b_bv"]):
                sp.dma_start(g.bias_qkv[:, i:i + 1], ins[n].rearrange("(c o) -> c o", o=1)).then_inc(s_small, 16)
            for i, n in enumerate(["b_conv_q", "b_conv_k", "b_conv_v"]):
                sp.dma_start(g.conv[:, i, :], ins[n].rearrange("c o k -> c (o k)")).then_inc(s_small, 16)
            sp.wait_ge(s_gates, 2)
            sp.dma_start(gates[0:H, :], ins["b_Wa"]).then_inc(s_w, 16)
            sp.dma_start(gates[32:32 + H, :], ins["b_Wb"]).then_inc(s_w, 16)
            sp.dma_start(g.bias_ab[0:H, :], ins["b_ba"].rearrange("(c o) -> c o", o=1)).then_inc(s_small, 16)
            sp.dma_start(g.bias_ab[32:32 + H, :], ins["b_bb"].rearrange("(c o) -> c o", o=1)).then_inc(s_small, 16)
            sp.dma_start(g.bo_row[:, :], ins["b_bo"].rearrange("(o c) -> o c", o=1)).then_inc(s_small, 16)
            sp.dma_start(g.gate_w[:, :], ins["f_gate_w"]).then_inc(s_small, 16)
            sp.wait_ge(s_x, 64)
            sp.wait_ge(s_small, 16 * 10)

        @block.gpsimd
        def _(pool):
            pool.memset(gates[:, :], 0.0).then_inc(s_gates, 1)
            pool.memset(g.bias_ab[:, :], 0.0).then_inc(s_gates, 1)
            pool.memset(g.ident[:, :], 0.0).then_inc(s_id0, 1)
            pool.memset(g.ones[:, :], 1.0).then_inc(s_id0, 1)
            pool.memset(g.varsel[:, :, :], 0.0).then_inc(s_id0, 1)
            pool.wait_ge(s_id0, 3)
            pool.affine_select(out=g.ident[:, :], in_=g.ident[:, :], compare_op=ALU.not_equal, fill=1.0,
                               base=0, pattern=[[-1, P]], channel_multiplier=1).then_inc(s_id, 1)
            for d in range(D):
                for i, w in enumerate([D / (D - 1), 1.0 / (D - 1)]):
                    v = g.varsel[:, i, 32 * i:32 * i + H]
                    pool.wait_ge(s_sel, 2 * d + i)
                    pool.affine_select(out=v, in_=v, compare_op=ALU.not_equal, fill=w, base=-H * d,
                                       pattern=[[-1, H]], channel_multiplier=1).then_inc(s_sel, 1)

        @block.tensor
        def _(pe):
            pe.wait_ge(s_id, 1)
            pe.wait_ge(s_w, 16 * 10)
            for i in range(8):
                mm = pe.transpose(turned_ps[i // 4][:, (i % 4) * P:(i % 4 + 1) * P], raw[:, i, :], g.ident[:, :])
            mm.then_inc(s_turned, 1)
            pe.transpose(gates_ps[:, 0:48], gates[:, :], g.ident[0:48, 0:48]).then_inc(s_turned, 1)

        @block.vector
        def _(dve):
            chain = Count(dve, s_chain)
            dve.wait_ge(s_turned, 2)
            dve.tensor_copy(g.wT[:, 2:4, :], turned_ps[0][:, 2 * P:4 * P])
            dve.tensor_copy(g.wT[:, 4:8, :], turned_ps[1][:, :])
            dve.tensor_copy(g.gatesT[:, :], gates_ps[:, 0:48])
            qk = turned_ps[0][:, 0:2 * P].rearrange("p (w h d) -> p w h d", w=2, h=H)
            chain.done(dve.tensor_reduce(headsum[:, :, :], qk, AX.X, ALU.add))
            chain.done(dve.tensor_scalar(headmean[:, :, :], headsum[:, :, :], 1.0 / D, None, ALU.mult))
            chain.done(dve.tensor_tensor(g.wT[:, 0:2, :].rearrange("p w (d h) -> p w h d", h=H), qk,
                                         headmean[:, :, :].unsqueeze(3).to_broadcast([P, 2, H, D]), ALU.subtract))
            dve.tensor_scalar(g.wT[:, 0, :], g.wT[:, 0, :], 1.0 / D, None, ALU.mult)


def layer_norm_stats(nc, g, phase):
    with ExitStack() as ctx:
        m = Mem(nc, ctx, phase)
        stats = m.sb("stats", [P, NT, 6])
        msum = m.sb("msum", [P, NT])
        mdiff = m.sb("mdiff", [P, NT])
        m2 = m.sb("m2", [P, NT])
        var = m.sb("var", [P, NT])
        std = m.sb("std", [P, NT])
        eps = m.sb("eps", [P, 1])
        s_stats = m.sem("stats")
        s_eps = m.sem("eps")
        s_chain = m.sem("chain")
        s_var = m.sem("var")
        s_std = m.sem("std")
        s_rstd = m.sem("rstd")
        block = m.block()

        @block.vector
        def _(dve):
            dve.memset(eps[:, :], LN_EPS).then_inc(s_eps, 1)
            with dve.Fori(0, NT) as t:
                dve.bn_stats(stats[:, t, :], g.x[:, t, :]).then_inc(s_stats, 1)
            dve.wait_ge(s_stats, NT)
            chain = Count(dve, s_chain)
            dve.tensor_tensor(msum[:, :], stats[:, :, 1], stats[:, :, 4], ALU.add)
            chain.done(dve.tensor_tensor(mdiff[:, :], stats[:, :, 1], stats[:, :, 4], ALU.subtract))
            dve.tensor_tensor(m2[:, :], stats[:, :, 2], stats[:, :, 5], ALU.add)
            chain.done(dve.scalar_tensor_tensor(out=var[:, :], in0=mdiff[:, :], scalar=0.25 * P,
                                                in1=mdiff[:, :], op0=ALU.mult, op1=ALU.mult))
            dve.tensor_tensor(var[:, :], var[:, :], m2[:, :], ALU.add).then_inc(s_var, 1)
            dve.wait_ge(s_std, 1)
            dve.reciprocal(g.rstd[:, :], std[:, :]).then_inc(s_rstd, 1)
            dve.wait_ge(s_rstd, 1)
            dve.scalar_tensor_tensor(out=g.nmr[:, :], in0=msum[:, :], scalar=-0.5, in1=g.rstd[:, :],
                                     op0=ALU.mult, op1=ALU.mult)

        @block.scalar
        def _(act):
            act.wait_ge(s_eps, 1)
            act.wait_ge(s_var, 1)
            act.activation(std[:, :], var[:, :], ACT.Sqrt, bias=eps[:, :], scale=1.0 / P).then_inc(s_std, 1)


def project_qkv(nc, g, scr):
    with ExitStack() as ctx:
        m = Mem(nc, ctx, "qkv")
        xn = m.sb("xn", [P, 2, CT, P])
        xnT = m.sb("xnT", [P, 2, CH])
        parts = [m.sb(f"parts_{w}", [P, 2, NPART, CH], BF16) for w in "qk"]
        square = [m.sb(f"square_{w}", [P, 2, CH]) for w in "qk"]
        rest = [m.sb(f"rest_{w}", [P, 2, CH]) for w in "qk"]
        vparts = m.sb("vparts", [48, 2, NPART, CH], BF16)
        vrest = m.sb("vrest", [48, 2, CH])
        ps_x = m.ps("ps_x", [P, CH])
        ps_qk = [[m.ps(f"ps_{w}{p}", [P, CH]) for p in range(2)] for w in "qk"]
        ps_v = m.ps("ps_v", [P, CH])
        ps_var = m.ps("ps_var", [P, CH])

        s_xn = m.sems("xn", 2)
        s_turn = m.sems("turned", 2)
        s_xnT = m.sems("xnT", 2)
        s_proj = [m.sems(f"proj_{w}", 2) for w in "qk"]
        s_v = m.sems("v", 2)
        s_vout = m.sems("v_out", 2)
        s_sq = [m.sems(f"square_{w}", 2) for w in "qk"]
        s_p1 = [m.sems(f"part1_{w}", 2) for w in "qk"]
        s_r = [m.sems(f"rest_{w}", 2) for w in "qk"]
        s_p2 = [m.sems(f"part2_{w}", 2) for w in "qk"]
        s_p3 = [m.sems(f"part3_{w}", 2) for w in "qk"]
        s_var = m.sems("var", 2)
        s_v1 = m.sems("vpart1_", 2)
        s_vr = m.sems("vrest", 2)
        s_v2 = m.sems("vpart2_", 2)
        s_v3 = m.sems("vpart3_", 2)
        s_out = m.sems("stored", 2)
        s_ones = m.sem("ones")
        NDMA = 4
        block = m.block()


        @block.gpsimd
        def _(pool):
            pool.memset(g.v1[:, :, :, D:VW], 1.0).then_inc(s_ones, 1)
            n = 1
            for op in (*g.q_op, *g.k_op):
                pool.wait_ge(s_ones, n)
                pool.memset(op[64:P, :, :].bitcast(mybir.dt.uint32), 0).then_inc(s_ones, 1)
                n += 1
            for op in g.k_op:
                pool.wait_ge(s_ones, n)
                pool.memset(op[R_MAX:R_END, :, :], 1.0).then_inc(s_ones, 1)
                n += 1

        @block.scalar
        def _(act):
            def body(i):
                for p in range(2):
                    wait_used(act, s_turn[p], i)
                    for t in range(CT):
                        tile = (2 * i + p) * CT + t
                        ins = act.activation(xn[:, p, t, :], g.x[:, bass.ds(tile, 1), :], ACT.Identity,
                                             bias=g.nmr[:, bass.ds(tile, 1)], scale=g.rstd[:, bass.ds(tile, 1)])
                    ins.then_inc(s_xn[p], 1)
                    wait_used(act, s_out[p], 16 * NDMA * i)
                    for w in range(2):
                        act.wait_ge(s_proj[w][p], i + 1)
                        wait_used(act, s_var[p], i)
                        act.activation(square[w][:, p, :], ps_qk[w][p][:, :], ACT.Square).then_inc(s_sq[w][p], 1)
                        act.activation(parts[w][:, p, 0, :], ps_qk[w][p][:, :], ACT.Copy).then_inc(s_p1[w][p], 1)
                    for w in range(2):
                        act.wait_ge(s_r[w][p], i + 1)
                        act.activation(parts[w][:, p, 1, :], rest[w][:, p, :], ACT.Copy).then_inc(s_p2[w][p], 1)
                    act.wait_ge(s_var[p], i + 1)
                    act.activation(vparts[:, p, 0, :], ps_var[0:48, :], ACT.Copy).then_inc(s_v1[p], 1)
                    act.wait_ge(s_vr[p], i + 1)
                    act.activation(vparts[:, p, 1, :], vrest[:, p, :], ACT.Copy).then_inc(s_v2[p], 1)
            repeat(act, NC_ // 2, body)

        @block.tensor
        def _(pe):
            def body(i):
                for p in range(2):
                    pe.wait_ge(s_xn[p], i + 1)
                    wait_used(pe, s_xnT[1 - p], i + p)
                    for t in range(CT):
                        mm = pe.transpose(ps_x[:, t * P:(t + 1) * P], xn[:, p, t, :], g.ident[:, :])
                    mm.then_inc(s_turn[p], 1)
                    pe.wait_ge(s_xnT[p], i + 1)
                    for w in range(2):
                        wait_used(pe, s_r[w][p], i)
                        pe.matmul(ps_qk[w][p][:, :], g.wT[:, w, :], xnT[:, p, :], start=True,
                                  stop=True).then_inc(s_proj[w][p], 1)
                    wait_used(pe, s_vout[1 - p], i + p)
                    for t in range(CT):
                        mm = pe.matmul(ps_v[:, t * P:(t + 1) * P], xnT[:, p, t * P:(t + 1) * P], g.wT[:, 2, :],
                                       start=True, stop=True)
                    mm.then_inc(s_v[p], 1)
                    wait_used(pe, s_vr[1 - p], i + p)
                    for w in range(2):
                        pe.wait_ge(s_sq[w][p], i + 1)
                        mm = pe.matmul(ps_var[0:48, :], g.varsel[:, w, :], square[w][:, p, :],
                                       start=(w == 0), stop=(w == 1))
                    mm.then_inc(s_var[p], 1)
            repeat(pe, NC_ // 2, body)

        @block.vector
        def _(dve):
            dve.wait_ge(s_ones, 1)
            def body(i):
                for p in range(2):
                    dve.wait_ge(s_turn[p], i + 1)
                    wait_used(dve, s_v[p], i)
                    dve.tensor_copy(xnT[:, p, :], ps_x[:, :]).then_inc(s_xnT[p], 1)
                    for w in range(2):
                        dve.wait_ge(s_p1[w][p], i + 1)
                        dve.tensor_tensor(rest[w][:, p, :], ps_qk[w][p][:, :], parts[w][:, p, 0, :],
                                          ALU.subtract).then_inc(s_r[w][p], 1)
                    dve.wait_ge(s_v[p], i + 1)
                    for t in range(CT):
                        ins = dve.tensor_copy(g.v1[:, bass.ds((2 * i + p) * CT + t, 1), :, 0:D],
                                              ps_v[:, t * P:(t + 1) * P].rearrange("p (h d) -> p h d", h=H))
                    ins.then_inc(s_vout[p], 1)
                    for w in range(2):
                        dve.wait_ge(s_p2[w][p], i + 1)
                        dve.tensor_tensor(parts[w][:, p, 2, :], rest[w][:, p, :], parts[w][:, p, 1, :],
                                          ALU.subtract).then_inc(s_p3[w][p], 1)
                    dve.wait_ge(s_v1[p], i + 1)
                    dve.tensor_tensor(vrest[:, p, :], ps_var[0:48, :], vparts[:, p, 0, :],
                                      ALU.subtract).then_inc(s_vr[p], 1)
                    dve.wait_ge(s_v2[p], i + 1)
                    dve.tensor_tensor(vparts[:, p, 2, :], vrest[:, p, :], vparts[:, p, 1, :],
                                      ALU.subtract).then_inc(s_v3[p], 1)
            repeat(dve, NC_ // 2, body)

        @block.sync
        def _(sp):
            def body(i):
                for p in range(2):
                    at = (2 * i + p) * CH
                    for w in range(2):
                        sp.wait_ge(s_p3[w][p], i + 1)
                        sp.dma_start(scr.terms[w][:, 0:D, :, bass.ds(at, CH)].rearrange("i d h t -> (d h) i t"),
                                     parts[w][:, p, :, :]).then_inc(s_out[p], 16)
                    sp.wait_ge(s_v3[p], i + 1)
                    for w in range(2):
                        sp.dma_start(scr.terms[w][:, D, :, bass.ds(at, CH)].rearrange("i h t -> h i t"),
                                     vparts[32 * w:32 * w + H, p, :, :]).then_inc(s_out[p], 16)
            repeat(sp, NC_ // 2, body)
            for p in range(2):
                sp.wait_ge(s_out[p], 16 * NDMA * (NC_ // 2))


LEAD = 6
STEPS = GH * TB


def attend(nc, g, scr):
    with ExitStack() as ctx:
        m = Mem(nc, ctx, "att")
        q_op, k_op = g.q_op, g.k_op
        probs = m.sb("probs", [P, 8, CH])
        vq = m.sb("vq", [P, 2, TB, 64])
        negmax = m.sb("negmax", [P, 2, STEPS])
        nm_rows = m.sb("nm_rows", [STEPS, P])
        nm_rest = m.sb("nm_rest", [STEPS, P])
        nm_parts = m.sb("nm_parts", [STEPS, 2, NPART, P], BF16)
        acc_sb = m.sb("acc_sb", [P, 2, CH])
        rsum = m.sb("rsum", [P, 2, CT, GH])
        ps_max = m.ps("ps_max", [P, 2, S])
        ps_prob = m.ps("ps_prob", [P, 2, CH])
        ps_acc = m.ps("ps_acc", [P, CH])
        ps_misc = m.ps("ps_misc", [P, CH])
        comb = ps_misc[:, P:P + CT * GH * VW].rearrange("p (t g r) -> p t g r", t=CT, g=GH)

        s_clear = m.sem("cleared")
        s_load = m.sems("loaded", NQ)
        s_scored = m.sem("scored")
        s_maxed = m.sem("maxed")
        s_nmT = m.sem("negmax_turned")
        s_nmch = m.sem("negmax_chain")
        s_nmp = m.sem("negmax_parts")
        s_nmrow = m.sem("negmax_rows")
        s_prob = m.sem("prob_scored")
        s_exp = m.sem("exped")
        s_vq = m.sem("v_staged")
        s_pv = m.sem("pv")
        s_acc = m.sem("acc_copied")
        s_comb = m.sem("combined")
        s_rsum = m.sem("rsum")
        s_misc = m.sem("misc_read")
        last_b = B - 1

        def batches(eng, body):
            body(0, True, False)
            with eng.Fori(1, last_b) as b:
                body(b, False, False)
            body(last_b, False, True)

        def prev(b, s):
            return (b, s - 1) if s else (b - 1, NQ - 1)

        def nxt(b, s, k):
            return (b, s + k) if s + k < NQ else (b + 1, s + k - NQ)

        block = m.block()

        @block.gpsimd
        def _(pool):
            pool.memset(vq[:, :, :, :], 0.0).then_inc(s_clear, 1)
            pool.wait_ge(s_clear, 1)

            def body(b, first, last):
                for s in range(NQ):
                    if not (first and s == 0):
                        pool.wait_ge(s_vq, NQ * b + s)
                    if not (first and s < 2):
                        pool.wait_ge(s_pv, 2 * TB * (NQ * b + s - 1))
                    pool.tensor_copy(vq[:, s % 2, :, 0:GH * VW],
                                     g.v1[:, bass.ds(b * TB, TB), s * GH:(s + 1) * GH, :].rearrange(
                                         "p t g r -> p t (g r)")).then_inc(s_vq, 1)
            batches(pool, body)

        @block.sync
        def _(sp):
            def load(b, s):
                heads = slice(s * GH, (s + 1) * GH)
                tok = bass.ds(b * S, S)
                for i in range(NPART):
                    row = i * NPART * K1
                    sp.dma_start(k_op[s][row:row + NPART * K1, :, :],
                                 scr.terms[1][:, :, heads, tok].rearrange("j d h t -> (j d) h t")
                                 ).then_inc(s_load[s], 16)
                    for j in range(NPART):
                        sp.dma_start(q_op[s][row + j * K1:row + (j + 1) * K1, :, :],
                                     scr.terms[0][i, :, heads, tok]).then_inc(s_load[s], 16)

            def max_rows(u, s):
                sp.wait_ge(s_nmp, u + 1)
                for i in range(NPART):
                    sp.dma_start(q_op[s][R_MAX + i:R_MAX + i + 1, :, :].rearrange("o g t -> o (g t)"),
                                 nm_parts[:, s % 2, i, :]).then_inc(s_nmrow, 16)

            for s in range(NQ):
                load(0, s)
            max_rows(0, 0)

            def body(b, first, last):
                for s in range(NQ):
                    if not (last and s == NQ - 1):
                        max_rows(NQ * b + s + 1, (s + 1) % NQ)
                    if not last:
                        sp.wait_ge(s_prob, 2 * STEPS * (NQ * b + s + 1))
                        load(b + 1, s)
            batches(sp, body)

        LOADS = 16 * (NPART + NPART * NPART)

        @block.tensor
        def _(pe):
            def scores_for_max(b, s, a):
                u = NQ * b + s
                if a == 0:
                    pe.wait_ge(s_load[s], LOADS * (b + 1))
                if not (isinstance(b, int) and b == 0 and s == 0 and a < 2):
                    pe.wait_ge(s_maxed, STEPS * u + a - 1)
                h, qt = a // TB, a % TB
                for k in range(S // CH):
                    mm = pe.matmul(ps_max[:, a % 2, k * CH:(k + 1) * CH],
                                   q_op[s][0:R_ALL, h, qt * P:(qt + 1) * P],
                                   k_op[s][0:R_ALL, h, k * CH:(k + 1) * CH], start=True, stop=True)
                mm.then_inc(s_scored, 1)

            def scores_for_prob(b, s, j):
                u = NQ * b + s
                half, kt, h = j // STEPS, j % STEPS // GH, j % GH
                if j == 0:
                    pe.wait_ge(s_nmrow, 16 * NPART * (u + 1))
                if not (isinstance(b, int) and b == 0 and s == 0 and j < 2):
                    pe.wait_ge(s_exp, 2 * STEPS * u + j - 1)
                pe.matmul(ps_prob[:, j % 2, :], k_op[s][0:R_END, h, kt * P:(kt + 1) * P],
                          q_op[s][0:R_END, h, half * CH:(half + 1) * CH], start=True,
                          stop=True).then_inc(s_prob, 1)

            def pv(b, s, v):
                u = NQ * b + s
                half, kt = v // TB, v % TB
                pe.wait_ge(s_exp, 2 * STEPS * u + GH * (v + 1))
                if v == 0:
                    pe.wait_ge(s_vq, u + 1)
                if kt == 0 and not (isinstance(b, int) and b == 0 and s == 0 and half == 0):
                    pe.wait_ge(s_acc, 2 * u + half)
                for h in range(GH):
                    mm = pe.matmul(ps_acc[32 * h:32 * h + 32, :], vq[:, s % 2, kt, VW * h:VW * h + 32],
                                   probs[:, (GH * v + h) % 8, :], start=(kt == 0), stop=(kt == TB - 1))
                mm.then_inc(s_pv, 1)

            def combine(b, s, half, last=False):
                u = NQ * b + s
                pe.wait_ge(s_acc, 2 * u + half + 1)
                pe.wait_ge(s_misc, 3 * u + 1 + 2 * half - last)
                for t in range(CT):
                    mm = pe.matmul(comb[:, t], acc_sb[:, half, t * P:(t + 1) * P],
                                   g.ident[:, :].rearrange("p (g r) -> p g r", g=GH)[:, :, 0:VW],
                                   start=True, stop=True)
                mm.then_inc(s_comb, 1)

            def turn_max(b, s):
                u = NQ * b + s
                pe.wait_ge(s_maxed, STEPS * (u + 1))
                if not (isinstance(b, int) and b == 0 and s == 0):
                    pe.wait_ge(s_misc, 3 * u - 1)
                pe.transpose(ps_misc[0:STEPS, 0:P], negmax[:, s % 2, :], g.ident[:, :]).then_inc(s_nmT, 1)

            for a in range(STEPS):
                scores_for_max(0, 0, a)
            turn_max(0, 0)
            for a in range(LEAD):
                scores_for_max(0, 1, a)

            def body(b, first, last):
                for s in range(NQ):
                    for i in range(STEPS):
                        a = i + LEAD
                        k, a = (1, a) if a < STEPS else (2, a - STEPS)
                        if not (last and s + k >= NQ):
                            scores_for_max(*nxt(b, s, k), a)
                        scores_for_prob(b, s, 2 * i)
                        scores_for_prob(b, s, 2 * i + 1)
                        if i % 2 == 1:
                            if i > 1:
                                pv(b, s, i // 2 - 1)
                            elif not (first and s == 0):
                                pv(*prev(b, s), 2 * TB - 1)
                        if i == 4 and not (first and s == 0):
                            combine(*prev(b, s), 1)
                        if i == 20:
                            combine(b, s, 0)
                        if i == STEPS - LEAD + 1 and not (last and s == NQ - 1):
                            turn_max(*nxt(b, s, 1))
            batches(pe, body)
            pv(last_b, NQ - 1, 2 * TB - 1)
            combine(last_b, NQ - 1, 1, last=True)

        @block.scalar
        def _(act):
            def body(b, first, last):
                for s in range(NQ):
                    u = NQ * b + s
                    for j in range(2 * STEPS):
                        act.wait_ge(s_prob, 2 * STEPS * u + j + 1)
                        if not (first and s == 0 and j < 8):
                            if j % GH == 0:
                                act.wait_ge(s_pv, 2 * TB * u + j // GH - 1)
                        act.activation(probs[:, j % 8, :], ps_prob[:, j % 2, :], ACT.Exp).then_inc(s_exp, 1)
            batches(act, body)

        @block.vector
        def _(dve):
            def reduce_max(b, s, a):
                dve.wait_ge(s_scored, STEPS * (NQ * b + s) + a + 1)
                dve.tensor_reduce(negmax[:, s % 2, a:a + 1], ps_max[:, a % 2, :], AX.X, ALU.max,
                                  negate=True).then_inc(s_maxed, 1)

            def split_max(b, s):
                u = NQ * b + s
                dve.wait_ge(s_nmT, u + 1)
                if not (isinstance(b, int) and b == 0 and s < 2):
                    dve.wait_ge(s_nmrow, 16 * NPART * (u - 1))
                chain = Count(dve, s_nmch, 4 * u)
                rows, rest, parts = nm_rows[:, :], nm_rest[:, :], nm_parts[:, s % 2]
                ins = dve.tensor_copy(rows, ps_misc[0:STEPS, 0:P])
                ins.then_inc(s_misc, 1)
                dve.wait_ge(s_misc, 1 if isinstance(u, int) and u == 0 else 3 * u)
                chain.done(dve.tensor_copy(parts[:, 0, :], rows))
                chain.done(dve.tensor_tensor(rest, rows, parts[:, 0, :], ALU.subtract))
                chain.done(dve.tensor_copy(parts[:, 1, :], rest))
                chain.done(dve.tensor_tensor(rows, rest, parts[:, 1, :], ALU.subtract))
                dve.tensor_copy(parts[:, 2, :], rows).then_inc(s_nmp, 1)

            def copy_acc(b, s, half):
                u = NQ * b + s
                dve.wait_ge(s_pv, 2 * TB * u + TB * (half + 1))
                if not (isinstance(b, int) and b == 0 and s == 0):
                    dve.wait_ge(s_comb, 2 * u + half - 1)
                dve.tensor_copy(acc_sb[:, half, :], ps_acc[:, :]).then_inc(s_acc, 1)

            def normalise(b, s, half):
                u = NQ * b + s
                dve.wait_ge(s_comb, 2 * u + half + 1)
                dve.reciprocal(rsum[:, half, :, :], comb[:, :, :, D]).then_inc(s_rsum, 1)
                dve.wait_ge(s_rsum, 2 * u + half + 1)
                for t in range(CT):
                    tile = b * TB + half * CT + t
                    out = g.o[:, bass.ds(tile, 1), s * GH * D:(s + 1) * GH * D].rearrange(
                        "p o (g d) -> p (o g) d", g=GH)
                    ins = dve.tensor_tensor(out, comb[:, t, :, 0:D],
                                            rsum[:, half, t, :].unsqueeze(2).to_broadcast([P, GH, D]), ALU.mult)
                ins.then_inc(s_misc, 1)

            for a in range(STEPS):
                reduce_max(0, 0, a)
            split_max(0, 0)
            for a in range(LEAD):
                reduce_max(0, 1, a)

            def body(b, first, last):
                for s in range(NQ):
                    for i in range(STEPS):
                        a = i + LEAD
                        k, a = (1, a) if a < STEPS else (2, a - STEPS)
                        if not (last and s + k >= NQ):
                            reduce_max(*nxt(b, s, k), a)
                        if i == 2 and not (first and s == 0):
                            copy_acc(*prev(b, s), 1)
                        if i == 5 and not (first and s == 0):
                            normalise(*prev(b, s), 1)
                        if i == 18:
                            copy_acc(b, s, 0)
                        if i == 21:
                            normalise(b, s, 0)
                        if i == STEPS - LEAD + 2 and not (last and s == NQ - 1):
                            split_max(*nxt(b, s, 1))
            batches(dve, body)
            copy_acc(last_b, NQ - 1, 1)
            normalise(last_b, NQ - 1, 1)


def project_out_a(nc, g):
    with ExitStack() as ctx:
        m = Mem(nc, ctx, "oproj")
        stage = m.sb("stage", [P, 2, CT, P])
        oT = m.sb("oT", [P, 2, CH])
        ps_t = [m.ps(f"ps_t{p}", [P, CH]) for p in range(2)]
        ps_y = [m.ps(f"ps_y{p}", [P, CH]) for p in range(2)]
        s_st = m.sems("staged", 2)
        s_turn = m.sems("turned", 2)
        s_oT = m.sems("oT", 2)
        s_y = m.sems("y", 2)
        s_add = m.sems("added", 2)
        block = m.block()

        @block.scalar
        def _(act):
            def body(i):
                for p in range(2):
                    wait_used(act, s_turn[p], i)
                    act.activation(stage[:, p, :, :], g.o[:, bass.ds((2 * i + p) * CT, CT), :],
                                   ACT.Copy).then_inc(s_st[p], 1)
            repeat(act, NC_ // 2, body)

        @block.tensor
        def _(pe):
            def body(i):
                for p in range(2):
                    pe.wait_ge(s_st[p], i + 1)
                    wait_used(pe, s_oT[p], i)
                    for t in range(CT):
                        mm = pe.transpose(ps_t[p][:, t * P:(t + 1) * P], stage[:, p, t, :], g.ident[:, :])
                    mm.then_inc(s_turn[p], 1)
                    pe.wait_ge(s_oT[p], i + 1)
                    wait_used(pe, s_add[p], i)
                    for t in range(CT):
                        mm = pe.matmul(ps_y[p][:, t * P:(t + 1) * P], oT[:, p, t * P:(t + 1) * P],
                                       g.wT[:, 3, :], start=True, stop=True)
                    mm.then_inc(s_y[p], 1)
            repeat(pe, NC_ // 2, body)

        @block.vector
        def _(dve):
            def body(i):
                for p in range(2):
                    dve.wait_ge(s_turn[p], i + 1)
                    wait_used(dve, s_y[p], i)
                    dve.tensor_copy(oT[:, p, :], ps_t[p][:, :]).then_inc(s_oT[p], 1)
                for p in range(2):
                    dve.wait_ge(s_y[p], i + 1)
                    xc = g.x[:, bass.ds((2 * i + p) * CT, CT), :]
                    dve.tensor_tensor(xc, xc, ps_y[p][:, :].rearrange("p (t c) -> p t c", t=CT),
                                      ALU.add).then_inc(s_add[p], 1)
            repeat(dve, NC_ // 2, body)


def normalise_and_turn(nc, g, phase, xnT, logits=None):
    with ExitStack() as ctx:
        m = Mem(nc, ctx, phase)
        xn = m.sb("xn", [P, 2, CT, P])
        xnc = m.sb("xnc", [P, 2, CH])
        ps_t = [m.ps(f"ps_t{p}", [P, CH]) for p in range(2)]
        ps_l = [m.ps(f"ps_l{p}", [P, CT, E]) for p in range(2)]
        s_xn = m.sems("xn", 2)
        s_turn = m.sems("turned", 2)
        s_xnc = m.sems("xnc", 2)
        s_copy = m.sems("copied", 2)
        s_log = m.sems("logits", 2)
        s_lout = m.sems("logits_out", 2)
        block = m.block()

        @block.scalar
        def _(act):
            def body(i):
                for p in range(2):
                    wait_used(act, s_turn[p], i)
                    for t in range(CT):
                        tile = (2 * i + p) * CT + t
                        ins = act.activation(xn[:, p, t, :], g.x[:, bass.ds(tile, 1), :], ACT.Identity,
                                             bias=g.nmr[:, bass.ds(tile, 1)], scale=g.rstd[:, bass.ds(tile, 1)])
                    ins.then_inc(s_xn[p], 1)
                for p in range(2):
                    act.wait_ge(s_xnc[p], i + 1)
                    act.activation(xnT[:, bass.ds((2 * i + p) * CH, CH)], xnc[:, p, :],
                                   ACT.Copy).then_inc(s_copy[p], 1)
            repeat(act, NC_ // 2, body)

        @block.tensor
        def _(pe):
            def body(i):
                for p in range(2):
                    pe.wait_ge(s_xn[p], i + 1)
                    wait_used(pe, s_xnc[p], i)
                    for t in range(CT):
                        mm = pe.transpose(ps_t[p][:, t * P:(t + 1) * P], xn[:, p, t, :], g.ident[:, :])
                    mm.then_inc(s_turn[p], 1)
                if logits is None:
                    return
                for p in range(2):
                    pe.wait_ge(s_xnc[p], i + 1)
                    wait_used(pe, s_lout[p], i)
                    for t in range(CT):
                        mm = pe.matmul(ps_l[p][:, t, :], xnc[:, p, t * P:(t + 1) * P], g.gate_w[:, :],
                                       start=True, stop=True)
                    mm.then_inc(s_log[p], 1)
            repeat(pe, NC_ // 2, body)

        @block.vector
        def _(dve):
            def body(i):
                for p in range(2):
                    dve.wait_ge(s_turn[p], i + 1)
                    wait_used(dve, s_copy[p], i)
                    if logits is not None:
                        wait_used(dve, s_log[p], i)
                    dve.tensor_copy(xnc[:, p, :], ps_t[p][:, :]).then_inc(s_xnc[p], 1)
                if logits is None:
                    return
                for p in range(2):
                    dve.wait_ge(s_log[p], i + 1)
                    dve.tensor_copy(logits[:, bass.ds((2 * i + p) * CT, CT), :], ps_l[p][:, :, :]
                                    ).then_inc(s_lout[p], 1)
            repeat(dve, NC_ // 2, body)


def route_top2(nc, g, phase, logits, route):
    with ExitStack() as ctx:
        m = Mem(nc, ctx, phase)
        rank = m.sb("rank", [P, E])
        best = m.sb("best", [P, 2, NT])
        at = m.sb("at", [P, NT, E])
        index = m.sb("index", [P, 2, NT])
        hot = [m.sb(f"hot{i}", [P, NT, E]) for i in range(2)]
        left = m.sb("left", [P, NT, E])
        gap = m.sb("gap", [P, 2, NT])
        weight = m.sb("weight", [P, 2, NT])
        s_rank = m.sem("rank")
        s_chain = m.sem("chain")
        s_gap = m.sem("gap")
        s_weight = m.sem("weight")
        block = m.block()
        wide = lambda a: a.unsqueeze(2).to_broadcast([P, NT, E])

        @block.gpsimd
        def _(pool):
            pool.iota(rank[:, :], pattern=[[-1, E]], base=E, channel_multiplier=0,
                      allow_small_or_imprecise_dtypes=True).then_inc(s_rank, 1)

        @block.vector
        def _(dve):
            chain = Count(dve, s_chain)
            ranks = rank[:, :].unsqueeze(1).to_broadcast([P, NT, E])
            dve.wait_ge(s_rank, 1)
            for i, src in enumerate((logits, left)):
                chain.done(dve.tensor_reduce(best[:, i, :], src[:, :, :], AX.X, ALU.max))
                chain.done(dve.tensor_tensor(at[:, :, :], src[:, :, :], wide(best[:, i, :]), ALU.is_equal))
                chain.done(dve.tensor_tensor(at[:, :, :], at[:, :, :], ranks, ALU.mult))
                chain.done(dve.tensor_reduce(index[:, i, :], at[:, :, :], AX.X, ALU.max))
                chain.done(dve.tensor_tensor(hot[i][:, :, :], wide(index[:, i, :]), ranks, ALU.is_equal))
                if i == 0:
                    chain.done(dve.scalar_tensor_tensor(out=left[:, :, :], in0=hot[0][:, :, :], scalar=-3e38,
                                                        in1=logits[:, :, :], op0=ALU.mult, op1=ALU.add))
            dve.tensor_tensor(gap[:, 0, :], best[:, 0, :], best[:, 1, :], ALU.subtract).then_inc(s_gap, 1)
            dve.tensor_tensor(gap[:, 1, :], best[:, 1, :], best[:, 0, :], ALU.subtract).then_inc(s_gap, 1)
            dve.wait_ge(s_weight, 1)
            chain.done(dve.tensor_tensor(hot[0][:, :, :], hot[0][:, :, :], wide(weight[:, 0, :]), ALU.mult))
            chain.done(dve.tensor_tensor(hot[1][:, :, :], hot[1][:, :, :], wide(weight[:, 1, :]), ALU.mult))
            dve.tensor_tensor(route[:, :, :], hot[0][:, :, :], hot[1][:, :, :], ALU.add)

        @block.scalar
        def _(act):
            act.wait_ge(s_gap, 2)
            act.activation(weight[:, :, :], gap[:, :, :], ACT.Sigmoid).then_inc(s_weight, 1)


def moe(nc, g, ins, phase, xnT, route):
    with ExitStack() as ctx:
        m = Mem(nc, ctx, phase)
        MF = F // P
        w1 = m.sb("w1", [P, E, F])
        w3 = m.sb("w3", [P, E, F])
        w2 = m.sb("w2", [P, E, MF, P])
        gate = m.sb("gate", [P, MF, CH])
        hT = m.sb("hT", [P, 2, MF, CH])
        ps_1 = [m.ps(f"ps_1{i}", [P, CH]) for i in range(MF)]
        ps_3 = [m.ps(f"ps_3{i}", [P, CH]) for i in range(MF)]
        ps_y = [m.ps(f"ps_y{i}", [P, CT, P]) for i in range(2)]
        s_w13 = m.sem("w13_loaded")
        s_w2 = m.sem("w2_loaded")
        s_1 = m.sem("h1")
        s_3 = m.sem("h3")
        s_silu = m.sem("silu")
        s_h = m.sem("h")
        s_y = m.sem("y")
        s_add = m.sem("added")
        block = m.block()


        @block.sync
        def _(sp):
            for e in range(E):
                sp.dma_start(w1[:, e, :], ins["f_w1"][e]).then_inc(s_w13, 16)
                sp.dma_start(w3[:, e, :], ins["f_w3"][e]).then_inc(s_w13, 16)
                sp.dma_start(w2[:, e, :, :], ins["f_w2"][e].rearrange("(m p) c -> p m c", p=P)).then_inc(s_w2, 16)

        @block.tensor
        def _(pe):
            def hidden(c, e):
                k = c * E + e
                for i in range(MF):
                    for w, ps, s, read in ((w1, ps_1, s_1, s_silu), (w3, ps_3, s_3, s_h)):
                        wait_used(pe, read, MF * (k - 1) + i + 1)
                        pe.matmul(ps[i][:, :], w[:, e, i * P:(i + 1) * P], xnT[:, bass.ds(c * CH, CH)],
                                  start=True, stop=True).then_inc(s, 1)

            def down(c, e):
                k = c * E + e
                wait_used(pe, s_add, k - 1)
                pe.wait_ge(s_h, MF * (k + 1))
                for t in range(CT):
                    for i in range(MF):
                        mm = pe.matmul(ps_y[e % 2][:, t, :], hT[:, e % 2, i, t * P:(t + 1) * P],
                                       w2[:, e, i, :], start=(i == 0), stop=(i == MF - 1))
                mm.then_inc(s_y, 1)

            pe.wait_ge(s_w13, 16 * 2 * E)
            pe.wait_ge(s_w2, 16 * E)

            def body(c):
                for e in range(E):
                    hidden(c, e)
                    if e:
                        down(c, e - 1)
                    elif not (isinstance(c, int) and c == 0):
                        down(c - 1, E - 1)
            repeat(pe, NC_, body)
            down(NC_ - 1, E - 1)

        @block.scalar
        def _(act):
            def body(c):
                for e in range(E):
                    for i in range(MF):
                        n = MF * (c * E + e) + i
                        act.wait_ge(s_1, n + 1)
                        wait_used(act, s_h, n - MF + 1)
                        act.activation(gate[:, i, :], ps_1[i][:, :], ACT.Silu).then_inc(s_silu, 1)
            repeat(act, NC_, body)

        @block.vector
        def _(dve):
            def product(c, e):
                k = c * E + e
                wait_used(dve, s_y, k - 1)
                for i in range(MF):
                    n = MF * k + i
                    dve.wait_ge(s_silu, n + 1)
                    dve.wait_ge(s_3, n + 1)
                    dve.tensor_tensor(hT[:, e % 2, i, :], gate[:, i, :], ps_3[i][:, :], ALU.mult).then_inc(s_h, 1)

            def add(c, e):
                k = c * E + e
                dve.wait_ge(s_y, k + 1)
                wait_used(dve, s_add, k)
                for t in range(CT):
                    xt = g.x[:, bass.ds(c * CT + t, 1), :].rearrange("p o c -> p (o c)")
                    ins = dve.scalar_tensor_tensor(
                        out=xt, in0=ps_y[e % 2][:, t, :],
                        scalar=route[:, bass.ds(c * CT + t, 1), e:e + 1].rearrange("p o c -> p (o c)"),
                        in1=xt, op0=ALU.mult, op1=ALU.add)
                ins.then_inc(s_add, 1)

            def body(c):
                for e in range(E):
                    product(c, e)
                    if e:
                        add(c, e - 1)
                    elif not (isinstance(c, int) and c == 0):
                        add(c - 1, E - 1)
            repeat(dve, NC_, body)
            add(NC_ - 1, E - 1)


def moe_layer(nc, g, ins, phase):
    with ExitStack() as ctx:
        m = Mem(nc, ctx, phase)
        xnT = m.sb("xnT", [P, N])
        logits = m.sb("logits", [P, NT, E])
        route = m.sb("route", [P, NT, E])
        layer_norm_stats(nc, g, phase + "_ln")
        normalise_and_turn(nc, g, phase + "_turn", xnT, logits)
        route_top2(nc, g, phase + "_route", logits, route)
        moe(nc, g, ins, phase + "_moe", xnT, route)


K = 4
LEFT = K // 2


def gates(nc, g, scr, xnT):
    with ExitStack() as ctx:
        m = Mem(nc, ctx, "gates")
        ab = m.sb("ab", [48, N])
        ps = [m.ps(f"ps{p}", [48, CH]) for p in range(2)]
        s_mm = m.sems("projected", 2)
        s_sig = m.sems("sigmoid", 2)
        s_out = m.sem("stored")
        block = m.block()

        @block.tensor
        def _(pe):
            def body(i):
                for p in range(2):
                    wait_used(pe, s_sig[p], i)
                    pe.matmul(ps[p][:, :], g.gatesT[:, :], xnT[:, bass.ds((2 * i + p) * CH, CH)],
                              start=True, stop=True).then_inc(s_mm[p], 1)
            repeat(pe, NC_ // 2, body)

        @block.scalar
        def _(act):
            def body(i):
                for p in range(2):
                    act.wait_ge(s_mm[p], i + 1)
                    act.activation(ab[:, bass.ds((2 * i + p) * CH, CH)], ps[p][:, :], ACT.Sigmoid,
                                   bias=g.bias_ab[:, :]).then_inc(s_sig[p], 1)
            repeat(act, NC_ // 2, body)

        @block.sync
        def _(sp):
            for p in range(2):
                sp.wait_ge(s_sig[p], NC_ // 2)
            for i in range(2):
                sp.dma_start(scr.ab[i], ab[32 * i:32 * i + H, :]).then_inc(s_out, 16)
            sp.wait_ge(s_out, 32)


def project_conv(nc, g, scr, xnT, sumsq):
    with ExitStack() as ctx:
        m = Mem(nc, ctx, "conv")
        u = m.sb("u", [P, 3, LEFT + S + K - 1 - LEFT])
        y = m.sb("y", [P, 3, S])
        z = m.sb("z", [P, 3, S])
        sq = m.sb("sq", [P, 2, S])
        HB = S // CH
        ps = [[m.ps(f"ps{w}{i}", [P, CH]) for i in range(HB)] for w in range(3)]
        ps_s = m.ps("ps_s", [P, 2, TB])
        s_pad = m.sem("padded")
        s_mm = m.sems("projected", 3)
        s_u = m.sems("u", 3)
        s_tap = m.sem("tap")
        s_y = m.sems("y", 3)
        s_z = m.sems("z", 3)
        s_sq = m.sems("squared", 2)
        s_sum = m.sem("summed")
        s_ss = m.sem("sums_out")
        s_out = m.sems("stored", 3)
        block = m.block()

        @block.gpsimd
        def _(pool):
            pool.memset(u[:, :, 0:LEFT], 0.0).then_inc(s_pad, 1)
            pool.wait_ge(s_pad, 1)
            pool.memset(u[:, :, LEFT + S:], 0.0).then_inc(s_pad, 1)

        @block.tensor
        def _(pe):
            def body(b):
                for w in range(3):
                    wait_used(pe, s_u[w], b)
                    for i in range(HB):
                        mm = pe.matmul(ps[w][i][:, :], g.wT[:, 4 + w, :],
                                       xnT[:, bass.ds(b * S + i * CH, CH)], start=True, stop=True)
                    mm.then_inc(s_mm[w], 1)
                wait_used(pe, s_ss, b)
                for w in range(2):
                    pe.wait_ge(s_sq[w], b + 1)
                    for t in range(TB):
                        mm = pe.matmul(ps_s[:, w, t:t + 1], sq[:, w, t * P:(t + 1) * P], g.ones[:, 0:1],
                                       start=True, stop=True)
                mm.then_inc(s_sum, 1)
            repeat(pe, B, body)

        @block.scalar
        def _(act):
            act.wait_ge(s_pad, 2)

            def body(b):
                for w in range(3):
                    act.wait_ge(s_mm[w], b + 1)
                    wait_used(act, s_y[w], b)
                    for i in range(HB):
                        ins = act.activation(u[:, w, LEFT + i * CH:LEFT + (i + 1) * CH], ps[w][i][:, :],
                                             ACT.Silu, bias=g.bias_qkv[:, w:w + 1])
                    ins.then_inc(s_u[w], 1)
                for w in range(3):
                    act.wait_ge(s_y[w], b + 1)
                    wait_used(act, s_out[w], 16 * b)
                    act.activation(z[:, w, :], y[:, w, :], ACT.Silu).then_inc(s_z[w], 1)
                    if w < 2:
                        act.wait_ge(s_z[w], b + 1)
                        wait_used(act, s_sum, b)
                        act.activation(sq[:, w, :], z[:, w, :], ACT.Square).then_inc(s_sq[w], 1)
            repeat(act, B, body)

        @block.vector
        def _(dve):
            def body(b):
                for w in range(3):
                    dve.wait_ge(s_u[w], b + 1)
                    wait_used(dve, s_z[w], b)
                    taps = Count(dve, s_tap, (K - 1) * (3 * b + w))
                    taps.done(dve.tensor_scalar(y[:, w, :], u[:, w, 0:S], g.conv[:, w, 0:1], None, ALU.mult))
                    for j in range(1, K):
                        ins = dve.scalar_tensor_tensor(out=y[:, w, :], in0=u[:, w, j:j + S],
                                                       scalar=g.conv[:, w, j:j + 1], in1=y[:, w, :],
                                                       op0=ALU.mult, op1=ALU.add)
                        if j < K - 1:
                            taps.done(ins)
                    ins.then_inc(s_y[w], 1)
                dve.wait_ge(s_sum, b + 1)
                dve.tensor_copy(sumsq[:, :, bass.ds(b * TB, TB)], ps_s[:, :, :]).then_inc(s_ss, 1)
            repeat(dve, B, body)

        @block.sync
        def _(sp):
            def body(b):
                for w in range(3):
                    sp.wait_ge(s_z[w], b + 1)
                    sp.dma_start(scr.qkv[w][:, bass.ds(b * S, S)], z[:, w, :]).then_inc(s_out[w], 16)
            repeat(sp, B, body)
            for w in range(3):
                sp.wait_ge(s_out[w], 16 * B)


def l2_norms(nc, g, scr, sumsq, q_scale):
    with ExitStack() as ctx:
        m = Mem(nc, ctx, "l2")
        norm = m.sb("norm", [P, 2, NT])
        inv = m.sb("inv", [P, 2, NT])
        rows = m.sb("rows", [NT, P])
        ps = m.ps("ps", [P, P])
        s_norm = m.sem("norm")
        s_chain = m.sem("chain")
        s_turn = m.sem("turned")
        s_rows = m.sem("rows")
        s_out = m.sem("stored")
        block = m.block()

        @block.scalar
        def _(act):
            act.activation(norm[:, :, :], sumsq[:, :, :], ACT.Sqrt).then_inc(s_norm, 1)

        @block.vector
        def _(dve):
            chain = Count(dve, s_chain)
            dve.wait_ge(s_norm, 1)
            chain.done(dve.tensor_scalar(norm[:, :, :], norm[:, :, :], L2_EPS, None, ALU.add))
            chain.done(dve.reciprocal(inv[:, :, :], norm[:, :, :]))
            dve.tensor_copy(q_scale[:, :], inv[:, 0, :])
            dve.wait_ge(s_turn, 1)
            dve.tensor_copy(rows[:, :], ps[0:NT, :]).then_inc(s_rows, 1)

        @block.tensor
        def _(pe):
            pe.wait_ge(s_chain, 2)
            pe.transpose(ps[0:NT, :], inv[:, 1, :], g.ident[:, :]).then_inc(s_turn, 1)

        @block.sync
        def _(sp):
            sp.wait_ge(s_rows, 1)
            sp.dma_start(scr.k_scale.rearrange("(t p) -> t p", p=P), rows[:, :]).then_inc(s_out, 16)
            sp.wait_ge(s_out, 16)


L = 8
TH = S // 2
LB = TH // L


def solve_and_scan(nc, g, scr):
    with ExitStack() as ctx:
        m = Mem(nc, ctx, "solve")
        g7 = m.sb("g7", [P, S // L])
        xv = m.sb("xv", [P, D // 2, S])
        xw = m.sb("xw", [P, D, S])
        kd = m.sb("kd", [P, D, S])
        with ExitStack() as lctx:
            m2 = Mem(nc, lctx, "solve2")
            k = m2.sb("k", [P, D, TH])
            X = m2.sb("X", [P, 2 * D, TH])
            ab = m2.sb("ab", [P, 2, TH])
            k_scale = m2.sb("k_scale", [P, TH])
            dec = m2.sb("dec", [P, L, LB, L])
            M = m2.sb("M", [P, L, LB, L])
            part = m2.sb("part", [P, D * LB * (L - 1)])
            red = m2.sb("red", [P, D, LB])
            whole = m2.sb("whole", [P, TH])
            end = m2.sb("end", [P, LB])
            s_in = m2.sem("loaded")
            s_one = m2.sem("ones")
            s_chain = m2.sem("chain")
            s_move = m2.sem("moved")
            s_ready = m2.sem("ready")
            block = m2.block()
            HALF = P // 2

            @block.sync
            def _(sp):
                for th in range(2):
                    for b in range(B):
                        lane = slice(HALF * th + H * b, HALF * th + H * (b + 1))
                        tok = slice(b * S + th * TH, b * S + (th + 1) * TH)
                        sp.dma_start(k[lane, :, :], scr.qkv[1][:, tok].rearrange("(h d) t -> h d t", h=H)
                                     ).then_inc(s_in, 16)
                        sp.dma_start(X[lane, 0:D, :], scr.qkv[2][:, tok].rearrange("(h d) t -> h d t", h=H)
                                     ).then_inc(s_in, 16)
                        sp.dma_start(ab[lane, :, :], scr.ab[:, :, tok].rearrange("i h t -> h i t")
                                     ).then_inc(s_in, 16)
                        sp.dma_start(k_scale[lane, :], scr.k_scale[tok].unsqueeze(0).to_broadcast([H, TH])
                                     ).then_inc(s_in, 16)
                sp.wait_ge(s_ready, 1)
                for th in range(2):
                    src, tok = slice(HALF * th, HALF * (th + 1)), slice(th * TH, (th + 1) * TH)
                    for dh in range(2):
                        dst = slice(HALF * dh, HALF * (dh + 1))
                        sp.dma_start(xv[dst, :, tok], X[src, dh * D // 2:(dh + 1) * D // 2, :]).then_inc(s_move, 16)
                        sp.dma_start(xw[dst, :, tok], X[src, D:2 * D, :]).then_inc(s_move, 16)
                        sp.dma_start(kd[dst, :, tok], k[src, :, :]).then_inc(s_move, 16)
                        sp.dma_start(g7[dst, th * LB:(th + 1) * LB],
                                     end[src, :]).then_inc(s_move, 16)
                sp.wait_ge(s_move, 16 * 16)

            @block.gpsimd
            def _(pool):
                pool.memset(dec[:, :, :, :], 1.0).then_inc(s_one, 1)

            @block.vector
            def _(dve):
                chain = Count(dve, s_chain)
                byblock = lambda a: a.rearrange("p (c j) -> p c j", j=L)
                a3, b3, w3 = byblock(ab[:, 0, :]), byblock(ab[:, 1, :]), byblock(whole[:, :])
                k4 = k[:, :, :].rearrange("p e (c j) -> p e c j", j=L)
                X4 = X[:, :, :].rearrange("p r (c j) -> p r c j", j=L)
                lanes = lambda a, n: a.unsqueeze(1).to_broadcast([P, n, TH])
                dve.wait_ge(s_one, 1)
                dve.wait_ge(s_in, 16 * 32)
                dve.tensor_tensor(k[:, :, :], k[:, :, :], lanes(k_scale[:, :], D), ALU.mult)
                dve.tensor_tensor(X[:, 0:D, :], X[:, 0:D, :], lanes(ab[:, 1, :], D), ALU.mult)
                for t in range(1, L):
                    chain.done(dve.tensor_tensor(dec[:, t, :, 0:t], dec[:, t - 1, :, 0:t],
                                                 a3[:, :, t:t + 1].to_broadcast([P, LB, t]), ALU.mult))
                chain.done(dve.tensor_tensor(w3, dec[:, :, :, 0].rearrange("p t c -> p c t"),
                                             a3[:, :, 0:1].to_broadcast([P, LB, L]), ALU.mult))
                chain.done(dve.tensor_copy(end[:, :], w3[:, :, L - 1]))
                chain.done(dve.scalar_tensor_tensor(out=k_scale[:, :], in0=whole[:, :], scalar=-1.0,
                                                    in1=ab[:, 1, :], op0=ALU.mult, op1=ALU.mult))
                chain.done(dve.tensor_tensor(X[:, D:2 * D, :], k[:, :, :], lanes(k_scale[:, :], D), ALU.mult))
                for t in range(1, L):
                    prod = part[:, 0:LB * t * D].rearrange("p (c i e) -> p c i e", c=LB, e=D)
                    at_t = k4[:, :, :, t].rearrange("p e c -> p c e").unsqueeze(2).to_broadcast([P, LB, t, D])
                    chain.done(dve.tensor_tensor(prod, k4[:, :, :, 0:t].rearrange("p e c i -> p c i e"), at_t,
                                                 ALU.mult))
                    Mt = M[:, t, :, 0:t]
                    chain.done(dve.tensor_reduce(Mt, prod, AX.X, ALU.add))
                    chain.done(dve.tensor_tensor(Mt, Mt, dec[:, t, :, 0:t], ALU.mult))
                    chain.done(dve.tensor_tensor(Mt, Mt, b3[:, :, t:t + 1].to_broadcast([P, LB, t]), ALU.mult))
                for t in range(1, L):
                    prod = part[:, 0:D * LB * t].rearrange("p (r c i) -> p r c i", r=D, c=LB)
                    for rows in (slice(0, D), slice(D, 2 * D)):
                        chain.done(dve.tensor_tensor(prod, X4[:, rows, :, 0:t],
                                                     M[:, t, :, 0:t].unsqueeze(1).to_broadcast([P, D, LB, t]),
                                                     ALU.mult))
                        chain.done(dve.tensor_reduce(red[:, :, :], prod, AX.X, ALU.add))
                        chain.done(dve.tensor_tensor(X4[:, rows, :, t], X4[:, rows, :, t], red[:, :, :],
                                                     ALU.subtract))
                dve.tensor_tensor(k4, k4, dec[:, L - 1, :, :].unsqueeze(1).to_broadcast([P, D, LB, L]),
                                  ALU.mult).then_inc(s_ready, 1)

        with ExitStack() as sctx:
            m3 = Mem(nc, sctx, "scan")
            R = D // 2
            St = m3.sb("state", [P, R, D])
            p1 = m3.sb("p1", [P, R, L, D])
            r1 = m3.sb("r1", [P, R, L])
            p2 = m3.sb("p2", [P, R, D, L])
            r2 = m3.sb("r2", [P, R, D])
            s_zero = m3.sem("zero")
            s_step = m3.sem("step")
            k_scale3 = m3.sb("k_scale3", [P, S])
            s_scale = m3.sem("k_scale")
            s_half = m3.sem("u_scaled")
            s_out = m3.sem("stored")
            HALF = P // 2
            block = m3.block()

            @block.vector
            def _(dve):
                dve.memset(St[:, :, :], 0.0).then_inc(s_zero, 1)
                dve.wait_ge(s_zero, 1)

                def body(c):
                    tok = bass.ds(c * L, L)
                    step = Count(dve, s_step, 6 * c)
                    xw_t = xw[:, :, tok].rearrange("p e i -> p i e").unsqueeze(1).to_broadcast([P, R, L, D])
                    step.done(dve.tensor_tensor(p1[:, :, :, :], St[:, :, :].unsqueeze(2).to_broadcast([P, R, L, D]),
                                                xw_t, ALU.mult))
                    step.done(dve.tensor_reduce(r1[:, :, :], p1[:, :, :, :], AX.X, ALU.add))
                    step.done(dve.tensor_tensor(xv[:, :, tok], xv[:, :, tok], r1[:, :, :], ALU.add))
                    step.done(dve.tensor_tensor(p2[:, :, :, :],
                                                xv[:, :, tok].unsqueeze(2).to_broadcast([P, R, D, L]),
                                                kd[:, :, tok].unsqueeze(1).to_broadcast([P, R, D, L]), ALU.mult))
                    step.done(dve.tensor_reduce(r2[:, :, :], p2[:, :, :, :], AX.X, ALU.add))
                    step.done(dve.scalar_tensor_tensor(out=St[:, :, :], in0=St[:, :, :], scalar=g7[:, bass.ds(c, 1)],
                                                       in1=r2[:, :, :], op0=ALU.mult, op1=ALU.add))
                repeat(dve, S // L, body)
                dve.wait_ge(s_scale, 16 * 2 * B)
                dve.tensor_tensor(xv[:, :, :], xv[:, :, :], k_scale3[:, :].unsqueeze(1).to_broadcast([P, R, S]),
                                  ALU.mult).then_inc(s_half, 1)

            @block.sync
            def _(sp):
                for dh in range(2):
                    for b in range(B):
                        lane = slice(HALF * dh + H * b, HALF * dh + H * (b + 1))
                        sp.dma_start(k_scale3[lane, :],
                                     scr.k_scale[b * S:(b + 1) * S].unsqueeze(0).to_broadcast([H, S])
                                     ).then_inc(s_scale, 16)
                sp.wait_ge(s_half, 1)
                for dh in range(2):
                    for b in range(B):
                        lane = slice(HALF * dh + H * b, HALF * dh + H * (b + 1))
                        rows = slice(dh * R, (dh + 1) * R)
                        sp.dma_start(scr.u.rearrange("(h d) t -> h d t", h=H)[:, rows, b * S:(b + 1) * S],
                                     xv[lane, :, :]).then_inc(s_out, 16)
                sp.wait_ge(s_out, 16 * 2 * B)


def delta_out(nc, g, scr, q_scale):
    with ExitStack() as ctx:
        m = Mem(nc, ctx, "out")
        u = m.sb("u", [P, N])
        q = m.sb("q", [P, N])
        k = m.sb("k", [P, N])
        a = m.sb("a", [P, N])
        same = m.sb("same", [P, H, D])
        rowsel = m.sb("rowsel", [P, D])
        spread = m.sb("spread", [P, D, P])
        gather = m.sb("gather", [P, D, H, D])
        bo = m.sb("bo", [P, P])
        kd = m.sb("kd", [P, 2, S])
        St = m.sb("St", [P, 2, S])
        qS = m.sb("qS", [P, 2, S])
        oT = m.sb("oT", [P, S])
        ps_k = [m.ps(f"ps_k{p}", [P, S]) for p in range(2)]
        ps_o = m.ps("ps_o", [P, S])
        ps_y = [m.ps(f"ps_y{i}", [P, CT, P]) for i in range(2)]
        s_in = m.sems("loaded", 4)
        s_same = m.sem("same")
        s_sel = m.sem("selectors")
        s_bo = m.sem("bo")
        s_bias = m.sem("bias_added")
        s_k = m.sem("k_spread")
        s_kd = m.sem("kd")
        s_S = m.sem("S")
        s_qS = m.sem("qS")
        s_o = m.sem("o")
        s_oT = m.sem("oT")
        s_y = m.sem("y")
        s_add = m.sem("added")
        block = m.block()

        @block.sync
        def _(sp):
            for b in range(B):
                tok = slice(b * S, (b + 1) * S)
                sp.dma_start(k[:, tok], scr.qkv[1][:, tok]).then_inc(s_in[b], 16)
                sp.dma_start(u[:, tok], scr.u[:, tok]).then_inc(s_in[b], 16)
                sp.dma_start(a[:, tok], scr.ab[0][:, tok].unsqueeze(1).to_broadcast([H, D, S])
                             ).then_inc(s_in[b], 16)
                sp.dma_start(q[:, tok], scr.qkv[0][:, tok]).then_inc(s_in[b], 16)

        @block.gpsimd
        def _(pool):
            pool.memset(same[:, :, :], 1.0).then_inc(s_same, 1)
            pool.wait_ge(s_same, 1)
            pool.affine_select(out=same[:, :, :], in_=same[:, :, :], compare_op=ALU.is_ge, fill=0.0, base=0,
                               pattern=[[-D, H], [0, D]], channel_multiplier=1).then_inc(s_same, 1)
            pool.wait_ge(s_same, 2)
            pool.affine_select(out=same[:, :, :], in_=same[:, :, :], compare_op=ALU.is_ge, fill=0.0, base=D - 1,
                               pattern=[[D, H], [0, D]], channel_multiplier=-1).then_inc(s_same, 1)
            pool.wait_ge(s_same, 3)
            pool.memset(gather[:, :, :, :], 0.0).then_inc(s_same, 1)

        @block.tensor
        def _(pe):
            pe.matmul(ps_y[0][:, 0, :], g.ones[0:1, :], g.bo_row[:, :], start=True, stop=True).then_inc(s_bo, 1)
            pe.wait_ge(s_sel, 2 * D + 1)
            pe.wait_ge(s_bias, 1)

            def spread_k(b, e):
                n = D * b + e
                if e == 0:
                    if isinstance(b, int):
                        pe.wait_ge(s_in[b], 64)
                wait_used(pe, s_kd, n - 1)
                for i in range(2):
                    mm = pe.matmul(ps_k[e % 2][:, i * CH:(i + 1) * CH], spread[:, e, :],
                                   k[:, bass.ds(b * S + i * CH, CH)], start=True, stop=True)
                mm.then_inc(s_k, 1)

            def sum_o(b, e):
                n = D * b + e
                pe.wait_ge(s_qS, n + 1)
                if e == 0:
                    wait_used(pe, s_oT, b)
                for i in range(2):
                    mm = pe.matmul(ps_o[:, i * CH:(i + 1) * CH], gather[:, e, :, :].rearrange("p h d -> p (h d)"),
                                   qS[:, e % 2, i * CH:(i + 1) * CH], start=(e == 0), stop=(e == D - 1))
                mm.then_inc(s_o, 1)

            def project(b):
                pe.wait_ge(s_oT, b + 1)
                wait_used(pe, s_add, b)
                for t in range(TB):
                    mm = pe.matmul(ps_y[t // CT][:, t % CT, :], oT[:, t * P:(t + 1) * P], g.wT[:, 7, :],
                                   start=True, stop=True)
                mm.then_inc(s_y, 1)

            for b in range(B):
                pe.wait_ge(s_in[b], 64)

            def body(b):
                for e in range(D):
                    spread_k(b, e)
                    if e:
                        sum_o(b, e - 1)
                sum_o(b, D - 1)
                project(b)
            repeat(pe, B, body)

        @block.vector
        def _(dve):
            dve.wait_ge(s_bo, 1)
            dve.tensor_copy(bo[:, :], ps_y[0][:, 0, :]).then_inc(s_bias, 1)
            dve.wait_ge(s_bias, 1)
            dve.tensor_tensor(g.x[:, :, :], g.x[:, :, :], bo[:, :].unsqueeze(1).to_broadcast([P, NT, P]), ALU.add)
            dve.wait_ge(s_same, 4)
            dve.tensor_reduce(rowsel[:, :], g.ident[:, :].rearrange("p (h e) -> p e h", h=H), AX.X,
                              ALU.add).then_inc(s_sel, 1)
            dve.wait_ge(s_sel, 1)
            for e in range(D):
                dve.tensor_scalar(spread[:, e, :], same[:, :, :].rearrange("p h d -> p (h d)"),
                                  rowsel[:, e:e + 1], None, ALU.mult).then_inc(s_sel, 1)
                dve.tensor_copy(gather[:, e, :, e], same[:, :, e]).then_inc(s_sel, 1)
            for b in range(B):
                dve.wait_ge(s_in[b], 64)

            def body(b):
                tok = bass.ds(b * S, S)
                for e in range(D):
                    n = D * b + e
                    dve.wait_ge(s_k, n + 1)
                    dve.tensor_tensor(kd[:, e % 2, :], u[:, tok], ps_k[e % 2][:, :], ALU.mult).then_inc(s_kd, 1)
                    dve.wait_ge(s_kd, n + 1)
                    dve.tensor_tensor_scan(St[:, e % 2, :], a[:, tok], kd[:, e % 2, :], 0.0, ALU.mult,
                                           ALU.add).then_inc(s_S, 1)
                    dve.wait_ge(s_S, n + 1)
                    wait_used(dve, s_o, n - 1)
                    dve.tensor_tensor(qS[:, e % 2, :], q[:, tok], St[:, e % 2, :], ALU.mult).then_inc(s_qS, 1)
                dve.wait_ge(s_y, b + 1)
                for t in range(TB):
                    xt = g.x[:, bass.ds(b * TB + t, 1), :].rearrange("p o c -> p (o c)")
                    ins = dve.scalar_tensor_tensor(out=xt, in0=ps_y[t // CT][:, t % CT, :],
                                                   scalar=q_scale[:, bass.ds(b * TB + t, 1)], in1=xt,
                                                   op0=ALU.mult, op1=ALU.add)
                ins.then_inc(s_add, 1)
            repeat(dve, B, body)

        @block.scalar
        def _(act):
            def body(b):
                act.wait_ge(s_o, D * (b + 1))
                wait_used(act, s_y, b)
                for i in range(2):
                    ins = act.activation(oT[:, i * CH:(i + 1) * CH], ps_o[:, i * CH:(i + 1) * CH], ACT.Copy)
                ins.then_inc(s_oT, 1)
            repeat(act, B, body)


class Shared:
    pass


def store(nc, out, x, name):
    with nc.semaphore(name) as s_out, nc.Block() as block:
        @block.sync
        def _(sp):
            sp.dma_start(out.rearrange("b (t p) c -> p (b t) c", p=P), x[:, :, :]).then_inc(s_out, 16)
            sp.wait_ge(s_out, 16)


def build(nc, ins, out, stop=None):
    g, scr = Shared(), Shared()
    scr.terms = [nc.dram_tensor(f"terms_{w}", (NPART, K1, H, N), BF16, kind="Internal").ap() for w in "qk"]
    scr.qkv = [nc.dram_tensor(f"delta_{w}", (P, N), F32, kind="Internal").ap() for w in "qkv"]
    scr.ab = nc.dram_tensor("delta_ab", (2, H, N), F32, kind="Internal").ap()
    scr.k_scale = nc.dram_tensor("delta_k_scale", (N,), F32, kind="Internal").ap()
    scr.u = nc.dram_tensor("delta_u", (P, N), F32, kind="Internal").ap()
    with ExitStack() as ctx:
        m = Mem(nc, ctx, "all")
        g.x = m.sb("x", [P, NT, P])
        g.ident = m.sb("ident", [P, P])
        g.ones = m.sb("ones", [P, P])
        g.varsel = m.sb("varsel", [P, 2, 48])
        g.wT = m.sb("wT", [P, 8, P])
        g.gatesT = m.sb("gatesT", [P, 48])
        g.bias_qkv = m.sb("bias_qkv", [P, 3])
        g.conv = m.sb("conv", [P, 3, K])
        g.bias_ab = m.sb("bias_ab", [48, 1])
        g.bo_row = m.sb("bo_row", [1, P])
        g.gate_w = m.sb("gate_w", [P, E])
        g.rstd = m.sb("rstd", [P, NT])
        g.nmr = m.sb("nmr", [P, NT])
        load_and_turn_weights(nc, g, ins)
        layer_norm_stats(nc, g, "ln_a")
        with ExitStack() as actx:
            ma = Mem(nc, actx, "a")
            g.o = ma.sb("o", [P, NT, P])
            with ExitStack() as vctx:
                mv = Mem(nc, vctx, "av")
                g.v1 = mv.sb("v1", [P, NT, H, VW])
                g.q_op = [mv.sb(f"q_op{s}", [P, GH, S], BF16) for s in range(NQ)]
                g.k_op = [mv.sb(f"k_op{s}", [P, GH, S], BF16) for s in range(NQ)]
                project_qkv(nc, g, scr)
                attend(nc, g, scr)
            if stop == "o":
                return store(nc, out, g.o, "dbg")
            project_out_a(nc, g)
        if stop == "x1":
            return store(nc, out, g.x, "dbg")
        moe_layer(nc, g, ins, "moe1")
        if stop == "x2":
            return store(nc, out, g.x, "dbg")
        with ExitStack() as bctx:
            mb = Mem(nc, bctx, "b")
            q_scale = mb.sb("q_scale", [P, NT])
            sumsq = mb.sb("sumsq", [P, 2, NT])
            with ExitStack() as xctx:
                xnT = Mem(nc, xctx, "bx").sb("xnT", [P, N])
                layer_norm_stats(nc, g, "ln_b")
                normalise_and_turn(nc, g, "turn_b", xnT)
                gates(nc, g, scr, xnT)
                project_conv(nc, g, scr, xnT, sumsq)
            l2_norms(nc, g, scr, sumsq, q_scale)
            solve_and_scan(nc, g, scr)
            delta_out(nc, g, scr, q_scale)
        if stop == "x3":
            return store(nc, out, g.x, "dbg")
        moe_layer(nc, g, ins, "moe2")
        store(nc, out, g.x, "stored_out")


_INS = ["a_x", "a_Wq", "a_Wk", "a_Wv", "a_Wo", "b_Wq", "b_bq", "b_Wk", "b_bk", "b_Wv", "b_bv", "b_Wa", "b_ba",
        "b_Wb", "b_bb", "b_conv_q", "b_conv_k", "b_conv_v", "b_Wo", "b_bo", "f_gate_w", "f_w1", "f_w2", "f_w3"]
_LAYERS = {"a": "L0_attn_a_", "b": "L0_attn_b_", "f": "L0_ffn_"}


def kernel(**inputs):
    import numpy as np
    import concourse.bacc as bacc
    from concourse.bass_utils import run_bass_kernel_spmd

    nc = bacc.Bacc("TRN2", target_bir_lowering=False, num_devices=1)
    arrays, ins = {}, {}
    for name in _INS:
        a = np.ascontiguousarray(inputs[_LAYERS[name[0]] + name[2:]])
        arrays[f"in_{name}"] = a
        ins[name] = nc.dram_tensor(f"in_{name}", a.shape, mybir.dt.from_np(a.dtype), kind="ExternalInput").ap()
    out = nc.dram_tensor("out_x", (B, S, P), F32, kind="ExternalOutput").ap()
    build(nc, ins, out)
    r = run_bass_kernel_spmd(nc, [arrays], core_ids=[0])
    return r.results[0]["out_x"]
```

```python
from contextlib import ExitStack

import concourse.bass as bass
from concourse import mybir

F32 = mybir.dt.float32
BF16 = mybir.dt.bfloat16
ALU = mybir.AluOpType
ACT = mybir.ActivationFunctionType
AX = mybir.AxisListType

P = 128
H = 16
D = P // H
B = 4
S = 1024
N = B * S
NT = N // P
TB = S // P
CH = 512
NC_ = N // CH
CT = CH // P
LN_EPS = 1e-5
L2_EPS = 1e-6

NPART = 3
K1 = D + 1
R_ALL = NPART * NPART * K1
R_MAX = 96
R_END = R_MAX + NPART
GH = 4
NQ = H // GH
E, F = 8, 256
VW = D + 1


class Count:

    def __init__(self, eng, sem, start=0):
        self.eng, self.sem, self.n = eng, sem, start

    def done(self, ins):
        ins.then_inc(self.sem, 1)
        self.n = self.n + 1
        self.eng.wait_ge(self.sem, self.n)


def wait_used(eng, sem, value):
    if not (isinstance(value, int) and value <= 0):
        eng.wait_ge(sem, value)


def repeat(eng, n, body):
    body(0)
    with eng.Fori(1, n) as i:
        body(i)


class Mem:

    def __init__(self, nc, ctx, phase):
        self.nc, self.ctx, self.phase, self.used = nc, ctx, phase, []

    def sb(self, name, shape, dt=F32):
        return self.ctx.enter_context(self.nc.sbuf_tensor(f"{self.phase}_{name}", shape, dt))

    def ps(self, name, shape, dt=F32):
        return self.ctx.enter_context(self.nc.psum_tensor(f"{self.phase}_{name}", shape, dt))

    def sem(self, name):
        s = self.ctx.enter_context(self.nc.semaphore(f"{self.phase}_{name}"))
        self.used.append(s)
        return s

    def sems(self, name, n):
        return [self.sem(f"{name}{i}") for i in range(n)]

    def block(self):
        self.ctx.callback(self.clear)
        return self.ctx.enter_context(self.nc.Block())

    def clear(self):
        numbers = sorted(s.num for s in self.used)
        with self.nc.Block() as block:
            @block.sync
            def _(sp):
                first = last = numbers[0]
                for n in numbers[1:] + [-1]:
                    if n == last + 1:
                        last = n
                        continue
                    sp.sem_clear(range(first, last + 1))
                    first = last = n


def load_and_turn_weights(nc, g, ins):
    with ExitStack() as ctx:
        m = Mem(nc, ctx, "w")
        names = ["a_Wq", "a_Wk", "a_Wv", "a_Wo", "b_Wq", "b_Wk", "b_Wv", "b_Wo"]
        raw = m.sb("raw", [P, len(names), P])
        gates = m.sb("gates", [48, P])
        headsum = m.sb("headsum", [P, 2, H])
        headmean = m.sb("headmean", [P, 2, H])
        turned_ps = [m.ps(f"turned{i}", [P, CH]) for i in range(2)]
        gates_ps = m.ps("gates_ps", [P, CH])
        s_w = m.sem("w_loaded")
        s_x = m.sems("x_loaded", B)
        s_small = m.sem("small_loaded")
        s_id0 = m.sem("ident_cleared")
        s_id = m.sem("ident_ready")
        s_sel = m.sem("selectors")
        s_turned = m.sem("turned")
        s_gates = m.sem("gates_cleared")
        s_chain = m.sem("chain")

        block = m.block()

        @block.sync
        def _(sp):
            for i, n in enumerate(names):
                sp.dma_start(raw[:, i, :], ins[n]).then_inc(s_w, 16)
            xd = ins["a_x"].rearrange("b (t p) c -> p (b t) c", p=P)
            for i in range(B):
                sp.dma_start(g.x[:, i * TB:(i + 1) * TB, :], xd[:, i * TB:(i + 1) * TB, :]).then_inc(s_x[i], 16)
            for i, n in enumerate(["b_bq", "b_bk", "b_bv"]):
                sp.dma_start(g.bias_qkv[:, i:i + 1], ins[n].rearrange("(c o) -> c o", o=1)).then_inc(s_small, 16)
            for i, n in enumerate(["b_conv_q", "b_conv_k", "b_conv_v"]):
                sp.dma_start(g.conv[:, i, :], ins[n].rearrange("c o k -> c (o k)")).then_inc(s_small, 16)
            sp.wait_ge(s_gates, 2)
            sp.dma_start(gates[0:H, :], ins["b_Wa"]).then_inc(s_w, 16)
            sp.dma_start(gates[32:32 + H, :], ins["b_Wb"]).then_inc(s_w, 16)
            sp.dma_start(g.bias_ab[0:H, :], ins["b_ba"].rearrange("(c o) -> c o", o=1)).then_inc(s_small, 16)
            sp.dma_start(g.bias_ab[32:32 + H, :], ins["b_bb"].rearrange("(c o) -> c o", o=1)).then_inc(s_small, 16)
            sp.dma_start(g.bo_row[:, :], ins["b_bo"].rearrange("(o c) -> o c", o=1)).then_inc(s_small, 16)
            sp.dma_start(g.gate_w[:, :], ins["f_gate_w"]).then_inc(s_small, 16)
            sp.wait_ge(s_small, 16 * 10)

        @block.gpsimd
        def _(pool):
            pool.memset(gates[:, :], 0.0).then_inc(s_gates, 1)
            pool.memset(g.bias_ab[:, :], 0.0).then_inc(s_gates, 1)
            pool.memset(g.ident[:, :], 0.0).then_inc(s_id0, 1)
            pool.memset(g.ones[:, :], 1.0).then_inc(s_id0, 1)
            pool.memset(g.varsel[:, :, :], 0.0).then_inc(s_id0, 1)
            pool.wait_ge(s_id0, 3)
            pool.affine_select(out=g.ident[:, :], in_=g.ident[:, :], compare_op=ALU.not_equal, fill=1.0,
                               base=0, pattern=[[-1, P]], channel_multiplier=1).then_inc(s_id, 1)
            for d in range(D):
                for i, w in enumerate([D / (D - 1), 1.0 / (D - 1)]):
                    v = g.varsel[:, i, 32 * i:32 * i + H]
                    pool.wait_ge(s_sel, 2 * d + i)
                    pool.affine_select(out=v, in_=v, compare_op=ALU.not_equal, fill=w, base=-H * d,
                                       pattern=[[-1, H]], channel_multiplier=1).then_inc(s_sel, 1)

        @block.tensor
        def _(pe):
            pe.wait_ge(s_id, 1)
            pe.wait_ge(s_w, 16 * 10)
            for i in range(8):
                mm = pe.transpose(turned_ps[i // 4][:, (i % 4) * P:(i % 4 + 1) * P], raw[:, i, :], g.ident[:, :])
            mm.then_inc(s_turned, 1)
            pe.transpose(gates_ps[:, 0:48], gates[:, :], g.ident[0:48, 0:48]).then_inc(s_turned, 1)

        @block.vector
        def _(dve):
            chain = Count(dve, s_chain)
            dve.wait_ge(s_turned, 2)
            dve.tensor_copy(g.wT[:, 2:4, :], turned_ps[0][:, 2 * P:4 * P])
            dve.tensor_copy(g.wT[:, 4:8, :], turned_ps[1][:, :])
            dve.tensor_copy(g.gatesT[:, :], gates_ps[:, 0:48])
            qk = turned_ps[0][:, 0:2 * P].rearrange("p (w h d) -> p w h d", w=2, h=H)
            chain.done(dve.tensor_reduce(headsum[:, :, :], qk, AX.X, ALU.add))
            chain.done(dve.tensor_scalar(headmean[:, :, :], headsum[:, :, :], 1.0 / D, None, ALU.mult))
            chain.done(dve.tensor_tensor(g.wT[:, 0:2, :].rearrange("p w (d h) -> p w h d", h=H), qk,
                                         headmean[:, :, :].unsqueeze(3).to_broadcast([P, 2, H, D]), ALU.subtract))
            for b in range(B):
                dve.wait_ge(s_x[b], 16)
                for t in range(TB):
                    bn_stats_of(nc, g, b * TB + t)
            dve.tensor_scalar(g.wT[:, 0, :], g.wT[:, 0, :], 1.0 / D, None, ALU.mult)


def bn_stats_of(nc, g, tile):
    if isinstance(tile, int):
        return nc.vector.bn_stats(g.stats[:, tile, :], g.x[:, tile, :])
    one = bass.ds(tile, 1)
    return nc.vector.bn_stats(g.stats[:, one, :].rearrange("p o s -> p (o s)"),
                              g.x[:, one, :].rearrange("p o c -> p (o c)"))


def layer_norm_scales(nc, g, phase):
    with ExitStack() as ctx:
        m = Mem(nc, ctx, phase)
        msum = m.sb("msum", [P, NT])
        mdiff = m.sb("mdiff", [P, NT])
        m2 = m.sb("m2", [P, NT])
        var = m.sb("var", [P, NT])
        std = m.sb("std", [P, NT])
        eps = m.sb("eps", [P, 1])
        s_eps = m.sem("eps")
        s_chain = m.sem("chain")
        s_var = m.sem("var")
        s_std = m.sem("std")
        s_rstd = m.sem("rstd")
        block = m.block()

        @block.vector
        def _(dve):
            dve.memset(eps[:, :], LN_EPS).then_inc(s_eps, 1)
            chain = Count(dve, s_chain)
            stats = g.stats
            dve.tensor_tensor(msum[:, :], stats[:, :, 1], stats[:, :, 4], ALU.add)
            chain.done(dve.tensor_tensor(mdiff[:, :], stats[:, :, 1], stats[:, :, 4], ALU.subtract))
            dve.tensor_tensor(m2[:, :], stats[:, :, 2], stats[:, :, 5], ALU.add)
            chain.done(dve.scalar_tensor_tensor(out=var[:, :], in0=mdiff[:, :], scalar=0.25 * P,
                                                in1=mdiff[:, :], op0=ALU.mult, op1=ALU.mult))
            dve.tensor_tensor(var[:, :], var[:, :], m2[:, :], ALU.add).then_inc(s_var, 1)
            dve.wait_ge(s_std, 1)
            dve.reciprocal(g.rstd[:, :], std[:, :]).then_inc(s_rstd, 1)
            dve.wait_ge(s_rstd, 1)
            dve.scalar_tensor_tensor(out=g.nmr[:, :], in0=msum[:, :], scalar=-0.5, in1=g.rstd[:, :],
                                     op0=ALU.mult, op1=ALU.mult)

        @block.scalar
        def _(act):
            act.wait_ge(s_eps, 1)
            act.wait_ge(s_var, 1)
            act.activation(std[:, :], var[:, :], ACT.Sqrt, bias=eps[:, :], scale=1.0 / P).then_inc(s_std, 1)


def project_qkv(nc, g, scr):
    with ExitStack() as ctx:
        m = Mem(nc, ctx, "qkv")
        xn = m.sb("xn", [P, 2, CT, P])
        xnT = m.sb("xnT", [P, 2, CH])
        parts = [m.sb(f"parts_{w}", [P, 2, NPART, CH], BF16) for w in "qk"]
        square = [m.sb(f"square_{w}", [P, 2, CH]) for w in "qk"]
        rest = [m.sb(f"rest_{w}", [P, 2, CH]) for w in "qk"]
        vparts = m.sb("vparts", [48, 2, NPART, CH], BF16)
        vrest = m.sb("vrest", [48, 2, CH])
        ps_x = m.ps("ps_x", [P, CH])
        ps_qk = [[m.ps(f"ps_{w}{p}", [P, CH]) for p in range(2)] for w in "qk"]
        ps_v = m.ps("ps_v", [P, CH])
        ps_var = m.ps("ps_var", [P, CH])

        s_xn = m.sems("xn", 2)
        s_turn = m.sems("turned", 2)
        s_xnT = m.sems("xnT", 2)
        s_proj = [m.sems(f"proj_{w}", 2) for w in "qk"]
        s_v = m.sems("v", 2)
        s_vout = m.sems("v_out", 2)
        s_sq = [m.sems(f"square_{w}", 2) for w in "qk"]
        s_p1 = [m.sems(f"part1_{w}", 2) for w in "qk"]
        s_r = [m.sems(f"rest_{w}", 2) for w in "qk"]
        s_p2 = [m.sems(f"part2_{w}", 2) for w in "qk"]
        s_p3 = [m.sems(f"part3_{w}", 2) for w in "qk"]
        s_var = m.sems("var", 2)
        s_v1 = m.sems("vpart1_", 2)
        s_vr = m.sems("vrest", 2)
        s_v2 = m.sems("vpart2_", 2)
        s_v3 = m.sems("vpart3_", 2)
        s_out = m.sems("stored", 2)
        s_ones = m.sem("ones")
        NDMA = 4
        block = m.block()


        @block.gpsimd
        def _(pool):
            pool.memset(g.v1[:, :, :, D:VW], 1.0).then_inc(s_ones, 1)
            n = 1
            for op in (*g.q_op, *g.k_op):
                pool.wait_ge(s_ones, n)
                pool.memset(op[64:P, :, :].bitcast(mybir.dt.uint32), 0).then_inc(s_ones, 1)
                n += 1
            for op in g.k_op:
                pool.wait_ge(s_ones, n)
                pool.memset(op[R_MAX:R_END, :, :], 1.0).then_inc(s_ones, 1)
                n += 1

        @block.scalar
        def _(act):
            def body(i):
                for p in range(2):
                    wait_used(act, s_turn[p], i)
                    for t in range(CT):
                        tile = (2 * i + p) * CT + t
                        ins = act.activation(xn[:, p, t, :], g.x[:, bass.ds(tile, 1), :], ACT.Identity,
                                             bias=g.nmr[:, bass.ds(tile, 1)], scale=g.rstd[:, bass.ds(tile, 1)])
                    ins.then_inc(s_xn[p], 1)
                    wait_used(act, s_out[p], 16 * NDMA * i)
                    for w in range(2):
                        act.wait_ge(s_proj[w][p], i + 1)
                        wait_used(act, s_var[p], i)
                        act.activation(square[w][:, p, :], ps_qk[w][p][:, :], ACT.Square).then_inc(s_sq[w][p], 1)
                        act.activation(parts[w][:, p, 0, :], ps_qk[w][p][:, :], ACT.Copy).then_inc(s_p1[w][p], 1)
                    for w in range(2):
                        act.wait_ge(s_r[w][p], i + 1)
                        act.activation(parts[w][:, p, 1, :], rest[w][:, p, :], ACT.Copy).then_inc(s_p2[w][p], 1)
                    act.wait_ge(s_var[p], i + 1)
                    act.activation(vparts[:, p, 0, :], ps_var[0:48, :], ACT.Copy).then_inc(s_v1[p], 1)
                    act.wait_ge(s_vr[p], i + 1)
                    act.activation(vparts[:, p, 1, :], vrest[:, p, :], ACT.Copy).then_inc(s_v2[p], 1)
            repeat(act, NC_ // 2, body)

        @block.tensor
        def _(pe):
            def body(i):
                for p in range(2):
                    pe.wait_ge(s_xn[p], i + 1)
                    wait_used(pe, s_xnT[1 - p], i + p)
                    for t in range(CT):
                        mm = pe.transpose(ps_x[:, t * P:(t + 1) * P], xn[:, p, t, :], g.ident[:, :])
                    mm.then_inc(s_turn[p], 1)
                    pe.wait_ge(s_xnT[p], i + 1)
                    for w in range(2):
                        wait_used(pe, s_r[w][p], i)
                        pe.matmul(ps_qk[w][p][:, :], g.wT[:, w, :], xnT[:, p, :], start=True,
                                  stop=True).then_inc(s_proj[w][p], 1)
                    wait_used(pe, s_vout[1 - p], i + p)
                    for t in range(CT):
                        mm = pe.matmul(ps_v[:, t * P:(t + 1) * P], xnT[:, p, t * P:(t + 1) * P], g.wT[:, 2, :],
                                       start=True, stop=True)
                    mm.then_inc(s_v[p], 1)
                    wait_used(pe, s_vr[1 - p], i + p)
                    for w in range(2):
                        pe.wait_ge(s_sq[w][p], i + 1)
                        mm = pe.matmul(ps_var[0:48, :], g.varsel[:, w, :], square[w][:, p, :],
                                       start=(w == 0), stop=(w == 1))
                    mm.then_inc(s_var[p], 1)
            repeat(pe, NC_ // 2, body)

        @block.vector
        def _(dve):
            dve.wait_ge(s_ones, 1)
            def body(i):
                for p in range(2):
                    dve.wait_ge(s_turn[p], i + 1)
                    wait_used(dve, s_v[p], i)
                    dve.tensor_copy(xnT[:, p, :], ps_x[:, :]).then_inc(s_xnT[p], 1)
                    for w in range(2):
                        dve.wait_ge(s_p1[w][p], i + 1)
                        dve.tensor_tensor(rest[w][:, p, :], ps_qk[w][p][:, :], parts[w][:, p, 0, :],
                                          ALU.subtract).then_inc(s_r[w][p], 1)
                    dve.wait_ge(s_v[p], i + 1)
                    for t in range(CT):
                        ins = dve.tensor_copy(g.v1[:, bass.ds((2 * i + p) * CT + t, 1), :, 0:D],
                                              ps_v[:, t * P:(t + 1) * P].rearrange("p (h d) -> p h d", h=H))
                    ins.then_inc(s_vout[p], 1)
                    for w in range(2):
                        dve.wait_ge(s_p2[w][p], i + 1)
                        dve.tensor_tensor(parts[w][:, p, 2, :], rest[w][:, p, :], parts[w][:, p, 1, :],
                                          ALU.subtract).then_inc(s_p3[w][p], 1)
                    dve.wait_ge(s_v1[p], i + 1)
                    dve.tensor_tensor(vrest[:, p, :], ps_var[0:48, :], vparts[:, p, 0, :],
                                      ALU.subtract).then_inc(s_vr[p], 1)
                    dve.wait_ge(s_v2[p], i + 1)
                    dve.tensor_tensor(vparts[:, p, 2, :], vrest[:, p, :], vparts[:, p, 1, :],
                                      ALU.subtract).then_inc(s_v3[p], 1)
            repeat(dve, NC_ // 2, body)

        @block.sync
        def _(sp):
            def body(i):
                for p in range(2):
                    at = (2 * i + p) * CH
                    for w in range(2):
                        sp.wait_ge(s_p3[w][p], i + 1)
                        sp.dma_start(scr.terms[w][:, 0:D, :, bass.ds(at, CH)].rearrange("i d h t -> (d h) i t"),
                                     parts[w][:, p, :, :]).then_inc(s_out[p], 16)
                    sp.wait_ge(s_v3[p], i + 1)
                    for w in range(2):
                        sp.dma_start(scr.terms[w][:, D, :, bass.ds(at, CH)].rearrange("i h t -> h i t"),
                                     vparts[32 * w:32 * w + H, p, :, :]).then_inc(s_out[p], 16)
            repeat(sp, NC_ // 2, body)
            for p in range(2):
                sp.wait_ge(s_out[p], 16 * NDMA * (NC_ // 2))


LEAD = 6
PV_LAG = 3
PROBS = 16
STEPS = GH * TB


def attend(nc, g, scr):
    with ExitStack() as ctx:
        m = Mem(nc, ctx, "att")
        q_op, k_op = g.q_op, g.k_op
        probs = m.sb("probs", [P, PROBS, CH])
        vq = m.sb("vq", [P, 2, TB, 64])
        negmax = m.sb("negmax", [P, 2, STEPS])
        nm_rows = m.sb("nm_rows", [STEPS, P])
        nm_rest = m.sb("nm_rest", [STEPS, P])
        nm_parts = m.sb("nm_parts", [STEPS, 2, NPART, P], BF16)
        acc_sb = m.sb("acc_sb", [P, 2, CH])
        rsum = m.sb("rsum", [P, 2, CT, GH])
        ps_max = m.ps("ps_max", [P, 2, S])
        ps_prob = m.ps("ps_prob", [P, 2, CH])
        ps_acc = m.ps("ps_acc", [P, CH])
        ps_misc = m.ps("ps_misc", [P, CH])
        comb = ps_misc[:, P:P + CT * GH * VW].rearrange("p (t g r) -> p t g r", t=CT, g=GH)

        s_clear = m.sem("cleared")
        s_load = m.sems("loaded", NQ)
        s_scored = m.sem("scored")
        s_maxed = m.sem("maxed")
        s_nmT = m.sem("negmax_turned")
        s_nmch = m.sem("negmax_chain")
        s_nmp = m.sem("negmax_parts")
        s_nmrow = m.sem("negmax_rows")
        s_prob = m.sem("prob_scored")
        s_exp = m.sem("exped")
        s_vq = m.sem("v_staged")
        s_pv = m.sem("pv")
        s_acc = m.sem("acc_copied")
        s_comb = m.sem("combined")
        s_rsum = m.sem("rsum")
        s_misc = m.sem("misc_read")
        last_b = B - 1

        def batches(eng, body):
            body(0, True, False)
            with eng.Fori(1, last_b) as b:
                body(b, False, False)
            body(last_b, False, True)

        def prev(b, s):
            return (b, s - 1) if s else (b - 1, NQ - 1)

        def nxt(b, s, k):
            return (b, s + k) if s + k < NQ else (b + 1, s + k - NQ)

        block = m.block()

        @block.gpsimd
        def _(pool):
            pool.memset(vq[:, :, :, :], 0.0).then_inc(s_clear, 1)
            pool.wait_ge(s_clear, 1)

            def body(b, first, last):
                for s in range(NQ):
                    if not (first and s == 0):
                        pool.wait_ge(s_vq, NQ * b + s)
                    if not (first and s < 2):
                        pool.wait_ge(s_pv, 4 * TB * (NQ * b + s - 1))
                    pool.tensor_copy(vq[:, s % 2, :, 0:GH * VW],
                                     g.v1[:, bass.ds(b * TB, TB), s * GH:(s + 1) * GH, :].rearrange(
                                         "p t g r -> p t (g r)")).then_inc(s_vq, 1)
            batches(pool, body)

        @block.sync
        def _(sp):
            def load(b, s):
                heads = slice(s * GH, (s + 1) * GH)
                tok = bass.ds(b * S, S)
                for i in range(NPART):
                    row = i * NPART * K1
                    sp.dma_start(k_op[s][row:row + NPART * K1, :, :],
                                 scr.terms[1][:, :, heads, tok].rearrange("j d h t -> (j d) h t")
                                 ).then_inc(s_load[s], 16)
                    for j in range(NPART):
                        sp.dma_start(q_op[s][row + j * K1:row + (j + 1) * K1, :, :],
                                     scr.terms[0][i, :, heads, tok]).then_inc(s_load[s], 16)

            def max_rows(u, s):
                sp.wait_ge(s_nmp, u + 1)
                for i in range(NPART):
                    sp.dma_start(q_op[s][R_MAX + i:R_MAX + i + 1, :, :].rearrange("o g t -> o (g t)"),
                                 nm_parts[:, s % 2, i, :]).then_inc(s_nmrow, 16)

            for s in range(NQ):
                load(0, s)
            max_rows(0, 0)

            def body(b, first, last):
                for s in range(NQ):
                    if not (last and s == NQ - 1):
                        max_rows(NQ * b + s + 1, (s + 1) % NQ)
                    if not last:
                        sp.wait_ge(s_prob, 2 * STEPS * (NQ * b + s + 1))
                        load(b + 1, s)
            batches(sp, body)

        LOADS = 16 * (NPART + NPART * NPART)

        @block.tensor
        def _(pe):
            def scores_for_max(b, s, a, k):
                u = NQ * b + s
                if k == 0:
                    if a == 0:
                        pe.wait_ge(s_load[s], LOADS * (b + 1))
                    if not (isinstance(b, int) and b == 0 and s == 0 and a < 2):
                        pe.wait_ge(s_maxed, STEPS * u + a - 1)
                h, qt = a // TB, a % TB
                mm = pe.matmul(ps_max[:, a % 2, k * CH:(k + 1) * CH], q_op[s][0:R_ALL, h, qt * P:(qt + 1) * P],
                               k_op[s][0:R_ALL, h, k * CH:(k + 1) * CH], start=True, stop=True)
                if k == 1:
                    mm.then_inc(s_scored, 1)

            def scores_for_prob(b, s, j):
                u = NQ * b + s
                half, kt, h = j // STEPS, j % STEPS // GH, j % GH
                if j == 0:
                    pe.wait_ge(s_nmrow, 16 * NPART * (u + 1))
                if not (isinstance(b, int) and b == 0 and s == 0 and j < 2):
                    pe.wait_ge(s_exp, 2 * STEPS * u + j - 1)
                pe.matmul(ps_prob[:, j % 2, :], k_op[s][0:R_END, h, kt * P:(kt + 1) * P],
                          q_op[s][0:R_END, h, half * CH:(half + 1) * CH], start=True,
                          stop=True).then_inc(s_prob, 1)

            def pv(b, s, v, part):
                u = NQ * b + s
                half, kt = v // TB, v % TB
                cols = slice(part * CH // 2, (part + 1) * CH // 2)
                if part == 0:
                    pe.wait_ge(s_exp, 2 * STEPS * u + GH * (v + 1))
                    if v == 0:
                        pe.wait_ge(s_vq, u + 1)
                    if kt == 0 and not (isinstance(b, int) and b == 0 and s == 0 and half == 0):
                        pe.wait_ge(s_acc, 2 * u + half)
                for h in range(GH):
                    mm = pe.matmul(ps_acc[32 * h:32 * h + 32, cols], vq[:, s % 2, kt, VW * h:VW * h + 32],
                                   probs[:, (GH * v + h) % PROBS, cols], start=(kt == 0 and part == 0),
                                   stop=(kt == TB - 1 and part == 1))
                mm.then_inc(s_pv, 1)

            def combine(b, s, half, last=False):
                u = NQ * b + s
                pe.wait_ge(s_acc, 2 * u + half + 1)
                pe.wait_ge(s_misc, 3 * u + 1 + 2 * half - last)
                for t in range(CT):
                    mm = pe.matmul(comb[:, t], acc_sb[:, half, t * P:(t + 1) * P],
                                   g.ident[:, :].rearrange("p (g r) -> p g r", g=GH)[:, :, 0:VW],
                                   start=True, stop=True)
                mm.then_inc(s_comb, 1)

            def turn_max(b, s):
                u = NQ * b + s
                pe.wait_ge(s_maxed, STEPS * (u + 1))
                if not (isinstance(b, int) and b == 0 and s == 0):
                    pe.wait_ge(s_misc, 3 * u - 1)
                pe.transpose(ps_misc[0:STEPS, 0:P], negmax[:, s % 2, :], g.ident[:, :]).then_inc(s_nmT, 1)

            for a in range(STEPS):
                for k in range(2):
                    scores_for_max(0, 0, a, k)
            turn_max(0, 0)
            for a in range(LEAD):
                for k in range(2):
                    scores_for_max(0, 1, a, k)

            def body(b, first, last):
                for s in range(NQ):
                    for i in range(STEPS):
                        a = i + LEAD
                        k, a = (1, a) if a < STEPS else (2, a - STEPS)
                        for half in range(2):
                            if not (last and s + k >= NQ):
                                scores_for_max(*nxt(b, s, k), a, half)
                            scores_for_prob(b, s, 2 * i + half)
                        w = i - PV_LAG
                        for w in (w - 1, w) if w % (2 * TB) == 1 else () if w % (2 * TB) == 0 else (w,):
                            if w >= 0:
                                pv(b, s, w // 2, w % 2)
                            elif not (first and s == 0):
                                pv(*prev(b, s), (w + STEPS) // 2, w % 2)
                        if i == PV_LAG + 1 and not (first and s == 0):
                            combine(*prev(b, s), 1)
                        if i == STEPS // 2 + PV_LAG + 1:
                            combine(b, s, 0)
                        if i == STEPS - LEAD + 1 and not (last and s == NQ - 1):
                            turn_max(*nxt(b, s, 1))
            batches(pe, body)
            for w in range(STEPS - PV_LAG, STEPS):
                pv(last_b, NQ - 1, w // 2, w % 2)
            combine(last_b, NQ - 1, 1, last=True)

        @block.scalar
        def _(act):
            def copy_acc(b, s, half):
                u = NQ * b + s
                act.wait_ge(s_pv, 4 * TB * u + 2 * TB * (half + 1))
                if not (isinstance(b, int) and b == 0 and s == 0):
                    act.wait_ge(s_comb, 2 * u + half - 1)
                act.activation(acc_sb[:, half, :], ps_acc[:, :], ACT.Copy).then_inc(s_acc, 1)

            def body(b, first, last):
                for s in range(NQ):
                    u = NQ * b + s
                    for j in range(2 * STEPS):
                        if j == 2 * PV_LAG + 1 and not (first and s == 0):
                            copy_acc(*prev(b, s), 1)
                        if j == STEPS + 2 * PV_LAG + 1:
                            copy_acc(b, s, 0)
                        act.wait_ge(s_prob, 2 * STEPS * u + j + 1)
                        if j % GH == 0 and not (first and s == 0 and j < PROBS):
                            act.wait_ge(s_pv, 4 * TB * u + 2 * ((j - PROBS) // GH + 1))
                        act.activation(probs[:, j % PROBS, :], ps_prob[:, j % 2, :], ACT.Exp).then_inc(s_exp, 1)
            batches(act, body)
            copy_acc(last_b, NQ - 1, 1)

        @block.vector
        def _(dve):
            def reduce_max(b, s, a):
                u = NQ * b + s
                dve.wait_ge(s_scored, STEPS * u + a + 1)
                if a == 0 and not (isinstance(b, int) and b == 0 and s < 2):
                    dve.wait_ge(s_nmT, u - 1)
                dve.tensor_reduce(negmax[:, s % 2, a:a + 1], ps_max[:, a % 2, :], AX.X, ALU.max,
                                  negate=True).then_inc(s_maxed, 1)

            def split_max(b, s):
                u = NQ * b + s
                dve.wait_ge(s_nmT, u + 1)
                if not (isinstance(b, int) and b == 0 and s < 2):
                    dve.wait_ge(s_nmrow, 16 * NPART * (u - 1))
                chain = Count(dve, s_nmch, 4 * u)
                rows, rest, parts = nm_rows[:, :], nm_rest[:, :], nm_parts[:, s % 2]
                ins = dve.tensor_copy(rows, ps_misc[0:STEPS, 0:P])
                ins.then_inc(s_misc, 1)
                dve.wait_ge(s_misc, 1 if isinstance(u, int) and u == 0 else 3 * u)
                chain.done(dve.tensor_copy(parts[:, 0, :], rows))
                chain.done(dve.tensor_tensor(rest, rows, parts[:, 0, :], ALU.subtract))
                chain.done(dve.tensor_copy(parts[:, 1, :], rest))
                chain.done(dve.tensor_tensor(rows, rest, parts[:, 1, :], ALU.subtract))
                dve.tensor_copy(parts[:, 2, :], rows).then_inc(s_nmp, 1)

            def normalise(b, s, half):
                u = NQ * b + s
                dve.wait_ge(s_comb, 2 * u + half + 1)
                dve.reciprocal(rsum[:, half, :, :], comb[:, :, :, D]).then_inc(s_rsum, 1)
                dve.wait_ge(s_rsum, 2 * u + half + 1)
                for t in range(CT):
                    tile = b * TB + half * CT + t
                    out = g.o[:, bass.ds(tile, 1), s * GH * D:(s + 1) * GH * D].rearrange(
                        "p o (g d) -> p (o g) d", g=GH)
                    ins = dve.tensor_tensor(out, comb[:, t, :, 0:D],
                                            rsum[:, half, t, :].unsqueeze(2).to_broadcast([P, GH, D]), ALU.mult)
                ins.then_inc(s_misc, 1)

            for a in range(STEPS):
                reduce_max(0, 0, a)
            split_max(0, 0)
            for a in range(LEAD):
                reduce_max(0, 1, a)

            def body(b, first, last):
                for s in range(NQ):
                    for i in range(STEPS):
                        a = i + LEAD
                        k, a = (1, a) if a < STEPS else (2, a - STEPS)
                        if not (last and s + k >= NQ):
                            reduce_max(*nxt(b, s, k), a)
                        if i == PV_LAG + 3 and not (first and s == 0):
                            normalise(*prev(b, s), 1)
                        if i == STEPS // 2 + PV_LAG + 3:
                            normalise(b, s, 0)
                        if i == STEPS - LEAD + 2 and not (last and s == NQ - 1):
                            split_max(*nxt(b, s, 1))
            batches(dve, body)
            normalise(last_b, NQ - 1, 1)


def project_out_a(nc, g):
    with ExitStack() as ctx:
        m = Mem(nc, ctx, "oproj")
        stage = m.sb("stage", [P, 2, CT, P])
        oT = m.sb("oT", [P, 2, CH])
        ps_t = [m.ps(f"ps_t{p}", [P, CH]) for p in range(2)]
        ps_y = [m.ps(f"ps_y{p}", [P, CH]) for p in range(2)]
        s_st = m.sems("staged", 2)
        s_turn = m.sems("turned", 2)
        s_oT = m.sems("oT", 2)
        s_y = m.sems("y", 2)
        s_add = m.sems("added", 2)
        block = m.block()

        @block.scalar
        def _(act):
            def body(i):
                for p in range(2):
                    wait_used(act, s_turn[p], i)
                    act.activation(stage[:, p, :, :], g.o[:, bass.ds((2 * i + p) * CT, CT), :],
                                   ACT.Copy).then_inc(s_st[p], 1)
            repeat(act, NC_ // 2, body)

        @block.tensor
        def _(pe):
            def body(i):
                for p in range(2):
                    pe.wait_ge(s_st[p], i + 1)
                    wait_used(pe, s_oT[p], i)
                    for t in range(CT):
                        mm = pe.transpose(ps_t[p][:, t * P:(t + 1) * P], stage[:, p, t, :], g.ident[:, :])
                    mm.then_inc(s_turn[p], 1)
                    pe.wait_ge(s_oT[p], i + 1)
                    wait_used(pe, s_add[p], i)
                    for t in range(CT):
                        mm = pe.matmul(ps_y[p][:, t * P:(t + 1) * P], oT[:, p, t * P:(t + 1) * P],
                                       g.wT[:, 3, :], start=True, stop=True)
                    mm.then_inc(s_y[p], 1)
            repeat(pe, NC_ // 2, body)

        @block.vector
        def _(dve):
            def body(i):
                for p in range(2):
                    dve.wait_ge(s_turn[p], i + 1)
                    wait_used(dve, s_y[p], i)
                    dve.tensor_copy(oT[:, p, :], ps_t[p][:, :]).then_inc(s_oT[p], 1)
                for p in range(2):
                    dve.wait_ge(s_y[p], i + 1)
                    xc = g.x[:, bass.ds((2 * i + p) * CT, CT), :]
                    dve.tensor_tensor(xc, xc, ps_y[p][:, :].rearrange("p (t c) -> p t c", t=CT),
                                      ALU.add).then_inc(s_add[p], 1)
                    dve.wait_ge(s_add[p], i + 1)
                    for t in range(CT):
                        bn_stats_of(nc, g, (2 * i + p) * CT + t)
            repeat(dve, NC_ // 2, body)


def normalise_and_turn(nc, g, phase, xnT):
    with ExitStack() as ctx:
        m = Mem(nc, ctx, phase)
        xn = m.sb("xn", [P, 2, CT, P])
        xnc = m.sb("xnc", [P, 2, CH])
        ps_t = [m.ps(f"ps_t{p}", [P, CH]) for p in range(2)]
        s_xn = m.sems("xn", 2)
        s_turn = m.sems("turned", 2)
        s_xnc = m.sems("xnc", 2)
        s_copy = m.sems("copied", 2)
        block = m.block()

        @block.scalar
        def _(act):
            def body(i):
                for p in range(2):
                    wait_used(act, s_turn[p], i)
                    for t in range(CT):
                        tile = (2 * i + p) * CT + t
                        ins = act.activation(xn[:, p, t, :], g.x[:, bass.ds(tile, 1), :], ACT.Identity,
                                             bias=g.nmr[:, bass.ds(tile, 1)], scale=g.rstd[:, bass.ds(tile, 1)])
                    ins.then_inc(s_xn[p], 1)
                for p in range(2):
                    act.wait_ge(s_xnc[p], i + 1)
                    act.activation(xnT[:, bass.ds((2 * i + p) * CH, CH)], xnc[:, p, :],
                                   ACT.Copy).then_inc(s_copy[p], 1)
            repeat(act, NC_ // 2, body)

        @block.tensor
        def _(pe):
            def body(i):
                for p in range(2):
                    pe.wait_ge(s_xn[p], i + 1)
                    wait_used(pe, s_xnc[p], i)
                    for t in range(CT):
                        mm = pe.transpose(ps_t[p][:, t * P:(t + 1) * P], xn[:, p, t, :], g.ident[:, :])
                    mm.then_inc(s_turn[p], 1)
            repeat(pe, NC_ // 2, body)

        @block.vector
        def _(dve):
            def body(i):
                for p in range(2):
                    dve.wait_ge(s_turn[p], i + 1)
                    wait_used(dve, s_copy[p], i)
                    dve.tensor_copy(xnc[:, p, :], ps_t[p][:, :]).then_inc(s_xnc[p], 1)
            repeat(dve, NC_ // 2, body)


def moe(nc, g, ins, phase, norm_next):
    with ExitStack() as ctx:
        m = Mem(nc, ctx, phase)
        MF = F // P
        w1 = m.sb("w1", [P, E, F])
        w3 = m.sb("w3", [P, E, F])
        w2 = m.sb("w2", [P, E, MF, P])
        gate = m.sb("gate", [P, MF, CH])
        hT = m.sb("hT", [P, 2, MF, CH])
        ps_1 = [m.ps(f"ps_1{i}", [P, CH]) for i in range(MF)]
        ps_3 = [m.ps(f"ps_3{i}", [P, CH]) for i in range(MF)]
        ps_y = [m.ps(f"ps_y{i}", [P, CT, P]) for i in range(2)]
        xn = m.sb("xn", [P, CT, P])
        xnc = m.sb("xnc", [P, CH])
        xnT = m.sb("xnT", [P, N])
        logits = m.sb("logits", [P, CT, E])
        route = m.sb("route", [P, NT, E])
        rank = m.sb("rank", [P, E])
        best = m.sb("best", [P, 2, CT])
        at = m.sb("at", [P, CT, E])
        index = m.sb("index", [P, 2, CT])
        hot = [m.sb(f"hot{i}", [P, CT, E]) for i in range(2)]
        left = m.sb("left", [P, CT, E])
        gap = m.sb("gap", [P, 2, CT])
        weight = m.sb("weight", [P, 2, CT])
        ps_t = m.ps("ps_t", [P, CH])
        ps_l = m.ps("ps_l", [P, CT, E])
        s_xn = m.sem("xn")
        s_turn = m.sem("turned")
        s_xnc = m.sem("xnc")
        s_copy = m.sem("xnT")
        s_log = m.sem("logits")
        s_lout = m.sem("logits_out")
        s_rank = m.sem("rank")
        s_chain = m.sem("route_chain")
        s_gap = m.sem("gap")
        s_weight = m.sem("weight")
        wide = lambda a: a.unsqueeze(2).to_broadcast([P, CT, E])
        ROUTE = 14
        s_w13 = m.sem("w13_loaded")
        s_w2 = m.sem("w2_loaded")
        s_1 = m.sem("h1")
        s_3 = m.sem("h3")
        s_silu = m.sem("silu")
        s_h = m.sem("h")
        s_y = m.sem("y")
        s_add = m.sem("added")
        block = m.block()

        def chunks(eng, body):
            body(0, False)
            with eng.Fori(1, NC_ - 1) as c:
                body(c, False)
            body(NC_ - 1, True)

        @block.gpsimd
        def _(pool):
            pool.iota(rank[:, :], pattern=[[-1, E]], base=E, channel_multiplier=0,
                      allow_small_or_imprecise_dtypes=True).then_inc(s_rank, 1)

        @block.sync
        def _(sp):
            for e in range(E):
                sp.dma_start(w1[:, e, :], ins["f_w1"][e]).then_inc(s_w13, 16)
                sp.dma_start(w3[:, e, :], ins["f_w3"][e]).then_inc(s_w13, 16)
                sp.dma_start(w2[:, e, :, :], ins["f_w2"][e].rearrange("(m p) c -> p m c", p=P)).then_inc(s_w2, 16)

        @block.tensor
        def _(pe):
            def turn(c):
                pe.wait_ge(s_xn, c + 1)
                wait_used(pe, s_xnc, c)
                for t in range(CT):
                    mm = pe.transpose(ps_t[:, t * P:(t + 1) * P], xn[:, t, :], g.ident[:, :])
                mm.then_inc(s_turn, 1)

            def router(c):
                pe.wait_ge(s_xnc, c + 1)
                wait_used(pe, s_lout, c)
                for t in range(CT):
                    mm = pe.matmul(ps_l[:, t, :], xnc[:, t * P:(t + 1) * P], g.gate_w[:, :], start=True, stop=True)
                mm.then_inc(s_log, 1)

            def hidden(c, e):
                k = c * E + e
                if e == 0:
                    pe.wait_ge(s_copy, c + 1)
                for i in range(MF):
                    for w, ps, s, read in ((w1, ps_1, s_1, s_silu), (w3, ps_3, s_3, s_h)):
                        wait_used(pe, read, MF * (k - 1) + i + 1)
                        pe.matmul(ps[i][:, :], w[:, e, i * P:(i + 1) * P], xnT[:, bass.ds(c * CH, CH)],
                                  start=True, stop=True).then_inc(s, 1)

            def down(c, e):
                k = c * E + e
                wait_used(pe, s_add, k - 1)
                pe.wait_ge(s_h, MF * (k + 1))
                for t in range(CT):
                    for i in range(MF):
                        mm = pe.matmul(ps_y[e % 2][:, t, :], hT[:, e % 2, i, t * P:(t + 1) * P],
                                       w2[:, e, i, :], start=(i == 0), stop=(i == MF - 1))
                mm.then_inc(s_y, 1)

            turn(0)
            router(0)
            pe.wait_ge(s_w13, 16 * 2 * E)
            pe.wait_ge(s_w2, 16 * E)

            def body(c, last):
                for e in range(E):
                    hidden(c, e)
                    if e:
                        down(c, e - 1)
                    elif not (isinstance(c, int) and c == 0):
                        down(c - 1, E - 1)
                    if e == 1 and not last:
                        turn(c + 1)
                    if e == 3 and not last:
                        router(c + 1)
            chunks(pe, body)
            down(NC_ - 1, E - 1)

        @block.scalar
        def _(act):
            def normalise(c):
                wait_used(act, s_turn, c)
                for t in range(CT):
                    tile = c * CT + t
                    ins = act.activation(xn[:, t, :], g.x[:, bass.ds(tile, 1), :], ACT.Identity,
                                         bias=g.nmr[:, bass.ds(tile, 1)], scale=g.rstd[:, bass.ds(tile, 1)])
                ins.then_inc(s_xn, 1)

            def copy(c):
                act.wait_ge(s_xnc, c + 1)
                act.activation(xnT[:, bass.ds(c * CH, CH)], xnc[:, :], ACT.Copy).then_inc(s_copy, 1)

            def weigh(c):
                act.wait_ge(s_gap, 2 * (c + 1))
                act.activation(weight[:, :, :], gap[:, :, :], ACT.Sigmoid).then_inc(s_weight, 1)

            normalise(0)
            copy(0)
            weigh(0)

            def body(c, last):
                for e in range(E):
                    for i in range(MF):
                        n = MF * (c * E + e) + i
                        act.wait_ge(s_1, n + 1)
                        wait_used(act, s_h, n - MF + 1)
                        act.activation(gate[:, i, :], ps_1[i][:, :], ACT.Silu).then_inc(s_silu, 1)
                    if e == 0 and not last:
                        normalise(c + 1)
                    if e == 3 and not last:
                        copy(c + 1)
                    if e == 5 and not last:
                        weigh(c + 1)
            chunks(act, body)

        @block.vector
        def _(dve):
            ranks = rank[:, :].unsqueeze(1).to_broadcast([P, CT, E])

            def take_turned(c):
                dve.wait_ge(s_turn, c + 1)
                wait_used(dve, s_copy, c)
                wait_used(dve, s_log, c)
                dve.tensor_copy(xnc[:, :], ps_t[:, :]).then_inc(s_xnc, 1)

            def find_best(c, i):
                src = (logits, left)[i]
                chain = Count(dve, s_chain, ROUTE * c + 6 * i)
                if i == 0:
                    dve.wait_ge(s_log, c + 1)
                    dve.tensor_copy(logits[:, :, :], ps_l[:, :, :]).then_inc(s_lout, 1)
                    dve.wait_ge(s_lout, c + 1)
                chain.done(dve.tensor_reduce(best[:, i, :], src[:, :, :], AX.X, ALU.max))
                chain.done(dve.tensor_tensor(at[:, :, :], src[:, :, :], wide(best[:, i, :]), ALU.is_equal))
                chain.done(dve.tensor_tensor(at[:, :, :], at[:, :, :], ranks, ALU.mult))
                chain.done(dve.tensor_reduce(index[:, i, :], at[:, :, :], AX.X, ALU.max))
                chain.done(dve.tensor_tensor(hot[i][:, :, :], wide(index[:, i, :]), ranks, ALU.is_equal))
                if i == 0:
                    chain.done(dve.scalar_tensor_tensor(out=left[:, :, :], in0=hot[0][:, :, :], scalar=-3e38,
                                                        in1=logits[:, :, :], op0=ALU.mult, op1=ALU.add))
                else:
                    dve.tensor_tensor(gap[:, 0, :], best[:, 0, :], best[:, 1, :], ALU.subtract).then_inc(s_gap, 1)
                    dve.tensor_tensor(gap[:, 1, :], best[:, 1, :], best[:, 0, :], ALU.subtract).then_inc(s_gap, 1)

            def write_route(c):
                chain = Count(dve, s_chain, ROUTE * c + 11)
                dve.wait_ge(s_weight, c + 1)
                for i in range(2):
                    chain.done(dve.tensor_tensor(hot[i][:, :, :], hot[i][:, :, :], wide(weight[:, i, :]), ALU.mult))
                chain.done(dve.tensor_tensor(route[:, bass.ds(c * CT, CT), :], hot[0][:, :, :], hot[1][:, :, :],
                                             ALU.add))

            def product(c, e):
                k = c * E + e
                wait_used(dve, s_y, k - 1)
                for i in range(MF):
                    n = MF * k + i
                    dve.wait_ge(s_silu, n + 1)
                    dve.wait_ge(s_3, n + 1)
                    dve.tensor_tensor(hT[:, e % 2, i, :], gate[:, i, :], ps_3[i][:, :], ALU.mult).then_inc(s_h, 1)

            def add(c, e):
                k = c * E + e
                dve.wait_ge(s_y, k + 1)
                wait_used(dve, s_add, k)
                for t in range(CT):
                    xt = g.x[:, bass.ds(c * CT + t, 1), :].rearrange("p o c -> p (o c)")
                    ins = dve.scalar_tensor_tensor(
                        out=xt, in0=ps_y[e % 2][:, t, :],
                        scalar=route[:, bass.ds(c * CT + t, 1), e:e + 1].rearrange("p o c -> p (o c)"),
                        in1=xt, op0=ALU.mult, op1=ALU.add)
                ins.then_inc(s_add, 1)

            def stats_of_chunk(c):
                dve.wait_ge(s_add, E * (c + 1))
                for t in range(CT):
                    bn_stats_of(nc, g, c * CT + t)

            take_turned(0)
            dve.wait_ge(s_rank, 1)
            find_best(0, 0)
            find_best(0, 1)
            write_route(0)

            def body(c, last):
                for e in range(E):
                    product(c, e)
                    if e:
                        add(c, e - 1)
                    elif not (isinstance(c, int) and c == 0):
                        add(c - 1, E - 1)
                        if norm_next:
                            stats_of_chunk(c - 1)
                    if last:
                        continue
                    if e == 2:
                        take_turned(c + 1)
                    if e in (4, 5):
                        find_best(c + 1, e - 4)
                    if e == 6:
                        write_route(c + 1)
            chunks(dve, body)
            add(NC_ - 1, E - 1)
            if norm_next:
                stats_of_chunk(NC_ - 1)


def moe_layer(nc, g, ins, phase, norm_next):
    layer_norm_scales(nc, g, phase + "_ln")
    moe(nc, g, ins, phase + "_moe", norm_next)


K = 4
LEFT = K // 2


def gates(nc, g, scr, xnT):
    with ExitStack() as ctx:
        m = Mem(nc, ctx, "gates")
        ab = m.sb("ab", [48, N])
        ps = [m.ps(f"ps{p}", [48, CH]) for p in range(2)]
        s_mm = m.sems("projected", 2)
        s_sig = m.sems("sigmoid", 2)
        s_out = m.sem("stored")
        block = m.block()

        @block.tensor
        def _(pe):
            def body(i):
                for p in range(2):
                    wait_used(pe, s_sig[p], i)
                    pe.matmul(ps[p][:, :], g.gatesT[:, :], xnT[:, bass.ds((2 * i + p) * CH, CH)],
                              start=True, stop=True).then_inc(s_mm[p], 1)
            repeat(pe, NC_ // 2, body)

        @block.scalar
        def _(act):
            def body(i):
                for p in range(2):
                    act.wait_ge(s_mm[p], i + 1)
                    act.activation(ab[:, bass.ds((2 * i + p) * CH, CH)], ps[p][:, :], ACT.Sigmoid,
                                   bias=g.bias_ab[:, :]).then_inc(s_sig[p], 1)
            repeat(act, NC_ // 2, body)

        @block.sync
        def _(sp):
            for p in range(2):
                sp.wait_ge(s_sig[p], NC_ // 2)
            for i in range(2):
                sp.dma_start(scr.ab[i], ab[32 * i:32 * i + H, :]).then_inc(s_out, 16)
            sp.wait_ge(s_out, 32)


def project_conv(nc, g, scr, xnT, sumsq):
    with ExitStack() as ctx:
        m = Mem(nc, ctx, "conv")
        u = m.sb("u", [P, 3, LEFT + S + K - 1 - LEFT])
        y = m.sb("y", [P, 3, S])
        z = m.sb("z", [P, 3, S])
        sq = m.sb("sq", [P, 2, S])
        HB = S // CH
        ps = [[m.ps(f"ps{w}{i}", [P, CH]) for i in range(HB)] for w in range(3)]
        ps_s = m.ps("ps_s", [P, 2, TB])
        s_pad = m.sem("padded")
        s_mm = m.sems("projected", 3)
        s_u = m.sems("u", 3)
        s_tap = m.sem("tap")
        s_y = m.sems("y", 3)
        s_z = m.sems("z", 3)
        s_sq = m.sems("squared", 2)
        s_sum = m.sem("summed")
        s_ss = m.sem("sums_out")
        s_out = m.sems("stored", 3)
        block = m.block()

        @block.gpsimd
        def _(pool):
            pool.memset(u[:, :, 0:LEFT], 0.0).then_inc(s_pad, 1)
            pool.wait_ge(s_pad, 1)
            pool.memset(u[:, :, LEFT + S:], 0.0).then_inc(s_pad, 1)

        @block.tensor
        def _(pe):
            def body(b):
                for w in range(3):
                    wait_used(pe, s_u[w], b)
                    for i in range(HB):
                        mm = pe.matmul(ps[w][i][:, :], g.wT[:, 4 + w, :],
                                       xnT[:, bass.ds(b * S + i * CH, CH)], start=True, stop=True)
                    mm.then_inc(s_mm[w], 1)
                wait_used(pe, s_ss, b)
                for w in range(2):
                    pe.wait_ge(s_sq[w], b + 1)
                    for t in range(TB):
                        mm = pe.matmul(ps_s[:, w, t:t + 1], sq[:, w, t * P:(t + 1) * P], g.ones[:, 0:1],
                                       start=True, stop=True)
                mm.then_inc(s_sum, 1)
            repeat(pe, B, body)

        @block.scalar
        def _(act):
            act.wait_ge(s_pad, 2)

            def body(b):
                for w in range(3):
                    act.wait_ge(s_mm[w], b + 1)
                    wait_used(act, s_y[w], b)
                    for i in range(HB):
                        ins = act.activation(u[:, w, LEFT + i * CH:LEFT + (i + 1) * CH], ps[w][i][:, :],
                                             ACT.Silu, bias=g.bias_qkv[:, w:w + 1])
                    ins.then_inc(s_u[w], 1)
                for w in range(3):
                    act.wait_ge(s_y[w], b + 1)
                    wait_used(act, s_out[w], 16 * b)
                    act.activation(z[:, w, :], y[:, w, :], ACT.Silu).then_inc(s_z[w], 1)
                    if w < 2:
                        act.wait_ge(s_z[w], b + 1)
                        wait_used(act, s_sum, b)
                        act.activation(sq[:, w, :], z[:, w, :], ACT.Square).then_inc(s_sq[w], 1)
            repeat(act, B, body)

        @block.vector
        def _(dve):
            def body(b):
                for w in range(3):
                    dve.wait_ge(s_u[w], b + 1)
                    wait_used(dve, s_z[w], b)
                    taps = Count(dve, s_tap, (K - 1) * (3 * b + w))
                    taps.done(dve.tensor_scalar(y[:, w, :], u[:, w, 0:S], g.conv[:, w, 0:1], None, ALU.mult))
                    for j in range(1, K):
                        ins = dve.scalar_tensor_tensor(out=y[:, w, :], in0=u[:, w, j:j + S],
                                                       scalar=g.conv[:, w, j:j + 1], in1=y[:, w, :],
                                                       op0=ALU.mult, op1=ALU.add)
                        if j < K - 1:
                            taps.done(ins)
                    ins.then_inc(s_y[w], 1)
                dve.wait_ge(s_sum, b + 1)
                dve.tensor_copy(sumsq[:, :, bass.ds(b * TB, TB)], ps_s[:, :, :]).then_inc(s_ss, 1)
            repeat(dve, B, body)

        @block.sync
        def _(sp):
            def body(b):
                for w in range(3):
                    sp.wait_ge(s_z[w], b + 1)
                    sp.dma_start(scr.qkv[w][:, bass.ds(b * S, S)], z[:, w, :]).then_inc(s_out[w], 16)
            repeat(sp, B, body)
            for w in range(3):
                sp.wait_ge(s_out[w], 16 * B)


def l2_norms(nc, g, scr, sumsq, q_scale):
    with ExitStack() as ctx:
        m = Mem(nc, ctx, "l2")
        norm = m.sb("norm", [P, 2, NT])
        inv = m.sb("inv", [P, 2, NT])
        rows = m.sb("rows", [NT, P])
        ps = m.ps("ps", [P, P])
        s_norm = m.sem("norm")
        s_chain = m.sem("chain")
        s_turn = m.sem("turned")
        s_rows = m.sem("rows")
        s_out = m.sem("stored")
        block = m.block()

        @block.scalar
        def _(act):
            act.activation(norm[:, :, :], sumsq[:, :, :], ACT.Sqrt).then_inc(s_norm, 1)

        @block.vector
        def _(dve):
            chain = Count(dve, s_chain)
            dve.wait_ge(s_norm, 1)
            chain.done(dve.tensor_scalar(norm[:, :, :], norm[:, :, :], L2_EPS, None, ALU.add))
            chain.done(dve.reciprocal(inv[:, :, :], norm[:, :, :]))
            dve.tensor_copy(q_scale[:, :], inv[:, 0, :])
            dve.wait_ge(s_turn, 1)
            dve.tensor_copy(rows[:, :], ps[0:NT, :]).then_inc(s_rows, 1)

        @block.tensor
        def _(pe):
            pe.wait_ge(s_chain, 2)
            pe.transpose(ps[0:NT, :], inv[:, 1, :], g.ident[:, :]).then_inc(s_turn, 1)

        @block.sync
        def _(sp):
            sp.wait_ge(s_rows, 1)
            sp.dma_start(scr.k_scale.rearrange("(t p) -> t p", p=P), rows[:, :]).then_inc(s_out, 16)
            sp.wait_ge(s_out, 16)


L = 8
TH = S // 2
LB = TH // L
R = D // 2
W = P
WB = W // L
NW = S // W


def solve_and_scan(nc, g, scr, q, k_chan, a_chan):
    with ExitStack() as ctx:
        m = Mem(nc, ctx, "solve")
        k = m.sb("k", [P, D, TH])
        X = m.sb("X", [P, 2 * D, TH])
        ab = m.sb("ab", [P, 2, TH])
        k_scale = m.sb("k_scale", [P, TH])
        dec = m.sb("dec", [P, L, LB, L])
        M = m.sb("M", [P, L, LB, L])
        part = m.sb("part", [P, D * LB * (L - 1)])
        red = m.sb("red", [P, D, LB])
        whole = m.sb("whole", [P, TH])
        end = m.sb("end", [P, LB])
        xw = m.sb("xw", [P, 2, D, W])
        kd = m.sb("kd", [P, 2, D, W])
        xv = m.sb("xv", [P, 2, R, W])
        decay = m.sb("decay", [P, 2, WB])
        St = m.sb("state", [P, R, D])
        p1 = m.sb("p1", [P, 2, R, L, D + 1])
        p2 = m.sb("p2", [P, R, D, L + 1])
        s_in = m.sem("loaded")
        s_one = m.sem("ones")
        s_scaled = m.sem("k_scaled")
        s_kout = m.sem("k_stored")
        s_chain = m.sem("chain")
        s_ready = m.sem("solved")
        s_win = m.sems("window_loaded", 2)
        s_step = m.sems("step", 2)
        s_addend = m.sem("addend")
        s_decayed = m.sem("decayed")
        s_uout = m.sems("u_stored", 2)
        s_chan = m.sem("channels_loaded")
        s_kchan = m.sem("k_channels_loaded")
        HALF = P // 2
        LOADS = 2 * 4
        STEP = 4
        block = m.block()

        @block.sync
        def _(sp):
            lanes = [(th, b, slice(HALF * th + H * b, HALF * th + H * (b + 1)),
                      slice(b * S + th * TH, b * S + (th + 1) * TH)) for th in range(2) for b in range(B)]
            for th, b, lane, tok in lanes:
                sp.dma_start(k[lane, :, :], scr.qkv[1][:, tok].rearrange("(h d) t -> h d t", h=H)
                             ).then_inc(s_in, 16)
                sp.dma_start(k_scale[lane, :], scr.k_scale[tok].unsqueeze(0).to_broadcast([H, TH])
                             ).then_inc(s_in, 16)
                sp.dma_start(ab[lane, :, :], scr.ab[:, :, tok].rearrange("i h t -> h i t")
                             ).then_inc(s_in, 16)
            for th, b, lane, tok in lanes:
                sp.dma_start(X[lane, 0:D, :], scr.qkv[2][:, tok].rearrange("(h d) t -> h d t", h=H)
                             ).then_inc(s_in, 16)
            sp.dma_start(q[:, :], scr.qkv[0]).then_inc(s_chan, 16)
            sp.dma_start(a_chan[:, :], scr.ab[0].unsqueeze(1).to_broadcast([H, D, N])).then_inc(s_chan, 16)
            sp.wait_ge(s_scaled, 1)
            for th, b, lane, tok in lanes:
                sp.dma_start(scr.k[:, tok].rearrange("(h d) t -> h d t", h=H), k[lane, :, :]).then_inc(s_kout, 16)
            sp.wait_ge(s_kout, 16 * 2 * B)
            sp.dma_start(k_chan[:, :], scr.k).then_inc(s_kchan, 16)

            def store_u(w):
                p = w % 2
                for r in range(2):
                    sp.wait_ge(s_step[r], STEP * WB * (w + 1))
                for dh in range(2):
                    for b in range(B):
                        lane = slice(HALF * dh + H * b, HALF * dh + H * (b + 1))
                        tok = slice(b * S + w * W, b * S + (w + 1) * W)
                        sp.dma_start(scr.u[:, tok].rearrange("(h d) t -> h d t", h=H)[:, dh * R:(dh + 1) * R, :],
                                     xv[lane, p, :, :]).then_inc(s_uout[p], 16)

            sp.wait_ge(s_ready, 1)
            for w in range(NW):
                p, n = w % 2, w // 2
                if n:
                    sp.wait_ge(s_uout[p], 16 * 2 * B * n)
                src = slice(HALF * (w * W // TH), HALF * (w * W // TH + 1))
                t0 = w * W % TH
                tok, blocks = slice(t0, t0 + W), slice(t0 // L, t0 // L + WB)
                for dh in range(2):
                    dst = slice(HALF * dh, HALF * (dh + 1))
                    sp.dma_start(xw[dst, p, :, :], X[src, D:2 * D, tok]).then_inc(s_win[p], 16)
                    sp.dma_start(kd[dst, p, :, :], k[src, :, tok]).then_inc(s_win[p], 16)
                    sp.dma_start(xv[dst, p, :, :], X[src, dh * R:(dh + 1) * R, tok]).then_inc(s_win[p], 16)
                    sp.dma_start(decay[dst, p, :], end[src, blocks]).then_inc(s_win[p], 16)
                if w:
                    store_u(w - 1)
            store_u(NW - 1)
            for p in range(2):
                sp.wait_ge(s_uout[p], 16 * 2 * B * (NW // 2))
            sp.wait_ge(s_chan, 32)
            sp.wait_ge(s_kchan, 16)

        @block.gpsimd
        def _(pool):
            pool.memset(dec[:, :, :, :], 1.0).then_inc(s_one, 1)
            pool.wait_ge(s_one, 1)
            pool.memset(St[:, :, :], 0.0).then_inc(s_one, 1)

        @block.vector
        def _(dve):
            chain = Count(dve, s_chain)
            byblock = lambda a: a.rearrange("p (c j) -> p c j", j=L)
            a3, b3, w3 = byblock(ab[:, 0, :]), byblock(ab[:, 1, :]), byblock(whole[:, :])
            k4 = k[:, :, :].rearrange("p e (c j) -> p e c j", j=L)
            X4 = X[:, :, :].rearrange("p r (c j) -> p r c j", j=L)
            lanes = lambda a, n: a.unsqueeze(1).to_broadcast([P, n, TH])
            dve.wait_ge(s_one, 2)
            dve.wait_ge(s_in, 16 * 8 * B)
            dve.tensor_tensor(k[:, :, :], k[:, :, :], lanes(k_scale[:, :], D), ALU.mult).then_inc(s_scaled, 1)
            dve.tensor_tensor(X[:, 0:D, :], X[:, 0:D, :], lanes(ab[:, 1, :], D), ALU.mult)
            for t in range(1, L):
                chain.done(dve.tensor_tensor(dec[:, t, :, 0:t], dec[:, t - 1, :, 0:t],
                                             a3[:, :, t:t + 1].to_broadcast([P, LB, t]), ALU.mult))
            chain.done(dve.tensor_tensor(w3, dec[:, :, :, 0].rearrange("p t c -> p c t"),
                                         a3[:, :, 0:1].to_broadcast([P, LB, L]), ALU.mult))
            dve.tensor_copy(end[:, :], w3[:, :, L - 1])
            dve.wait_ge(s_scaled, 1)
            chain.done(dve.scalar_tensor_tensor(out=k_scale[:, :], in0=whole[:, :], scalar=-1.0,
                                                in1=ab[:, 1, :], op0=ALU.mult, op1=ALU.mult))
            chain.done(dve.tensor_tensor(X[:, D:2 * D, :], k[:, :, :], lanes(k_scale[:, :], D), ALU.mult))
            for t in range(1, L):
                prod = part[:, 0:LB * t * D].rearrange("p (c i e) -> p c i e", c=LB, e=D)
                at_t = k4[:, :, :, t].rearrange("p e c -> p c e").unsqueeze(2).to_broadcast([P, LB, t, D])
                chain.done(dve.tensor_tensor(prod, k4[:, :, :, 0:t].rearrange("p e c i -> p c i e"), at_t,
                                             ALU.mult))
                Mt = M[:, t, :, 0:t]
                chain.done(dve.tensor_reduce(Mt, prod, AX.X, ALU.add))
                chain.done(dve.tensor_tensor(Mt, Mt, dec[:, t, :, 0:t], ALU.mult))
                chain.done(dve.tensor_tensor(Mt, Mt, b3[:, :, t:t + 1].to_broadcast([P, LB, t]), ALU.mult))
            for t in range(1, L):
                prod = part[:, 0:D * LB * t].rearrange("p (r c i) -> p r c i", r=D, c=LB)
                for rows in (slice(0, D), slice(D, 2 * D)):
                    chain.done(dve.tensor_tensor(prod, X4[:, rows, :, 0:t],
                                                 M[:, t, :, 0:t].unsqueeze(1).to_broadcast([P, D, LB, t]),
                                                 ALU.mult))
                    chain.done(dve.tensor_reduce(red[:, :, :], prod, AX.X, ALU.add))
                    chain.done(dve.tensor_tensor(X4[:, rows, :, t], X4[:, rows, :, t], red[:, :, :],
                                                 ALU.subtract))
            dve.wait_ge(s_kout, 16 * 2 * B)
            dve.tensor_tensor(k4, k4, dec[:, L - 1, :, :].unsqueeze(1).to_broadcast([P, D, LB, L]),
                              ALU.mult).then_inc(s_ready, 1)

            def body(i):
                halves = [slice(r * R // 2, (r + 1) * R // 2) for r in range(2)]
                for p in range(2):
                    dve.wait_ge(s_win[p], 16 * LOADS * (i + 1))
                    for c in range(WB):
                        n = WB * (2 * i + p) + c
                        tok = slice(c * L, (c + 1) * L)
                        xw_t = xw[:, p, :, tok].rearrange("p e i -> p i e")
                        kd_t = kd[:, p, :, tok]
                        for r, rows in enumerate(halves):
                            wait_used(dve, s_step[r], STEP * n)
                            dve.tensor_tensor(p1[:, c % 2, rows, :, 0:D],
                                              St[:, rows, :].unsqueeze(2).to_broadcast([P, R // 2, L, D]),
                                              xw_t.unsqueeze(1).to_broadcast([P, R // 2, L, D]), ALU.mult
                                              ).then_inc(s_step[r], 1)
                        dve.wait_ge(s_addend, n + 1)
                        for r, rows in enumerate(halves):
                            dve.wait_ge(s_step[r], STEP * n + 1)
                            dve.tensor_reduce(xv[:, p, rows, tok], p1[:, c % 2, rows, :, :], AX.X, ALU.add
                                              ).then_inc(s_step[r], 1)
                        for r, rows in enumerate(halves):
                            dve.wait_ge(s_step[r], STEP * n + 2)
                            dve.tensor_tensor(p2[:, rows, :, 0:L],
                                              xv[:, p, rows, tok].unsqueeze(2).to_broadcast([P, R // 2, D, L]),
                                              kd_t.unsqueeze(1).to_broadcast([P, R // 2, D, L]), ALU.mult
                                              ).then_inc(s_step[r], 1)
                        dve.wait_ge(s_decayed, n + 1)
                        for r, rows in enumerate(halves):
                            dve.wait_ge(s_step[r], STEP * n + 3)
                            dve.tensor_reduce(St[:, rows, :], p2[:, rows, :, :], AX.X, ALU.add
                                              ).then_inc(s_step[r], 1)
            repeat(dve, NW // 2, body)

        @block.scalar
        def _(act):
            def body(i):
                for p in range(2):
                    act.wait_ge(s_win[p], 16 * LOADS * (i + 1))
                    for c in range(WB):
                        n = WB * (2 * i + p) + c
                        if c == 0:
                            add_x(p, n, c)
                        wait_used(act, s_step[1], STEP * n)
                        if isinstance(n, int) and n == 0:
                            act.wait_ge(s_one, 2)
                        act.activation(p2[:, :, :, L], St[:, :, :], ACT.Copy, scale=decay[:, p, c:c + 1]
                                       ).then_inc(s_decayed, 1)
                        if c + 1 < WB:
                            add_x(p, n + 1, c + 1)

            def add_x(p, n, c):
                wait_used(act, s_step[1], STEP * (n - 2) + 2)
                act.activation(p1[:, c % 2, :, :, D], xv[:, p, :, c * L:(c + 1) * L], ACT.Copy
                               ).then_inc(s_addend, 1)
            repeat(act, NW // 2, body)


def delta_out(nc, g, scr, q_scale, q, k, a):
    with ExitStack() as ctx:
        m = Mem(nc, ctx, "out")
        u = m.sb("u", [P, N])
        same = m.sb("same", [P, H, D])
        rowsel = m.sb("rowsel", [P, D])
        spread = m.sb("spread", [P, D, P])
        gather = m.sb("gather", [P, D, H, D])
        bo = m.sb("bo", [P, P])
        kd = m.sb("kd", [P, 2, S])
        St = m.sb("St", [P, 2, S])
        qS = m.sb("qS", [P, 2, S])
        oT = m.sb("oT", [P, S])
        ps_k = [m.ps(f"ps_k{p}", [P, S]) for p in range(2)]
        ps_o = m.ps("ps_o", [P, S])
        ps_y = [m.ps(f"ps_y{i}", [P, CT, P]) for i in range(2)]
        s_in = m.sems("loaded", 4)
        s_same = m.sem("same")
        s_sel = m.sem("selectors")
        s_bo = m.sem("bo")
        s_bias = m.sem("bias_added")
        s_k = m.sem("k_spread")
        s_kd = m.sem("kd")
        s_S = m.sem("S")
        s_qS = m.sem("qS")
        s_o = m.sem("o")
        s_oT = m.sem("oT")
        s_y = m.sem("y")
        s_add = m.sem("added")
        block = m.block()

        @block.sync
        def _(sp):
            for b in range(B):
                tok = slice(b * S, (b + 1) * S)
                sp.dma_start(u[:, tok], scr.u[:, tok]).then_inc(s_in[b], 16)

        @block.gpsimd
        def _(pool):
            pool.memset(same[:, :, :], 1.0).then_inc(s_same, 1)
            pool.wait_ge(s_same, 1)
            pool.affine_select(out=same[:, :, :], in_=same[:, :, :], compare_op=ALU.is_ge, fill=0.0, base=0,
                               pattern=[[-D, H], [0, D]], channel_multiplier=1).then_inc(s_same, 1)
            pool.wait_ge(s_same, 2)
            pool.affine_select(out=same[:, :, :], in_=same[:, :, :], compare_op=ALU.is_ge, fill=0.0, base=D - 1,
                               pattern=[[D, H], [0, D]], channel_multiplier=-1).then_inc(s_same, 1)
            pool.wait_ge(s_same, 3)
            pool.memset(gather[:, :, :, :], 0.0).then_inc(s_same, 1)

        @block.tensor
        def _(pe):
            pe.matmul(ps_y[0][:, 0, :], g.ones[0:1, :], g.bo_row[:, :], start=True, stop=True).then_inc(s_bo, 1)
            pe.wait_ge(s_sel, 2 * D + 1)
            pe.wait_ge(s_bias, 1)

            def spread_k(b, e):
                n = D * b + e
                wait_used(pe, s_kd, n - 1)
                for i in range(2):
                    mm = pe.matmul(ps_k[e % 2][:, i * CH:(i + 1) * CH], spread[:, e, :],
                                   k[:, bass.ds(b * S + i * CH, CH)], start=True, stop=True)
                mm.then_inc(s_k, 1)

            def sum_o(b, e):
                n = D * b + e
                pe.wait_ge(s_qS, n + 1)
                if e == 0:
                    wait_used(pe, s_oT, b)
                for i in range(2):
                    mm = pe.matmul(ps_o[:, i * CH:(i + 1) * CH], gather[:, e, :, :].rearrange("p h d -> p (h d)"),
                                   qS[:, e % 2, i * CH:(i + 1) * CH], start=(e == 0), stop=(e == D - 1))
                mm.then_inc(s_o, 1)

            def project(b):
                pe.wait_ge(s_oT, b + 1)
                wait_used(pe, s_add, b)
                for t in range(TB):
                    mm = pe.matmul(ps_y[t // CT][:, t % CT, :], oT[:, t * P:(t + 1) * P], g.wT[:, 7, :],
                                   start=True, stop=True)
                mm.then_inc(s_y, 1)

            def body(b):
                before = not (isinstance(b, int) and b == 0)
                for e in range(D):
                    spread_k(b, e)
                    if e >= 2:
                        sum_o(b, e - 2)
                    elif before:
                        sum_o(b - 1, D - 2 + e)
                    if e == 2 and before:
                        project(b - 1)
            repeat(pe, B, body)
            sum_o(B - 1, D - 2)
            sum_o(B - 1, D - 1)
            project(B - 1)

        @block.vector
        def _(dve):
            dve.wait_ge(s_bo, 1)
            dve.tensor_copy(bo[:, :], ps_y[0][:, 0, :]).then_inc(s_bias, 1)
            dve.wait_ge(s_bias, 1)
            dve.tensor_tensor(g.x[:, :, :], g.x[:, :, :], bo[:, :].unsqueeze(1).to_broadcast([P, NT, P]), ALU.add)
            dve.wait_ge(s_same, 4)
            dve.tensor_reduce(rowsel[:, :], g.ident[:, :].rearrange("p (h e) -> p e h", h=H), AX.X,
                              ALU.add).then_inc(s_sel, 1)
            dve.wait_ge(s_sel, 1)
            for e in range(D):
                dve.tensor_scalar(spread[:, e, :], same[:, :, :].rearrange("p h d -> p (h d)"),
                                  rowsel[:, e:e + 1], None, ALU.mult).then_inc(s_sel, 1)
                dve.tensor_copy(gather[:, e, :, e], same[:, :, e]).then_inc(s_sel, 1)
            for b in range(B):
                dve.wait_ge(s_in[b], 16)

            def spread_u(b, e):
                n = D * b + e
                dve.wait_ge(s_k, n + 1)
                dve.tensor_tensor(kd[:, e % 2, :], u[:, bass.ds(b * S, S)], ps_k[e % 2][:, :],
                                  ALU.mult).then_inc(s_kd, 1)

            def add(b):
                dve.wait_ge(s_y, b + 1)
                for t in range(TB):
                    xt = g.x[:, bass.ds(b * TB + t, 1), :].rearrange("p o c -> p (o c)")
                    ins = dve.scalar_tensor_tensor(out=xt, in0=ps_y[t // CT][:, t % CT, :],
                                                   scalar=q_scale[:, bass.ds(b * TB + t, 1)], in1=xt,
                                                   op0=ALU.mult, op1=ALU.add)
                ins.then_inc(s_add, 1)
                dve.wait_ge(s_add, b + 1)
                for t in range(TB):
                    bn_stats_of(nc, g, b * TB + t)

            def body(b):
                tok = bass.ds(b * S, S)
                spread_u(b, 0)
                for e in range(D):
                    n = D * b + e
                    dve.wait_ge(s_kd, n + 1)
                    dve.tensor_tensor_scan(St[:, e % 2, :], a[:, tok], kd[:, e % 2, :], 0.0, ALU.mult,
                                           ALU.add).then_inc(s_S, 1)
                    if e < D - 1:
                        spread_u(b, e + 1)
                    dve.wait_ge(s_S, n + 1)
                    wait_used(dve, s_o, n - 1)
                    dve.tensor_tensor(qS[:, e % 2, :], q[:, tok], St[:, e % 2, :], ALU.mult).then_inc(s_qS, 1)
                    if e == 3 and not (isinstance(b, int) and b == 0):
                        add(b - 1)
            repeat(dve, B, body)
            add(B - 1)

        @block.scalar
        def _(act):
            def body(b):
                act.wait_ge(s_o, D * (b + 1))
                wait_used(act, s_y, b)
                for i in range(2):
                    ins = act.activation(oT[:, i * CH:(i + 1) * CH], ps_o[:, i * CH:(i + 1) * CH], ACT.Copy)
                ins.then_inc(s_oT, 1)
            repeat(act, B, body)


class Shared:
    pass


def store(nc, out, x, name):
    with nc.semaphore(name) as s_out, nc.Block() as block:
        @block.sync
        def _(sp):
            sp.dma_start(out.rearrange("b (t p) c -> p (b t) c", p=P), x[:, :, :]).then_inc(s_out, 16)
            sp.wait_ge(s_out, 16)


def build(nc, ins, out, stop=None):
    g, scr = Shared(), Shared()
    scr.terms = [nc.dram_tensor(f"terms_{w}", (NPART, K1, H, N), BF16, kind="Internal").ap() for w in "qk"]
    scr.qkv = [nc.dram_tensor(f"delta_{w}", (P, N), F32, kind="Internal").ap() for w in "qkv"]
    scr.ab = nc.dram_tensor("delta_ab", (2, H, N), F32, kind="Internal").ap()
    scr.k_scale = nc.dram_tensor("delta_k_scale", (N,), F32, kind="Internal").ap()
    scr.k = nc.dram_tensor("delta_k_normed", (P, N), F32, kind="Internal").ap()
    scr.u = nc.dram_tensor("delta_u", (P, N), F32, kind="Internal").ap()
    with ExitStack() as ctx:
        m = Mem(nc, ctx, "all")
        g.x = m.sb("x", [P, NT, P])
        g.ident = m.sb("ident", [P, P])
        g.ones = m.sb("ones", [P, P])
        g.varsel = m.sb("varsel", [P, 2, 48])
        g.wT = m.sb("wT", [P, 8, P])
        g.gatesT = m.sb("gatesT", [P, 48])
        g.bias_qkv = m.sb("bias_qkv", [P, 3])
        g.conv = m.sb("conv", [P, 3, K])
        g.bias_ab = m.sb("bias_ab", [48, 1])
        g.bo_row = m.sb("bo_row", [1, P])
        g.gate_w = m.sb("gate_w", [P, E])
        g.stats = m.sb("stats", [P, NT, 6])
        g.rstd = m.sb("rstd", [P, NT])
        g.nmr = m.sb("nmr", [P, NT])
        load_and_turn_weights(nc, g, ins)
        layer_norm_scales(nc, g, "ln_a")
        with ExitStack() as actx:
            ma = Mem(nc, actx, "a")
            g.o = ma.sb("o", [P, NT, P])
            with ExitStack() as vctx:
                mv = Mem(nc, vctx, "av")
                g.v1 = mv.sb("v1", [P, NT, H, VW])
                g.q_op = [mv.sb(f"q_op{s}", [P, GH, S], BF16) for s in range(NQ)]
                g.k_op = [mv.sb(f"k_op{s}", [P, GH, S], BF16) for s in range(NQ)]
                project_qkv(nc, g, scr)
                attend(nc, g, scr)
            if stop == "o":
                return store(nc, out, g.o, "dbg")
            project_out_a(nc, g)
        if stop == "x1":
            return store(nc, out, g.x, "dbg")
        moe_layer(nc, g, ins, "moe1", True)
        if stop == "x2":
            return store(nc, out, g.x, "dbg")
        with ExitStack() as bctx:
            mb = Mem(nc, bctx, "b")
            q_scale = mb.sb("q_scale", [P, NT])
            sumsq = mb.sb("sumsq", [P, 2, NT])
            with ExitStack() as xctx:
                xnT = Mem(nc, xctx, "bx").sb("xnT", [P, N])
                layer_norm_scales(nc, g, "ln_b")
                normalise_and_turn(nc, g, "turn_b", xnT)
                gates(nc, g, scr, xnT)
                project_conv(nc, g, scr, xnT, sumsq)
            l2_norms(nc, g, scr, sumsq, q_scale)
            q = mb.sb("q", [P, N])
            k = mb.sb("k", [P, N])
            a = mb.sb("a", [P, N])
            solve_and_scan(nc, g, scr, q, k, a)
            delta_out(nc, g, scr, q_scale, q, k, a)
        if stop == "x3":
            return store(nc, out, g.x, "dbg")
        moe_layer(nc, g, ins, "moe2", False)
        store(nc, out, g.x, "stored_out")


_INS = ["a_x", "a_Wq", "a_Wk", "a_Wv", "a_Wo", "b_Wq", "b_bq", "b_Wk", "b_bk", "b_Wv", "b_bv", "b_Wa", "b_ba",
        "b_Wb", "b_bb", "b_conv_q", "b_conv_k", "b_conv_v", "b_Wo", "b_bo", "f_gate_w", "f_w1", "f_w2", "f_w3"]
_LAYERS = {"a": "L0_attn_a_", "b": "L0_attn_b_", "f": "L0_ffn_"}


def kernel(**inputs):
    import numpy as np
    import concourse.bacc as bacc
    from concourse.bass_utils import run_bass_kernel_spmd

    nc = bacc.Bacc("TRN2", target_bir_lowering=False, num_devices=1)
    arrays, ins = {}, {}
    for name in _INS:
        a = np.ascontiguousarray(inputs[_LAYERS[name[0]] + name[2:]])
        arrays[f"in_{name}"] = a
        ins[name] = nc.dram_tensor(f"in_{name}", a.shape, mybir.dt.from_np(a.dtype), kind="ExternalInput").ap()
    out = nc.dram_tensor("out_x", (B, S, P), F32, kind="ExternalOutput").ap()
    build(nc, ins, out)
    r = run_bass_kernel_spmd(nc, [arrays], core_ids=[0])
    return r.results[0]["out_x"]
```

```python
from contextlib import ExitStack

import concourse.bass as bass
from concourse import mybir

F32 = mybir.dt.float32
BF16 = mybir.dt.bfloat16
ALU = mybir.AluOpType
ACT = mybir.ActivationFunctionType
AX = mybir.AxisListType

P = 128
H = 16
D = P // H
B = 4
S = 1024
N = B * S
NT = N // P
TB = S // P
CH = 512
NC_ = N // CH
CT = CH // P
LN_EPS = 1e-5
L2_EPS = 1e-6

NPART = 3
K1 = D + 1
R_ALL = NPART * NPART * K1
R_MAX = 96
R_END = R_MAX + NPART
GH = 4
NQ = H // GH
E, F = 8, 256
MF = F // P
VW = D + 1


class Count:

    def __init__(self, eng, sem, start=0):
        self.eng, self.sem, self.n = eng, sem, start

    def done(self, ins):
        ins.then_inc(self.sem, 1)
        self.n = self.n + 1
        self.eng.wait_ge(self.sem, self.n)


def wait_used(eng, sem, value):
    if not (isinstance(value, int) and value <= 0):
        eng.wait_ge(sem, value)


def repeat(eng, n, body):
    body(0)
    with eng.Fori(1, n) as i:
        body(i)


def chunk_pairs(eng, body):
    body(0, False)
    with eng.Fori(1, NC_ // 2 - 1) as i:
        body(i, False)
    body(NC_ // 2 - 1, True)


class Mem:

    def __init__(self, nc, ctx, phase):
        self.nc, self.ctx, self.phase, self.used = nc, ctx, phase, []

    def sb(self, name, shape, dt=F32):
        return self.ctx.enter_context(self.nc.sbuf_tensor(f"{self.phase}_{name}", shape, dt))

    def ps(self, name, shape, dt=F32):
        return self.ctx.enter_context(self.nc.psum_tensor(f"{self.phase}_{name}", shape, dt))

    def sem(self, name):
        s = self.ctx.enter_context(self.nc.semaphore(f"{self.phase}_{name}"))
        self.used.append(s)
        return s

    def sems(self, name, n):
        return [self.sem(f"{name}{i}") for i in range(n)]

    def block(self):
        self.ctx.callback(self.clear)
        return self.ctx.enter_context(self.nc.Block())

    def clear(self):
        numbers = sorted(s.num for s in self.used)
        with self.nc.Block() as block:
            @block.sync
            def _(sp):
                first = last = numbers[0]
                for n in numbers[1:] + [-1]:
                    if n == last + 1:
                        last = n
                        continue
                    sp.sem_clear(range(first, last + 1))
                    first = last = n


def load_and_turn_weights(nc, g, ins):
    with ExitStack() as ctx:
        m = Mem(nc, ctx, "w")
        names = ["a_Wq", "a_Wk", "a_Wv", "a_Wo", "b_Wq", "b_Wk", "b_Wv", "b_Wo"]
        raw = m.sb("raw", [P, len(names), P])
        gates = m.sb("gates", [48, P])
        headsum = m.sb("headsum", [P, 2, H])
        headmean = m.sb("headmean", [P, 2, H])
        turned_ps = [m.ps(f"turned{i}", [P, CH]) for i in range(2)]
        gates_ps = m.ps("gates_ps", [P, CH])
        s_w = m.sem("w_loaded")
        s_x = m.sems("x_loaded", B)
        s_small = m.sem("small_loaded")
        s_id0 = m.sem("ident_cleared")
        s_id = m.sem("ident_ready")
        s_sel = m.sem("selectors")
        s_turned = m.sem("turned")
        s_gates = m.sem("gates_cleared")
        s_chain = m.sem("chain")

        block = m.block()

        @block.sync
        def _(sp):
            for i, n in enumerate(names):
                sp.dma_start(raw[:, i, :], ins[n]).then_inc(s_w, 16)
            sp.wait_ge(s_gates, 2)
            sp.dma_start(gates[0:H, :], ins["b_Wa"]).then_inc(s_w, 16)
            sp.dma_start(gates[32:32 + H, :], ins["b_Wb"]).then_inc(s_w, 16)
            for i, n in enumerate(["b_bq", "b_bk", "b_bv"]):
                sp.dma_start(g.bias_qkv[:, i:i + 1], ins[n].rearrange("(c o) -> c o", o=1)).then_inc(s_small, 16)
            for i, n in enumerate(["b_conv_q", "b_conv_k", "b_conv_v"]):
                sp.dma_start(g.conv[:, i, :], ins[n].rearrange("c o k -> c (o k)")).then_inc(s_small, 16)
            sp.dma_start(g.bias_ab[0:H, :], ins["b_ba"].rearrange("(c o) -> c o", o=1)).then_inc(s_small, 16)
            sp.dma_start(g.bias_ab[32:32 + H, :], ins["b_bb"].rearrange("(c o) -> c o", o=1)).then_inc(s_small, 16)
            sp.dma_start(g.bo_row[:, :], ins["b_bo"].rearrange("(o c) -> o c", o=1)).then_inc(s_small, 16)
            sp.dma_start(g.gate_w[:, :], ins["f_gate_w"]).then_inc(s_small, 16)
            sp.wait_ge(s_small, 16 * 10)

        @block.scalar
        def _(act):
            xd = ins["a_x"].rearrange("b (t p) c -> p (b t) c", p=P)
            for i in range(B):
                act.dma_start(g.x[:, i * TB:(i + 1) * TB, :], xd[:, i * TB:(i + 1) * TB, :]).then_inc(s_x[i], 16)

        @block.gpsimd
        def _(pool):
            pool.memset(gates[:, :], 0.0).then_inc(s_gates, 1)
            pool.memset(g.bias_ab[:, :], 0.0).then_inc(s_gates, 1)
            pool.memset(g.ident[:, :], 0.0).then_inc(s_id0, 1)
            pool.memset(g.ones[:, :], 1.0).then_inc(s_id0, 1)
            pool.memset(g.varsel[:, :, :], 0.0).then_inc(s_id0, 1)
            pool.wait_ge(s_id0, 3)
            pool.affine_select(out=g.ident[:, :], in_=g.ident[:, :], compare_op=ALU.not_equal, fill=1.0,
                               base=0, pattern=[[-1, P]], channel_multiplier=1).then_inc(s_id, 1)
            for d in range(D):
                for i, w in enumerate([D / (D - 1), 1.0 / (D - 1)]):
                    v = g.varsel[:, i, 32 * i:32 * i + H]
                    pool.wait_ge(s_sel, 2 * d + i)
                    pool.affine_select(out=v, in_=v, compare_op=ALU.not_equal, fill=w, base=-H * d,
                                       pattern=[[-1, H]], channel_multiplier=1).then_inc(s_sel, 1)

        @block.tensor
        def _(pe):
            pe.wait_ge(s_id, 1)
            pe.wait_ge(s_w, 16 * 10)
            for i in range(8):
                mm = pe.transpose(turned_ps[i // 4][:, (i % 4) * P:(i % 4 + 1) * P], raw[:, i, :], g.ident[:, :])
            mm.then_inc(s_turned, 1)
            pe.transpose(gates_ps[:, 0:48], gates[:, :], g.ident[0:48, 0:48]).then_inc(s_turned, 1)

        @block.vector
        def _(dve):
            chain = Count(dve, s_chain)
            for b in range(B):
                dve.wait_ge(s_x[b], 16)
                for t in range(TB):
                    bn_stats_of(nc, g, b * TB + t)
            dve.wait_ge(s_turned, 2)
            dve.tensor_copy(g.wT[:, 2:4, :], turned_ps[0][:, 2 * P:4 * P])
            dve.tensor_copy(g.wT[:, 4:8, :], turned_ps[1][:, :])
            dve.tensor_copy(g.gatesT[:, :], gates_ps[:, 0:48])
            qk = turned_ps[0][:, 0:2 * P].rearrange("p (w h d) -> p w h d", w=2, h=H)
            chain.done(dve.tensor_reduce(headsum[:, :, :], qk, AX.X, ALU.add))
            chain.done(dve.tensor_scalar(headmean[:, :, :], headsum[:, :, :], 1.0 / D, None, ALU.mult))
            chain.done(dve.tensor_tensor(g.wT[:, 0:2, :].rearrange("p w (d h) -> p w h d", h=H), qk,
                                         headmean[:, :, :].unsqueeze(3).to_broadcast([P, 2, H, D]), ALU.subtract))
            dve.tensor_scalar(g.wT[:, 0, :], g.wT[:, 0, :], 1.0 / D, None, ALU.mult)


def bn_stats_of(nc, g, tile):
    if isinstance(tile, int):
        return nc.vector.bn_stats(g.stats[:, tile, :], g.x[:, tile, :])
    one = bass.ds(tile, 1)
    return nc.vector.bn_stats(g.stats[:, one, :].rearrange("p o s -> p (o s)"),
                              g.x[:, one, :].rearrange("p o c -> p (o c)"))


def layer_norm_scales(nc, g, phase):
    with ExitStack() as ctx:
        m = Mem(nc, ctx, phase)
        msum = m.sb("msum", [P, NT])
        mdiff = m.sb("mdiff", [P, NT])
        m2 = m.sb("m2", [P, NT])
        var = m.sb("var", [P, NT])
        std = m.sb("std", [P, NT])
        eps = m.sb("eps", [P, 1])
        s_eps = m.sem("eps")
        s_chain = m.sem("chain")
        s_var = m.sem("var")
        s_std = m.sem("std")
        s_rstd = m.sem("rstd")
        block = m.block()

        @block.vector
        def _(dve):
            dve.memset(eps[:, :], LN_EPS).then_inc(s_eps, 1)
            chain = Count(dve, s_chain)
            stats = g.stats
            dve.tensor_tensor(msum[:, :], stats[:, :, 1], stats[:, :, 4], ALU.add)
            chain.done(dve.tensor_tensor(mdiff[:, :], stats[:, :, 1], stats[:, :, 4], ALU.subtract))
            dve.tensor_tensor(m2[:, :], stats[:, :, 2], stats[:, :, 5], ALU.add)
            chain.done(dve.scalar_tensor_tensor(out=var[:, :], in0=mdiff[:, :], scalar=0.25 * P,
                                                in1=mdiff[:, :], op0=ALU.mult, op1=ALU.mult))
            dve.tensor_tensor(var[:, :], var[:, :], m2[:, :], ALU.add).then_inc(s_var, 1)
            dve.wait_ge(s_std, 1)
            dve.reciprocal(g.rstd[:, :], std[:, :]).then_inc(s_rstd, 1)
            dve.wait_ge(s_rstd, 1)
            dve.scalar_tensor_tensor(out=g.nmr[:, :], in0=msum[:, :], scalar=-0.5, in1=g.rstd[:, :],
                                     op0=ALU.mult, op1=ALU.mult)

        @block.scalar
        def _(act):
            act.wait_ge(s_eps, 1)
            act.wait_ge(s_var, 1)
            act.activation(std[:, :], var[:, :], ACT.Sqrt, bias=eps[:, :], scale=1.0 / P).then_inc(s_std, 1)


def project_qkv(nc, g, scr):
    with ExitStack() as ctx:
        m = Mem(nc, ctx, "qkv")
        xn = m.sb("xn", [P, 2, CT, P])
        xnT = m.sb("xnT", [P, 2, CH])
        parts = [m.sb(f"parts_{w}", [P, 2, NPART, CH], BF16) for w in "qk"]
        square = [m.sb(f"square_{w}", [P, 2, CH]) for w in "qk"]
        rest = [m.sb(f"rest_{w}", [P, 2, CH]) for w in "qk"]
        vparts = m.sb("vparts", [48, 2, NPART, CH], BF16)
        vrest = m.sb("vrest", [48, 2, CH])
        ps_x = m.ps("ps_x", [P, CH])
        ps_qk = [[m.ps(f"ps_{w}{p}", [P, CH]) for p in range(2)] for w in "qk"]
        ps_v = m.ps("ps_v", [P, CH])
        ps_var = m.ps("ps_var", [P, CH])

        s_xn = m.sems("xn", 2)
        s_turn = m.sems("turned", 2)
        s_xnT = m.sems("xnT", 2)
        s_proj = [m.sems(f"proj_{w}", 2) for w in "qk"]
        s_v = m.sems("v", 2)
        s_vout = m.sems("v_out", 2)
        s_sq = [m.sems(f"square_{w}", 2) for w in "qk"]
        s_p1 = [m.sems(f"part1_{w}", 2) for w in "qk"]
        s_r = [m.sems(f"rest_{w}", 2) for w in "qk"]
        s_p2 = [m.sems(f"part2_{w}", 2) for w in "qk"]
        s_p3 = [m.sems(f"part3_{w}", 2) for w in "qk"]
        s_var = m.sems("var", 2)
        s_v1 = m.sems("vpart1_", 2)
        s_vr = m.sems("vrest", 2)
        s_v2 = m.sems("vpart2_", 2)
        s_v3 = m.sems("vpart3_", 2)
        s_out = m.sems("stored", 2)
        s_ones = m.sem("ones")
        NDMA = 4
        block = m.block()


        @block.gpsimd
        def _(pool):
            pool.memset(g.v1[:, :, :, D:VW], 1.0).then_inc(s_ones, 1)
            n = 1
            for op in (*g.q_op, *g.k_op):
                pool.wait_ge(s_ones, n)
                pool.memset(op[64:P, :, :].bitcast(mybir.dt.uint32), 0).then_inc(s_ones, 1)
                n += 1
            for op in g.k_op:
                pool.wait_ge(s_ones, n)
                pool.memset(op[R_MAX:R_END, :, :], 1.0).then_inc(s_ones, 1)
                n += 1

        @block.scalar
        def _(act):
            def normalise(i, p):
                wait_used(act, s_turn[p], i)
                for t in range(CT):
                    tile = (2 * i + p) * CT + t
                    ins = act.activation(xn[:, p, t, :], g.x[:, bass.ds(tile, 1), :], ACT.Identity,
                                         bias=g.nmr[:, bass.ds(tile, 1)], scale=g.rstd[:, bass.ds(tile, 1)])
                ins.then_inc(s_xn[p], 1)

            normalise(0, 0)

            def body(i, last):
                for p in range(2):
                    if not (last and p == 1):
                        normalise(i + p, 1 - p)
                    wait_used(act, s_out[p], 16 * NDMA * i)
                    for w in range(2):
                        act.wait_ge(s_proj[w][p], i + 1)
                        wait_used(act, s_var[p], i)
                        act.activation(square[w][:, p, :], ps_qk[w][p][:, :], ACT.Square).then_inc(s_sq[w][p], 1)
                        act.activation(parts[w][:, p, 0, :], ps_qk[w][p][:, :], ACT.Copy).then_inc(s_p1[w][p], 1)
                    for w in range(2):
                        act.wait_ge(s_r[w][p], i + 1)
                        act.activation(parts[w][:, p, 1, :], rest[w][:, p, :], ACT.Copy).then_inc(s_p2[w][p], 1)
                    act.wait_ge(s_var[p], i + 1)
                    act.activation(vparts[:, p, 0, :], ps_var[0:48, :], ACT.Copy).then_inc(s_v1[p], 1)
                    act.wait_ge(s_vr[p], i + 1)
                    act.activation(vparts[:, p, 1, :], vrest[:, p, :], ACT.Copy).then_inc(s_v2[p], 1)
            chunk_pairs(act, body)

        @block.tensor
        def _(pe):
            def turn(i, p):
                pe.wait_ge(s_xn[p], i + 1)
                wait_used(pe, s_xnT[1 - p], i + p)
                for t in range(CT):
                    mm = pe.transpose(ps_x[:, t * P:(t + 1) * P], xn[:, p, t, :], g.ident[:, :])
                mm.then_inc(s_turn[p], 1)

            turn(0, 0)

            def body(i, last):
                for p in range(2):
                    pe.wait_ge(s_xnT[p], i + 1)
                    for w in range(2):
                        wait_used(pe, s_r[w][p], i)
                        pe.matmul(ps_qk[w][p][:, :], g.wT[:, w, :], xnT[:, p, :], start=True,
                                  stop=True).then_inc(s_proj[w][p], 1)
                    wait_used(pe, s_vout[1 - p], i + p)
                    for t in range(CT):
                        mm = pe.matmul(ps_v[:, t * P:(t + 1) * P], xnT[:, p, t * P:(t + 1) * P], g.wT[:, 2, :],
                                       start=True, stop=True)
                    mm.then_inc(s_v[p], 1)
                    if not (last and p == 1):
                        turn(i + p, 1 - p)
                    wait_used(pe, s_vr[1 - p], i + p)
                    for w in range(2):
                        pe.wait_ge(s_sq[w][p], i + 1)
                        mm = pe.matmul(ps_var[0:48, :], g.varsel[:, w, :], square[w][:, p, :],
                                       start=(w == 0), stop=(w == 1))
                    mm.then_inc(s_var[p], 1)
            chunk_pairs(pe, body)

        @block.vector
        def _(dve):
            def take_turned(i, p):
                dve.wait_ge(s_turn[p], i + 1)
                wait_used(dve, s_v[p], i)
                dve.tensor_copy(xnT[:, p, :], ps_x[:, :]).then_inc(s_xnT[p], 1)

            dve.wait_ge(s_ones, 1)
            take_turned(0, 0)

            def body(i, last):
                for p in range(2):
                    for w in range(2):
                        dve.wait_ge(s_p1[w][p], i + 1)
                        dve.tensor_tensor(rest[w][:, p, :], ps_qk[w][p][:, :], parts[w][:, p, 0, :],
                                          ALU.subtract).then_inc(s_r[w][p], 1)
                    if not (last and p == 1):
                        take_turned(i + p, 1 - p)
                    dve.wait_ge(s_v[p], i + 1)
                    for t in range(CT):
                        ins = dve.tensor_copy(g.v1[:, bass.ds((2 * i + p) * CT + t, 1), :, 0:D],
                                              ps_v[:, t * P:(t + 1) * P].rearrange("p (h d) -> p h d", h=H))
                    ins.then_inc(s_vout[p], 1)
                    for w in range(2):
                        dve.wait_ge(s_p2[w][p], i + 1)
                        dve.tensor_tensor(parts[w][:, p, 2, :], rest[w][:, p, :], parts[w][:, p, 1, :],
                                          ALU.subtract).then_inc(s_p3[w][p], 1)
                    dve.wait_ge(s_v1[p], i + 1)
                    dve.tensor_tensor(vrest[:, p, :], ps_var[0:48, :], vparts[:, p, 0, :],
                                      ALU.subtract).then_inc(s_vr[p], 1)
                    dve.wait_ge(s_v2[p], i + 1)
                    dve.tensor_tensor(vparts[:, p, 2, :], vrest[:, p, :], vparts[:, p, 1, :],
                                      ALU.subtract).then_inc(s_v3[p], 1)
            chunk_pairs(dve, body)

        @block.sync
        def _(sp):
            def body(i):
                for p in range(2):
                    at = (2 * i + p) * CH
                    for w in range(2):
                        sp.wait_ge(s_p3[w][p], i + 1)
                        sp.dma_start(scr.terms[w][:, 0:D, :, bass.ds(at, CH)].rearrange("i d h t -> (d h) i t"),
                                     parts[w][:, p, :, :]).then_inc(s_out[p], 16)
                    sp.wait_ge(s_v3[p], i + 1)
                    for w in range(2):
                        sp.dma_start(scr.terms[w][:, D, :, bass.ds(at, CH)].rearrange("i h t -> h i t"),
                                     vparts[32 * w:32 * w + H, p, :, :]).then_inc(s_out[p], 16)
            repeat(sp, NC_ // 2, body)
            for p in range(2):
                sp.wait_ge(s_out[p], 16 * NDMA * (NC_ // 2))


LEAD = 8
PV_LAG = 3
COPY_AT = 2 * PV_LAG + 1
PROBS = 16
STEPS = GH * TB


def attend(nc, g, scr):
    with ExitStack() as ctx:
        m = Mem(nc, ctx, "att")
        q_op, k_op = g.q_op, g.k_op
        probs = m.sb("probs", [P, PROBS, CH])
        vq = m.sb("vq", [P, 2, TB, 64])
        negmax = m.sb("negmax", [P, 2, STEPS])
        nm_rows = m.sb("nm_rows", [STEPS, P])
        nm_rest = m.sb("nm_rest", [STEPS, P])
        nm_parts = m.sb("nm_parts", [STEPS, 2, NPART, P], BF16)
        acc_sb = m.sb("acc_sb", [P, 2, CH])
        rsum = m.sb("rsum", [P, 2, CT, GH])
        ps_max = m.ps("ps_max", [P, 2, S])
        ps_prob = m.ps("ps_prob", [P, 2, CH])
        ps_acc = m.ps("ps_acc", [P, CH])
        ps_misc = m.ps("ps_misc", [P, CH])
        comb = ps_misc[:, P:P + CT * GH * VW].rearrange("p (t g r) -> p t g r", t=CT, g=GH)

        s_clear = m.sem("cleared")
        s_load = m.sems("loaded", NQ)
        s_scored = m.sem("scored")
        s_maxed = m.sem("maxed")
        s_nmT = m.sem("negmax_turned")
        s_nmch = m.sem("negmax_chain")
        s_nmp = m.sem("negmax_parts")
        s_nmrow = m.sem("negmax_rows")
        s_prob = m.sem("prob_scored")
        s_exp = m.sem("exped")
        s_vq = m.sem("v_staged")
        s_pv = m.sem("pv")
        s_acc = m.sem("acc_copied")
        s_comb = m.sem("combined")
        s_rsum = m.sem("rsum")
        s_misc = m.sem("misc_read")
        last_b = B - 1

        def batches(eng, body):
            body(0, True, False)
            with eng.Fori(1, last_b) as b:
                body(b, False, False)
            body(last_b, False, True)

        def prev(b, s):
            return (b, s - 1) if s else (b - 1, NQ - 1)

        def nxt(b, s, k):
            return (b, s + k) if s + k < NQ else (b + 1, s + k - NQ)

        block = m.block()

        @block.gpsimd
        def _(pool):
            pool.memset(vq[:, :, :, :], 0.0).then_inc(s_clear, 1)
            pool.wait_ge(s_clear, 1)

            def body(b, first, last):
                for s in range(NQ):
                    if not (first and s == 0):
                        pool.wait_ge(s_vq, NQ * b + s)
                    if not (first and s < 2):
                        pool.wait_ge(s_pv, 4 * TB * (NQ * b + s - 1))
                    pool.tensor_copy(vq[:, s % 2, :, 0:GH * VW],
                                     g.v1[:, bass.ds(b * TB, TB), s * GH:(s + 1) * GH, :].rearrange(
                                         "p t g r -> p t (g r)")).then_inc(s_vq, 1)
            batches(pool, body)

        @block.sync
        def _(sp):
            def load(b, s):
                heads = slice(s * GH, (s + 1) * GH)
                tok = bass.ds(b * S, S)
                for i in range(NPART):
                    row = i * NPART * K1
                    sp.dma_start(k_op[s][row:row + NPART * K1, :, :],
                                 scr.terms[1][:, :, heads, tok].rearrange("j d h t -> (j d) h t")
                                 ).then_inc(s_load[s], 16)
                    for j in range(NPART):
                        sp.dma_start(q_op[s][row + j * K1:row + (j + 1) * K1, :, :],
                                     scr.terms[0][i, :, heads, tok]).then_inc(s_load[s], 16)

            def max_rows(u, s):
                sp.wait_ge(s_nmp, u + 1)
                for i in range(NPART):
                    sp.dma_start(q_op[s][R_MAX + i:R_MAX + i + 1, :, :].rearrange("o g t -> o (g t)"),
                                 nm_parts[:, s % 2, i, :]).then_inc(s_nmrow, 16)

            for s in range(NQ):
                load(0, s)
            max_rows(0, 0)

            def body(b, first, last):
                for s in range(NQ):
                    if not (last and s == NQ - 1):
                        max_rows(NQ * b + s + 1, (s + 1) % NQ)
                    if not last:
                        sp.wait_ge(s_prob, 2 * STEPS * (NQ * b + s + 1))
                        load(b + 1, s)
            batches(sp, body)

        LOADS = 16 * (NPART + NPART * NPART)

        @block.tensor
        def _(pe):
            def scores_for_max(b, s, a, k):
                u = NQ * b + s
                if k == 0:
                    if a == 0:
                        pe.wait_ge(s_load[s], LOADS * (b + 1))
                    if not (isinstance(b, int) and b == 0 and s == 0 and a < 2):
                        pe.wait_ge(s_maxed, STEPS * u + a - 1)
                h, qt = a // TB, a % TB
                mm = pe.matmul(ps_max[:, a % 2, k * CH:(k + 1) * CH], q_op[s][0:R_ALL, h, qt * P:(qt + 1) * P],
                               k_op[s][0:R_ALL, h, k * CH:(k + 1) * CH], start=True, stop=True)
                if k == 1:
                    mm.then_inc(s_scored, 1)

            def scores_for_prob(b, s, j):
                u = NQ * b + s
                half, kt, h = j // STEPS, j % STEPS // GH, j % GH
                if j == 0:
                    pe.wait_ge(s_nmrow, 16 * NPART * (u + 1))
                if not (isinstance(b, int) and b == 0 and s == 0 and j < 2):
                    pe.wait_ge(s_exp, 2 * STEPS * u + j - 1)
                pe.matmul(ps_prob[:, j % 2, :], k_op[s][0:R_END, h, kt * P:(kt + 1) * P],
                          q_op[s][0:R_END, h, half * CH:(half + 1) * CH], start=True,
                          stop=True).then_inc(s_prob, 1)

            def pv(b, s, v, part):
                u = NQ * b + s
                half, kt = v // TB, v % TB
                cols = slice(part * CH // 2, (part + 1) * CH // 2)
                if part == 0:
                    pe.wait_ge(s_exp, 2 * STEPS * u + GH * (v + 1))
                    if v == 0:
                        pe.wait_ge(s_vq, u + 1)
                    if kt == 0 and not (isinstance(b, int) and b == 0 and s == 0 and half == 0):
                        pe.wait_ge(s_acc, 2 * u + half)
                for h in range(GH):
                    mm = pe.matmul(ps_acc[32 * h:32 * h + 32, cols], vq[:, s % 2, kt, VW * h:VW * h + 32],
                                   probs[:, (GH * v + h) % PROBS, cols], start=(kt == 0 and part == 0),
                                   stop=(kt == TB - 1 and part == 1))
                mm.then_inc(s_pv, 1)

            def combine(b, s, half, last=False):
                u = NQ * b + s
                pe.wait_ge(s_acc, 2 * u + half + 1)
                pe.wait_ge(s_misc, 3 * u + 1 + 2 * half - last)
                for t in range(CT):
                    mm = pe.matmul(comb[:, t], acc_sb[:, half, t * P:(t + 1) * P],
                                   g.ident[:, :].rearrange("p (g r) -> p g r", g=GH)[:, :, 0:VW],
                                   start=True, stop=True)
                mm.then_inc(s_comb, 1)

            def turn_max(b, s):
                u = NQ * b + s
                pe.wait_ge(s_maxed, STEPS * (u + 1))
                if not (isinstance(b, int) and b == 0 and s == 0):
                    pe.wait_ge(s_misc, 3 * u - 1)
                pe.transpose(ps_misc[0:STEPS, 0:P], negmax[:, s % 2, :], g.ident[:, :]).then_inc(s_nmT, 1)

            for a in range(STEPS):
                for k in range(2):
                    scores_for_max(0, 0, a, k)
            turn_max(0, 0)
            for a in range(LEAD):
                for k in range(2):
                    scores_for_max(0, 1, a, k)

            def body(b, first, last):
                for s in range(NQ):
                    for i in range(STEPS):
                        a = i + LEAD
                        k, a = (1, a) if a < STEPS else (2, a - STEPS)
                        for half in range(2):
                            if not (last and s + k >= NQ):
                                scores_for_max(*nxt(b, s, k), a, half)
                            scores_for_prob(b, s, 2 * i + half)
                        w = i - PV_LAG
                        for w in (w - 1, w) if w % (2 * TB) == 1 else () if w % (2 * TB) == 0 else (w,):
                            if w >= 0:
                                pv(b, s, w // 2, w % 2)
                            elif not (first and s == 0):
                                pv(*prev(b, s), (w + STEPS) // 2, w % 2)
                        if i == PV_LAG + 1 and not (first and s == 0):
                            combine(*prev(b, s), 1)
                        if i == STEPS // 2 + PV_LAG + 1:
                            combine(b, s, 0)
                        if i == STEPS - LEAD + 1 and not (last and s == NQ - 1):
                            turn_max(*nxt(b, s, 1))
            batches(pe, body)
            for w in range(STEPS - PV_LAG, STEPS):
                pv(last_b, NQ - 1, w // 2, w % 2)
            combine(last_b, NQ - 1, 1, last=True)

        @block.scalar
        def _(act):
            def copy_acc(b, s, half, part):
                u = NQ * b + s
                if part == 0:
                    act.wait_ge(s_pv, 4 * TB * u + 2 * TB * (half + 1))
                    if not (isinstance(b, int) and b == 0 and s == 0):
                        act.wait_ge(s_comb, 2 * u + half - 1)
                cols = slice(part * CH // 2, (part + 1) * CH // 2)
                ins = act.activation(acc_sb[:, half, cols], ps_acc[:, cols], ACT.Copy)
                if part == 1:
                    ins.then_inc(s_acc, 1)

            def body(b, first, last):
                for s in range(NQ):
                    u = NQ * b + s
                    for j in range(2 * STEPS):
                        if COPY_AT <= j <= COPY_AT + 1 and not (first and s == 0):
                            copy_acc(*prev(b, s), 1, j - COPY_AT)
                        if STEPS + COPY_AT <= j <= STEPS + COPY_AT + 1:
                            copy_acc(b, s, 0, j - STEPS - COPY_AT)
                        act.wait_ge(s_prob, 2 * STEPS * u + j + 1)
                        if j % GH == 0 and not (first and s == 0 and j < PROBS):
                            act.wait_ge(s_pv, 4 * TB * u + 2 * ((j - PROBS) // GH + 1))
                        act.activation(probs[:, j % PROBS, :], ps_prob[:, j % 2, :], ACT.Exp).then_inc(s_exp, 1)
            batches(act, body)
            for part in range(2):
                copy_acc(last_b, NQ - 1, 1, part)

        @block.vector
        def _(dve):
            def reduce_max(b, s, a):
                u = NQ * b + s
                dve.wait_ge(s_scored, STEPS * u + a + 1)
                if a == 0 and not (isinstance(b, int) and b == 0 and s < 2):
                    dve.wait_ge(s_nmT, u - 1)
                dve.tensor_reduce(negmax[:, s % 2, a:a + 1], ps_max[:, a % 2, :], AX.X, ALU.max,
                                  negate=True).then_inc(s_maxed, 1)

            def split_max(b, s):
                u = NQ * b + s
                dve.wait_ge(s_nmT, u + 1)
                if not (isinstance(b, int) and b == 0 and s < 2):
                    dve.wait_ge(s_nmrow, 16 * NPART * (u - 1))
                chain = Count(dve, s_nmch, 4 * u)
                rows, rest, parts = nm_rows[:, :], nm_rest[:, :], nm_parts[:, s % 2]
                ins = dve.tensor_copy(rows, ps_misc[0:STEPS, 0:P])
                ins.then_inc(s_misc, 1)
                dve.wait_ge(s_misc, 1 if isinstance(u, int) and u == 0 else 3 * u)
                chain.done(dve.tensor_copy(parts[:, 0, :], rows))
                chain.done(dve.tensor_tensor(rest, rows, parts[:, 0, :], ALU.subtract))
                chain.done(dve.tensor_copy(parts[:, 1, :], rest))
                chain.done(dve.tensor_tensor(rows, rest, parts[:, 1, :], ALU.subtract))
                dve.tensor_copy(parts[:, 2, :], rows).then_inc(s_nmp, 1)

            def normalise(b, s, half):
                u = NQ * b + s
                dve.wait_ge(s_comb, 2 * u + half + 1)
                dve.reciprocal(rsum[:, half, :, :], comb[:, :, :, D]).then_inc(s_rsum, 1)
                dve.wait_ge(s_rsum, 2 * u + half + 1)
                for t in range(CT):
                    tile = b * TB + half * CT + t
                    out = g.o[:, bass.ds(tile, 1), s * GH * D:(s + 1) * GH * D].rearrange(
                        "p o (g d) -> p (o g) d", g=GH)
                    ins = dve.tensor_tensor(out, comb[:, t, :, 0:D],
                                            rsum[:, half, t, :].unsqueeze(2).to_broadcast([P, GH, D]), ALU.mult)
                ins.then_inc(s_misc, 1)

            for a in range(STEPS):
                reduce_max(0, 0, a)
            split_max(0, 0)
            for a in range(LEAD):
                reduce_max(0, 1, a)

            def body(b, first, last):
                for s in range(NQ):
                    for i in range(STEPS):
                        a = i + LEAD
                        k, a = (1, a) if a < STEPS else (2, a - STEPS)
                        if not (last and s + k >= NQ):
                            reduce_max(*nxt(b, s, k), a)
                        if i == PV_LAG + 3 and not (first and s == 0):
                            normalise(*prev(b, s), 1)
                        if i == STEPS // 2 + PV_LAG + 3:
                            normalise(b, s, 0)
                        if i == STEPS - LEAD + 2 and not (last and s == NQ - 1):
                            split_max(*nxt(b, s, 1))
            batches(dve, body)
            normalise(last_b, NQ - 1, 1)


def project_out_a(nc, g, ins):
    with ExitStack() as ctx:
        m = Mem(nc, ctx, "oproj")
        stage = m.sb("stage", [P, 2, CT, P])
        oT = m.sb("oT", [P, 2, CH])
        ps_t = [m.ps(f"ps_t{p}", [P, CH]) for p in range(2)]
        ps_y = [m.ps(f"ps_y{p}", [P, CH]) for p in range(2)]
        s_st = m.sems("staged", 2)
        s_turn = m.sems("turned", 2)
        s_oT = m.sems("oT", 2)
        s_y = m.sems("y", 2)
        s_add = m.sems("added", 2)
        block = m.block()

        @block.sync
        def _(sp):
            for e in range(E):
                sp.dma_start(g.w1[:, e, :], ins["f_w1"][e]).then_inc(g.s_experts, 16)
                sp.dma_start(g.w3[:, e, :], ins["f_w3"][e]).then_inc(g.s_experts, 16)
                sp.dma_start(g.w2[:, e, :, :], ins["f_w2"][e].rearrange("(m p) c -> p m c", p=P)
                             ).then_inc(g.s_experts, 16)

        @block.scalar
        def _(act):
            def body(i):
                for p in range(2):
                    wait_used(act, s_turn[p], i)
                    act.activation(stage[:, p, :, :], g.o[:, bass.ds((2 * i + p) * CT, CT), :],
                                   ACT.Copy).then_inc(s_st[p], 1)
            repeat(act, NC_ // 2, body)

        @block.tensor
        def _(pe):
            def turn(i, p):
                pe.wait_ge(s_st[p], i + 1)
                wait_used(pe, s_oT[p], i)
                for t in range(CT):
                    mm = pe.transpose(ps_t[p][:, t * P:(t + 1) * P], stage[:, p, t, :], g.ident[:, :])
                mm.then_inc(s_turn[p], 1)

            turn(0, 0)

            def body(i, last):
                for p in range(2):
                    if not (last and p == 1):
                        turn(i + p, 1 - p)
                    pe.wait_ge(s_oT[p], i + 1)
                    wait_used(pe, s_add[p], i)
                    for t in range(CT):
                        mm = pe.matmul(ps_y[p][:, t * P:(t + 1) * P], oT[:, p, t * P:(t + 1) * P],
                                       g.wT[:, 3, :], start=True, stop=True)
                    mm.then_inc(s_y[p], 1)
            chunk_pairs(pe, body)

        @block.vector
        def _(dve):
            def take_turned(i, p):
                dve.wait_ge(s_turn[p], i + 1)
                wait_used(dve, s_y[p], i)
                dve.tensor_copy(oT[:, p, :], ps_t[p][:, :]).then_inc(s_oT[p], 1)

            take_turned(0, 0)

            def body(i, last):
                for p in range(2):
                    if not (last and p == 1):
                        take_turned(i + p, 1 - p)
                    dve.wait_ge(s_y[p], i + 1)
                    xc = g.x[:, bass.ds((2 * i + p) * CT, CT), :]
                    dve.tensor_tensor(xc, xc, ps_y[p][:, :].rearrange("p (t c) -> p t c", t=CT),
                                      ALU.add).then_inc(s_add[p], 1)
                    dve.wait_ge(s_add[p], i + 1)
                    for t in range(CT):
                        bn_stats_of(nc, g, (2 * i + p) * CT + t)
            chunk_pairs(dve, body)


def moe(nc, g, ins, phase, norm_next):
    with ExitStack() as ctx:
        m = Mem(nc, ctx, phase)
        w1, w3, w2 = g.w1, g.w3, g.w2
        gate = m.sb("gate", [P, MF, CH])
        hT = m.sb("hT", [P, 2, MF, CH])
        ps_1 = [m.ps(f"ps_1{i}", [P, CH]) for i in range(MF)]
        ps_3 = [m.ps(f"ps_3{i}", [P, CH]) for i in range(MF)]
        ps_y = [m.ps(f"ps_y{i}", [P, CT, P]) for i in range(2)]
        xn = m.sb("xn", [P, CT, P])
        xnc = m.sb("xnc", [P, CH])
        xnT = m.sb("xnT", [P, N])
        logits = m.sb("logits", [P, CT, E])
        route = m.sb("route", [P, NT, E])
        rank = m.sb("rank", [P, E])
        best = m.sb("best", [P, 2, CT])
        at = m.sb("at", [P, CT, E])
        index = m.sb("index", [P, 2, CT])
        hot = [m.sb(f"hot{i}", [P, CT, E]) for i in range(2)]
        left = m.sb("left", [P, CT, E])
        gap = m.sb("gap", [P, 2, CT])
        weight = m.sb("weight", [P, 2, CT])
        ps_t = m.ps("ps_t", [P, CH])
        ps_l = m.ps("ps_l", [P, CT, E])
        s_xn = m.sem("xn")
        s_turn = m.sem("turned")
        s_xnc = m.sem("xnc")
        s_copy = m.sem("xnT")
        s_log = m.sem("logits")
        s_lout = m.sem("logits_out")
        s_rank = m.sem("rank")
        s_chain = m.sem("route_chain")
        s_gap = m.sem("gap")
        s_weight = m.sem("weight")
        wide = lambda a: a.unsqueeze(2).to_broadcast([P, CT, E])
        ROUTE = 14
        s_1 = m.sem("h1")
        s_3 = m.sem("h3")
        s_silu = m.sem("silu")
        s_h = m.sem("h")
        s_y = m.sem("y")
        s_add = m.sem("added")
        block = m.block()

        def chunks(eng, body):
            body(0, False)
            with eng.Fori(1, NC_ - 1) as c:
                body(c, False)
            body(NC_ - 1, True)

        @block.gpsimd
        def _(pool):
            pool.iota(rank[:, :], pattern=[[-1, E]], base=E, channel_multiplier=0,
                      allow_small_or_imprecise_dtypes=True).then_inc(s_rank, 1)

        @block.tensor
        def _(pe):
            def turn(c):
                pe.wait_ge(s_xn, c + 1)
                wait_used(pe, s_xnc, c)
                for t in range(CT):
                    mm = pe.transpose(ps_t[:, t * P:(t + 1) * P], xn[:, t, :], g.ident[:, :])
                mm.then_inc(s_turn, 1)

            def router(c):
                pe.wait_ge(s_xnc, c + 1)
                wait_used(pe, s_lout, c)
                for t in range(CT):
                    mm = pe.matmul(ps_l[:, t, :], xnc[:, t * P:(t + 1) * P], g.gate_w[:, :], start=True, stop=True)
                mm.then_inc(s_log, 1)

            def hidden(c, e):
                k = c * E + e
                if e == 0:
                    pe.wait_ge(s_copy, c + 1)
                for i in range(MF):
                    for w, ps, s, read in ((w1, ps_1, s_1, s_silu), (w3, ps_3, s_3, s_h)):
                        wait_used(pe, read, MF * (k - 1) + i + 1)
                        pe.matmul(ps[i][:, :], w[:, e, i * P:(i + 1) * P], xnT[:, bass.ds(c * CH, CH)],
                                  start=True, stop=True).then_inc(s, 1)

            def down(c, e):
                k = c * E + e
                wait_used(pe, s_add, k - 1)
                pe.wait_ge(s_h, MF * (k + 1))
                for t in range(CT):
                    for i in range(MF):
                        mm = pe.matmul(ps_y[e % 2][:, t, :], hT[:, e % 2, i, t * P:(t + 1) * P],
                                       w2[:, e, i, :], start=(i == 0), stop=(i == MF - 1))
                mm.then_inc(s_y, 1)

            turn(0)
            router(0)
            pe.wait_ge(g.s_experts, 16 * 3 * E)

            def body(c, last):
                for e in range(E):
                    hidden(c, e)
                    if e:
                        down(c, e - 1)
                    elif not (isinstance(c, int) and c == 0):
                        down(c - 1, E - 1)
                    if e == 1 and not last:
                        turn(c + 1)
                    if e == 3 and not last:
                        router(c + 1)
            chunks(pe, body)
            down(NC_ - 1, E - 1)

        @block.scalar
        def _(act):
            def normalise(c):
                wait_used(act, s_turn, c)
                for t in range(CT):
                    tile = c * CT + t
                    ins = act.activation(xn[:, t, :], g.x[:, bass.ds(tile, 1), :], ACT.Identity,
                                         bias=g.nmr[:, bass.ds(tile, 1)], scale=g.rstd[:, bass.ds(tile, 1)])
                ins.then_inc(s_xn, 1)

            def copy(c):
                act.wait_ge(s_xnc, c + 1)
                act.activation(xnT[:, bass.ds(c * CH, CH)], xnc[:, :], ACT.Copy).then_inc(s_copy, 1)

            def weigh(c):
                act.wait_ge(s_gap, 2 * (c + 1))
                act.activation(weight[:, :, :], gap[:, :, :], ACT.Sigmoid).then_inc(s_weight, 1)

            normalise(0)
            copy(0)
            weigh(0)

            def body(c, last):
                for e in range(E):
                    for i in range(MF):
                        n = MF * (c * E + e) + i
                        act.wait_ge(s_1, n + 1)
                        wait_used(act, s_h, n - MF + 1)
                        act.activation(gate[:, i, :], ps_1[i][:, :], ACT.Silu).then_inc(s_silu, 1)
                    if e == 0 and not last:
                        normalise(c + 1)
                    if e == 3 and not last:
                        copy(c + 1)
                    if e == 5 and not last:
                        weigh(c + 1)
            chunks(act, body)

        @block.vector
        def _(dve):
            ranks = rank[:, :].unsqueeze(1).to_broadcast([P, CT, E])

            def take_turned(c):
                dve.wait_ge(s_turn, c + 1)
                wait_used(dve, s_copy, c)
                wait_used(dve, s_log, c)
                dve.tensor_copy(xnc[:, :], ps_t[:, :]).then_inc(s_xnc, 1)

            def find_best(c, i):
                src = (logits, left)[i]
                chain = Count(dve, s_chain, ROUTE * c + 6 * i)
                if i == 0:
                    dve.wait_ge(s_log, c + 1)
                    dve.tensor_copy(logits[:, :, :], ps_l[:, :, :]).then_inc(s_lout, 1)
                    dve.wait_ge(s_lout, c + 1)
                chain.done(dve.tensor_reduce(best[:, i, :], src[:, :, :], AX.X, ALU.max))
                chain.done(dve.tensor_tensor(at[:, :, :], src[:, :, :], wide(best[:, i, :]), ALU.is_equal))
                chain.done(dve.tensor_tensor(at[:, :, :], at[:, :, :], ranks, ALU.mult))
                chain.done(dve.tensor_reduce(index[:, i, :], at[:, :, :], AX.X, ALU.max))
                chain.done(dve.tensor_tensor(hot[i][:, :, :], wide(index[:, i, :]), ranks, ALU.is_equal))
                if i == 0:
                    chain.done(dve.scalar_tensor_tensor(out=left[:, :, :], in0=hot[0][:, :, :], scalar=-3e38,
                                                        in1=logits[:, :, :], op0=ALU.mult, op1=ALU.add))
                else:
                    dve.tensor_tensor(gap[:, 0, :], best[:, 0, :], best[:, 1, :], ALU.subtract).then_inc(s_gap, 1)
                    dve.tensor_tensor(gap[:, 1, :], best[:, 1, :], best[:, 0, :], ALU.subtract).then_inc(s_gap, 1)

            def write_route(c):
                chain = Count(dve, s_chain, ROUTE * c + 11)
                dve.wait_ge(s_weight, c + 1)
                for i in range(2):
                    chain.done(dve.tensor_tensor(hot[i][:, :, :], hot[i][:, :, :], wide(weight[:, i, :]), ALU.mult))
                chain.done(dve.tensor_tensor(route[:, bass.ds(c * CT, CT), :], hot[0][:, :, :], hot[1][:, :, :],
                                             ALU.add))

            def product(c, e):
                k = c * E + e
                wait_used(dve, s_y, k - 1)
                for i in range(MF):
                    n = MF * k + i
                    dve.wait_ge(s_silu, n + 1)
                    dve.wait_ge(s_3, n + 1)
                    dve.tensor_tensor(hT[:, e % 2, i, :], gate[:, i, :], ps_3[i][:, :], ALU.mult).then_inc(s_h, 1)

            def add(c, e):
                k = c * E + e
                dve.wait_ge(s_y, k + 1)
                wait_used(dve, s_add, k)
                for t in range(CT):
                    xt = g.x[:, bass.ds(c * CT + t, 1), :].rearrange("p o c -> p (o c)")
                    ins = dve.scalar_tensor_tensor(
                        out=xt, in0=ps_y[e % 2][:, t, :],
                        scalar=route[:, bass.ds(c * CT + t, 1), e:e + 1].rearrange("p o c -> p (o c)"),
                        in1=xt, op0=ALU.mult, op1=ALU.add)
                ins.then_inc(s_add, 1)

            def stats_of_chunk(c):
                dve.wait_ge(s_add, E * (c + 1))
                for t in range(CT):
                    bn_stats_of(nc, g, c * CT + t)

            take_turned(0)
            dve.wait_ge(s_rank, 1)
            find_best(0, 0)
            find_best(0, 1)
            write_route(0)

            def body(c, last):
                for e in range(E):
                    product(c, e)
                    if e:
                        add(c, e - 1)
                    elif not (isinstance(c, int) and c == 0):
                        add(c - 1, E - 1)
                        if norm_next:
                            stats_of_chunk(c - 1)
                    if last:
                        continue
                    if e == 2:
                        take_turned(c + 1)
                    if e in (4, 5):
                        find_best(c + 1, e - 4)
                    if e == 6:
                        write_route(c + 1)
            chunks(dve, body)
            add(NC_ - 1, E - 1)
            if norm_next:
                stats_of_chunk(NC_ - 1)


def moe_layer(nc, g, ins, phase, norm_next):
    layer_norm_scales(nc, g, phase + "_ln")
    moe(nc, g, ins, phase + "_moe", norm_next)


K = 4
LEFT = K // 2


def project_conv(nc, g, scr, sumsq):
    with ExitStack() as ctx:
        m = Mem(nc, ctx, "conv")
        HB = S // CH
        UNITS = 3 * HB
        xn = m.sb("xn", [P, HB, CT, P])
        xnT = m.sb("xnT", [P, HB, CH])
        ab = m.sb("ab", [48, HB, CH])
        u = m.sb("u", [P, 3, LEFT + S + K - 1 - LEFT])
        y = m.sb("y", [P, 3, S])
        z = m.sb("z", [P, 3, S])
        sq = m.sb("sq", [P, 2, S])
        ps_x = [m.ps(f"ps_x{i}", [P, CH]) for i in range(HB)]
        ps = [m.ps(f"ps{i}", [P, CH]) for i in range(3)]
        ps_g = [m.ps(f"ps_g{i}", [48, CH]) for i in range(HB)]
        ps_s = m.ps("ps_s", [P, 2, TB])
        s_pad = m.sem("padded")
        s_xn = m.sems("xn", HB)
        s_turn = m.sems("turned", HB)
        s_xnT = m.sem("xnT")
        s_mm = m.sem("projected")
        s_got = m.sem("u")
        s_gmm = m.sem("gates")
        s_ab = m.sem("ab")
        s_about = m.sem("ab_stored")
        s_tap = m.sem("tap")
        s_y = m.sems("y", 3)
        s_z = m.sems("z", 3)
        s_sq = m.sems("squared", 2)
        s_sum = m.sem("summed")
        s_ss = m.sem("sums_out")
        s_out = m.sems("stored", 3)
        block = m.block()

        def batches(eng, body):
            body(0, False)
            with eng.Fori(1, B - 1) as b:
                body(b, False)
            body(B - 1, True)

        @block.gpsimd
        def _(pool):
            pool.memset(u[:, :, 0:LEFT], 0.0).then_inc(s_pad, 1)
            pool.wait_ge(s_pad, 1)
            pool.memset(u[:, :, LEFT + S:], 0.0).then_inc(s_pad, 1)

        @block.tensor
        def _(pe):
            def turn(b):
                for i in range(HB):
                    pe.wait_ge(s_xn[i], b + 1)
                    wait_used(pe, s_xnT, HB * (b - 1) + i + 1)
                    for t in range(CT):
                        mm = pe.transpose(ps_x[i][:, t * P:(t + 1) * P], xn[:, i, t, :], g.ident[:, :])
                    mm.then_inc(s_turn[i], 1)

            def project(b):
                pe.wait_ge(s_xnT, HB * (b + 1))
                for j in range(UNITS):
                    wait_used(pe, s_got, UNITS * b + j - 2)
                    pe.matmul(ps[j % 3][:, :], g.wT[:, 4 + j // HB, :], xnT[:, j % HB, :],
                              start=True, stop=True).then_inc(s_mm, 1)

            def gates(b):
                for i in range(HB):
                    wait_used(pe, s_ab, HB * (b - 1) + i + 1)
                    pe.matmul(ps_g[i][:, :], g.gatesT[:, :], xnT[:, i, :], start=True, stop=True
                              ).then_inc(s_gmm, 1)

            def sums(b):
                wait_used(pe, s_ss, b)
                for w in range(2):
                    pe.wait_ge(s_sq[w], b + 1)
                    for t in range(TB):
                        mm = pe.matmul(ps_s[:, w, t:t + 1], sq[:, w, t * P:(t + 1) * P], g.ones[:, 0:1],
                                       start=True, stop=True)
                mm.then_inc(s_sum, 1)

            turn(0)
            project(0)

            def body(b, last):
                gates(b)
                if not last:
                    turn(b + 1)
                    project(b + 1)
                sums(b)
            batches(pe, body)

        @block.scalar
        def _(act):
            def normalise(b):
                for i in range(HB):
                    wait_used(act, s_turn[i], b)
                    for t in range(CT):
                        tile = b * TB + i * CT + t
                        ins = act.activation(xn[:, i, t, :], g.x[:, bass.ds(tile, 1), :], ACT.Identity,
                                             bias=g.nmr[:, bass.ds(tile, 1)], scale=g.rstd[:, bass.ds(tile, 1)])
                    ins.then_inc(s_xn[i], 1)

            def first_silu(b, w):
                wait_used(act, s_y[w], b)
                for i in range(HB):
                    j = HB * w + i
                    act.wait_ge(s_mm, UNITS * b + j + 1)
                    act.activation(u[:, w, LEFT + i * CH:LEFT + (i + 1) * CH], ps[j % 3][:, :],
                                   ACT.Silu, bias=g.bias_qkv[:, w:w + 1]).then_inc(s_got, 1)

            def gates(b):
                wait_used(act, s_about, 32 * b)
                for i in range(HB):
                    act.wait_ge(s_gmm, HB * b + i + 1)
                    act.activation(ab[:, i, :], ps_g[i][:, :], ACT.Identity, bias=g.bias_ab[:, :]).then_inc(s_ab, 1)

            def second_silu(b, w):
                act.wait_ge(s_y[w], b + 1)
                wait_used(act, s_out[w], 16 * b)
                act.activation(z[:, w, :], y[:, w, :], ACT.Silu).then_inc(s_z[w], 1)
                if w < 2:
                    act.wait_ge(s_z[w], b + 1)
                    wait_used(act, s_sum, b)
                    act.activation(sq[:, w, :], z[:, w, :], ACT.Square).then_inc(s_sq[w], 1)

            normalise(0)
            act.wait_ge(s_pad, 2)
            for w in range(3):
                first_silu(0, w)

            def body(b, last):
                if not last:
                    normalise(b + 1)
                gates(b)
                second_silu(b, 0)
                second_silu(b, 1)
                if not last:
                    first_silu(b + 1, 0)
                second_silu(b, 2)
                if not last:
                    first_silu(b + 1, 1)
                    first_silu(b + 1, 2)
            batches(act, body)

        @block.vector
        def _(dve):
            def take_turned(b):
                for i in range(HB):
                    dve.wait_ge(s_turn[i], b + 1)
                    wait_used(dve, s_gmm, HB * b)
                    dve.tensor_copy(xnT[:, i, :], ps_x[i][:, :]).then_inc(s_xnT, 1)

            def convolve(b, w):
                dve.wait_ge(s_got, UNITS * b + HB * (w + 1))
                wait_used(dve, s_z[w], b)
                taps = Count(dve, s_tap, (K - 1) * (3 * b + w))
                taps.done(dve.tensor_scalar(y[:, w, :], u[:, w, 0:S], g.conv[:, w, 0:1], None, ALU.mult))
                for j in range(1, K):
                    ins = dve.scalar_tensor_tensor(out=y[:, w, :], in0=u[:, w, j:j + S],
                                                   scalar=g.conv[:, w, j:j + 1], in1=y[:, w, :],
                                                   op0=ALU.mult, op1=ALU.add)
                    if j < K - 1:
                        taps.done(ins)
                ins.then_inc(s_y[w], 1)

            def take_sums(b):
                dve.wait_ge(s_sum, b + 1)
                dve.tensor_copy(sumsq[:, :, bass.ds(b * TB, TB)], ps_s[:, :, :]).then_inc(s_ss, 1)

            take_turned(0)

            def body(b, last):
                convolve(b, 0)
                convolve(b, 1)
                if not last:
                    take_turned(b + 1)
                if not (isinstance(b, int) and b == 0):
                    take_sums(b - 1)
                convolve(b, 2)
            batches(dve, body)
            take_sums(B - 1)

        @block.sync
        def _(sp):
            def store_gates(b):
                sp.wait_ge(s_ab, HB * (b + 1))
                for i in range(2):
                    sp.dma_start(scr.ab[i][:, bass.ds(b * S, S)],
                                 ab[32 * i:32 * i + H, :, :].rearrange("h i t -> h (i t)")).then_inc(s_about, 16)

            def body(b, last):
                store_gates(b)
                for w in range(3):
                    sp.wait_ge(s_z[w], b + 1)
                    sp.dma_start(scr.qkv[w][:, bass.ds(b * S, S)], z[:, w, :]).then_inc(s_out[w], 16)
            batches(sp, body)
            for w in range(3):
                sp.wait_ge(s_out[w], 16 * B)
            sp.wait_ge(s_about, 32 * B)


L = 8
TH = S // 2
LB = TH // L
R = D // 2
W = P
WB = W // L
NW = S // W


def solve_and_scan(nc, g, scr, sumsq, q_scale, q, k_chan, a_chan):
    with ExitStack() as ctx:
        m = Mem(nc, ctx, "solve")
        k = m.sb("k", [P, D, TH])
        X = m.sb("X", [P, 2 * D, TH])
        ab = m.sb("ab", [P, 2, TH])
        k_scale = m.sb("k_scale", [P, TH])
        dec = m.sb("dec", [P, L, LB, L])
        M_and_windows = m.sb("M_and_windows", [P, L * LB * L])
        M = M_and_windows[:, :].rearrange("p (t c i) -> p t c i", t=L, c=LB)
        windows = M_and_windows[:, :].rearrange("p (x p2 e t) -> p x p2 e t", x=2, p2=2, e=D)
        xw, kd = windows[:, 0], windows[:, 1]
        part = m.sb("part", [P, D * LB * (L - 1)])
        red = m.sb("red", [P, D, LB])
        whole = m.sb("whole", [P, TH])
        end = m.sb("end", [P, LB])
        xv = m.sb("xv", [P, 2, R, W])
        decay = m.sb("decay", [P, 2, WB])
        St = m.sb("state", [P, R, D])
        p1 = m.sb("p1", [P, 2, R, L, D + 1])
        p2 = m.sb("p2", [P, R, D, L + 1])
        norm = sumsq
        norm_rows = part[0:NT, 0:P]
        ps_norm = m.ps("ps_norm", [P, P])
        s_norm = m.sem("norm")
        s_inv = m.sem("inverse_norm")
        s_turn = m.sem("norms_turned")
        s_rows = m.sem("norm_rows")
        s_nout = m.sem("norms_stored")
        s_in = m.sem("loaded")
        s_one = m.sem("ones")
        s_scaled = m.sem("k_scaled")
        s_kout = m.sem("k_stored")
        s_chain = m.sem("chain")
        s_ready = m.sem("solved")
        s_win = m.sems("window_loaded", 2)
        s_step = m.sems("step", 2)
        s_sig = m.sem("sigmoids")
        s_addend = m.sem("addend")
        s_decayed = m.sem("decayed")
        s_uout = m.sems("u_stored", 2)
        s_chan = m.sem("channels_loaded")
        s_kchan = m.sem("k_channels_loaded")
        HALF = P // 2
        LOADS = 2 * 4
        STEP = 4
        block = m.block()

        def of_half(a, th):
            return a.rearrange("(h d) (b x t) -> x b h d t", h=H, b=B, x=2)[th]

        lanes = [slice(HALF * th, HALF * (th + 1)) for th in range(2)]

        @block.sync
        def _(sp):
            for th, lane in enumerate(lanes):
                sp.dma_start(k[lane, :, :], of_half(scr.qkv[1], th)).then_inc(s_in, 16)
                for i in range(2):
                    sp.dma_start(ab[lane, i, :], scr.ab[i].rearrange("h (b x t) -> x b h t", b=B, x=2)[th]
                                 ).then_inc(s_in, 16)
            sp.wait_ge(s_rows, 1)
            sp.dma_start(scr.k_scale.rearrange("(t p) -> t p", p=P), norm_rows).then_inc(s_nout, 16)
            sp.wait_ge(s_nout, 16)
            for th, lane in enumerate(lanes):
                sp.dma_start(k_scale[lane, :], scr.k_scale.rearrange("(b x t) -> x b t", b=B, x=2)[th]
                             .unsqueeze(1).to_broadcast([B, H, TH])).then_inc(s_in, 16)
            sp.dma_start(q[:, :], scr.qkv[0]).then_inc(s_chan, 16)
            sp.dma_start(a_chan[:, :], scr.ab[0].unsqueeze(1).to_broadcast([H, D, N])).then_inc(s_chan, 16)
            sp.wait_ge(s_scaled, 1)
            for th, lane in enumerate(lanes):
                sp.dma_start(of_half(scr.k, th), k[lane, :, :]).then_inc(s_kout, 16)
            sp.wait_ge(s_kout, 16 * 2)
            sp.dma_start(k_chan[:, :], scr.k).then_inc(s_kchan, 16)

            def store_u(w):
                p = w % 2
                for r in range(2):
                    sp.wait_ge(s_step[r], STEP * WB * (w + 1))
                for dh in range(2):
                    for b in range(B):
                        lane = slice(HALF * dh + H * b, HALF * dh + H * (b + 1))
                        tok = slice(b * S + w * W, b * S + (w + 1) * W)
                        sp.dma_start(scr.u[:, tok].rearrange("(h d) t -> h d t", h=H)[:, dh * R:(dh + 1) * R, :],
                                     xv[lane, p, :, :]).then_inc(s_uout[p], 16)

            sp.wait_ge(s_ready, 1)
            for w in range(NW):
                p, n = w % 2, w // 2
                if n:
                    sp.wait_ge(s_uout[p], 16 * 2 * B * n)
                src = slice(HALF * (w * W // TH), HALF * (w * W // TH + 1))
                t0 = w * W % TH
                tok, blocks = slice(t0, t0 + W), slice(t0 // L, t0 // L + WB)
                for dh in range(2):
                    dst = slice(HALF * dh, HALF * (dh + 1))
                    sp.dma_start(xw[dst, p, :, :], X[src, D:2 * D, tok]).then_inc(s_win[p], 16)
                    sp.dma_start(kd[dst, p, :, :], k[src, :, tok]).then_inc(s_win[p], 16)
                    sp.dma_start(xv[dst, p, :, :], X[src, dh * R:(dh + 1) * R, tok]).then_inc(s_win[p], 16)
                    sp.dma_start(decay[dst, p, :], end[src, blocks]).then_inc(s_win[p], 16)
                if w:
                    store_u(w - 1)
            store_u(NW - 1)
            for p in range(2):
                sp.wait_ge(s_uout[p], 16 * 2 * B * (NW // 2))
            sp.wait_ge(s_chan, 32)
            sp.wait_ge(s_kchan, 16)

        @block.gpsimd
        def _(pool):
            pool.memset(dec[:, :, :, :], 1.0).then_inc(s_one, 1)
            pool.wait_ge(s_one, 1)
            pool.memset(St[:, :, :], 0.0).then_inc(s_one, 1)

        @block.tensor
        def _(pe):
            pe.wait_ge(s_inv, 2)
            pe.transpose(ps_norm[0:NT, :], norm[:, 1, :], g.ident[:, :]).then_inc(s_turn, 1)

        @block.vector
        def _(dve):
            norms = Count(dve, s_inv)
            dve.wait_ge(s_norm, 1)
            norms.done(dve.tensor_scalar(norm[:, :, :], norm[:, :, :], L2_EPS, None, ALU.add))
            norms.done(dve.reciprocal(norm[:, :, :], norm[:, :, :]))
            dve.tensor_copy(q_scale[:, :], norm[:, 0, :])
            dve.wait_ge(s_turn, 1)
            dve.tensor_copy(norm_rows, ps_norm[0:NT, :]).then_inc(s_rows, 1)

            chain = Count(dve, s_chain)
            byblock = lambda a: a.rearrange("p (c j) -> p c j", j=L)
            a3, b3, w3 = byblock(ab[:, 0, :]), byblock(ab[:, 1, :]), byblock(whole[:, :])
            k4 = k[:, :, :].rearrange("p e (c j) -> p e c j", j=L)
            X4 = X[:, :, :].rearrange("p r (c j) -> p r c j", j=L)
            lanes = lambda a, n: a.unsqueeze(1).to_broadcast([P, n, TH])
            dve.wait_ge(s_one, 2)
            dve.wait_ge(s_in, 16 * 10)
            dve.wait_ge(s_sig, 1)
            dve.tensor_tensor(k[:, :, :], k[:, :, :], lanes(k_scale[:, :], D), ALU.mult).then_inc(s_scaled, 1)
            dve.tensor_tensor(X[:, 0:D, :], X[:, 0:D, :], lanes(ab[:, 1, :], D), ALU.mult)
            for t in range(1, L):
                chain.done(dve.tensor_tensor(dec[:, t, :, 0:t], dec[:, t - 1, :, 0:t],
                                             a3[:, :, t:t + 1].to_broadcast([P, LB, t]), ALU.mult))
            chain.done(dve.tensor_tensor(w3, dec[:, :, :, 0].rearrange("p t c -> p c t"),
                                         a3[:, :, 0:1].to_broadcast([P, LB, L]), ALU.mult))
            dve.tensor_copy(end[:, :], w3[:, :, L - 1])
            dve.wait_ge(s_scaled, 1)
            chain.done(dve.scalar_tensor_tensor(out=k_scale[:, :], in0=whole[:, :], scalar=-1.0,
                                                in1=ab[:, 1, :], op0=ALU.mult, op1=ALU.mult))
            chain.done(dve.tensor_tensor(X[:, D:2 * D, :], k[:, :, :], lanes(k_scale[:, :], D), ALU.mult))
            for t in range(1, L):
                prod = part[:, 0:LB * t * D].rearrange("p (c i e) -> p c i e", c=LB, e=D)
                at_t = k4[:, :, :, t].rearrange("p e c -> p c e").unsqueeze(2).to_broadcast([P, LB, t, D])
                chain.done(dve.tensor_tensor(prod, k4[:, :, :, 0:t].rearrange("p e c i -> p c i e"), at_t,
                                             ALU.mult))
                Mt = M[:, t, :, 0:t]
                chain.done(dve.tensor_reduce(Mt, prod, AX.X, ALU.add))
                chain.done(dve.tensor_tensor(Mt, Mt, dec[:, t, :, 0:t], ALU.mult))
                chain.done(dve.tensor_tensor(Mt, Mt, b3[:, :, t:t + 1].to_broadcast([P, LB, t]), ALU.mult))
            for t in range(1, L):
                prod = part[:, 0:D * LB * t].rearrange("p (r c i) -> p r c i", r=D, c=LB)
                for rows in (slice(0, D), slice(D, 2 * D)):
                    chain.done(dve.tensor_tensor(prod, X4[:, rows, :, 0:t],
                                                 M[:, t, :, 0:t].unsqueeze(1).to_broadcast([P, D, LB, t]),
                                                 ALU.mult))
                    chain.done(dve.tensor_reduce(red[:, :, :], prod, AX.X, ALU.add))
                    chain.done(dve.tensor_tensor(X4[:, rows, :, t], X4[:, rows, :, t], red[:, :, :],
                                                 ALU.subtract))
            dve.wait_ge(s_kout, 16 * 2)
            dve.tensor_tensor(k4, k4, dec[:, L - 1, :, :].unsqueeze(1).to_broadcast([P, D, LB, L]),
                              ALU.mult).then_inc(s_ready, 1)

            def body(i):
                halves = [slice(r * R // 2, (r + 1) * R // 2) for r in range(2)]
                for p in range(2):
                    dve.wait_ge(s_win[p], 16 * LOADS * (i + 1))
                    for c in range(WB):
                        n = WB * (2 * i + p) + c
                        tok = slice(c * L, (c + 1) * L)
                        xw_t = xw[:, p, :, tok].rearrange("p e i -> p i e")
                        kd_t = kd[:, p, :, tok]
                        for r, rows in enumerate(halves):
                            wait_used(dve, s_step[r], STEP * n)
                            dve.tensor_tensor(p1[:, c % 2, rows, :, 0:D],
                                              St[:, rows, :].unsqueeze(2).to_broadcast([P, R // 2, L, D]),
                                              xw_t.unsqueeze(1).to_broadcast([P, R // 2, L, D]), ALU.mult
                                              ).then_inc(s_step[r], 1)
                        dve.wait_ge(s_addend, n + 1)
                        for r, rows in enumerate(halves):
                            dve.wait_ge(s_step[r], STEP * n + 1)
                            dve.tensor_reduce(xv[:, p, rows, tok], p1[:, c % 2, rows, :, :], AX.X, ALU.add
                                              ).then_inc(s_step[r], 1)
                        for r, rows in enumerate(halves):
                            dve.wait_ge(s_step[r], STEP * n + 2)
                            dve.tensor_tensor(p2[:, rows, :, 0:L],
                                              xv[:, p, rows, tok].unsqueeze(2).to_broadcast([P, R // 2, D, L]),
                                              kd_t.unsqueeze(1).to_broadcast([P, R // 2, D, L]), ALU.mult
                                              ).then_inc(s_step[r], 1)
                        dve.wait_ge(s_decayed, n + 1)
                        for r, rows in enumerate(halves):
                            dve.wait_ge(s_step[r], STEP * n + 3)
                            dve.tensor_reduce(St[:, rows, :], p2[:, rows, :, :], AX.X, ALU.add
                                              ).then_inc(s_step[r], 1)
            repeat(dve, NW // 2, body)

        @block.scalar
        def _(act):
            def body(i):
                for p in range(2):
                    act.wait_ge(s_win[p], 16 * LOADS * (i + 1))
                    for c in range(WB):
                        n = WB * (2 * i + p) + c
                        if c == 0:
                            add_x(p, n, c)
                        wait_used(act, s_step[1], STEP * n)
                        if isinstance(n, int) and n == 0:
                            act.wait_ge(s_one, 2)
                        act.activation(p2[:, :, :, L], St[:, :, :], ACT.Copy, scale=decay[:, p, c:c + 1]
                                       ).then_inc(s_decayed, 1)
                        if c + 1 < WB:
                            add_x(p, n + 1, c + 1)

            act.activation(norm[:, :, :], sumsq[:, :, :], ACT.Sqrt).then_inc(s_norm, 1)
            for th, lane in enumerate(lanes):
                act.dma_start(X[lane, 0:D, :], of_half(scr.qkv[2], th)).then_inc(s_in, 16)
            act.wait_ge(s_in, 16 * 10)
            act.activation(ab[:, :, :], ab[:, :, :], ACT.Sigmoid).then_inc(s_sig, 1)
            act.wait_ge(s_chan, 32)
            act.activation(a_chan[:, :], a_chan[:, :], ACT.Sigmoid)

            def add_x(p, n, c):
                wait_used(act, s_step[1], STEP * (n - 2) + 2)
                act.activation(p1[:, c % 2, :, :, D], xv[:, p, :, c * L:(c + 1) * L], ACT.Copy
                               ).then_inc(s_addend, 1)
            repeat(act, NW // 2, body)


def delta_out(nc, g, scr, q_scale, q, k, a):
    with ExitStack() as ctx:
        m = Mem(nc, ctx, "out")
        u = m.sb("u", [P, N])
        same = m.sb("same", [P, H, D])
        rowsel = m.sb("rowsel", [P, D])
        spread = m.sb("spread", [P, D, P])
        gather = m.sb("gather", [P, D, H, D])
        bo = m.sb("bo", [P, P])
        kd = m.sb("kd", [P, 2, S])
        St = m.sb("St", [P, 2, S])
        qS = m.sb("qS", [P, 2, S])
        oT = m.sb("oT", [P, S])
        ps_k = [m.ps(f"ps_k{p}", [P, S]) for p in range(2)]
        ps_o = m.ps("ps_o", [P, S])
        ps_y = [m.ps(f"ps_y{i}", [P, CT, P]) for i in range(2)]
        s_in = m.sems("loaded", 4)
        s_same = m.sem("same")
        s_sel = m.sem("selectors")
        s_bo = m.sem("bo")
        s_bias = m.sem("bias_added")
        s_k = m.sem("k_spread")
        s_kd = m.sem("kd")
        s_S = m.sem("S")
        s_qS = m.sem("qS")
        s_o = m.sem("o")
        s_oT = m.sem("oT")
        s_y = m.sem("y")
        s_add = m.sem("added")
        block = m.block()

        @block.sync
        def _(sp):
            for b in range(B):
                tok = slice(b * S, (b + 1) * S)
                sp.dma_start(u[:, tok], scr.u[:, tok]).then_inc(s_in[b], 16)

        @block.gpsimd
        def _(pool):
            pool.memset(same[:, :, :], 1.0).then_inc(s_same, 1)
            pool.wait_ge(s_same, 1)
            pool.affine_select(out=same[:, :, :], in_=same[:, :, :], compare_op=ALU.is_ge, fill=0.0, base=0,
                               pattern=[[-D, H], [0, D]], channel_multiplier=1).then_inc(s_same, 1)
            pool.wait_ge(s_same, 2)
            pool.affine_select(out=same[:, :, :], in_=same[:, :, :], compare_op=ALU.is_ge, fill=0.0, base=D - 1,
                               pattern=[[D, H], [0, D]], channel_multiplier=-1).then_inc(s_same, 1)
            pool.wait_ge(s_same, 3)
            pool.memset(gather[:, :, :, :], 0.0).then_inc(s_same, 1)

        @block.tensor
        def _(pe):
            pe.matmul(ps_y[0][:, 0, :], g.ones[0:1, :], g.bo_row[:, :], start=True, stop=True).then_inc(s_bo, 1)
            pe.wait_ge(s_sel, 2 * D + 1)
            pe.wait_ge(s_bias, 1)

            def spread_k(b, e):
                n = D * b + e
                wait_used(pe, s_kd, n - 1)
                for i in range(2):
                    mm = pe.matmul(ps_k[e % 2][:, i * CH:(i + 1) * CH], spread[:, e, :],
                                   k[:, bass.ds(b * S + i * CH, CH)], start=True, stop=True)
                mm.then_inc(s_k, 1)

            def sum_o(b, e):
                n = D * b + e
                pe.wait_ge(s_qS, n + 1)
                if e == 0:
                    wait_used(pe, s_oT, b)
                for i in range(2):
                    mm = pe.matmul(ps_o[:, i * CH:(i + 1) * CH], gather[:, e, :, :].rearrange("p h d -> p (h d)"),
                                   qS[:, e % 2, i * CH:(i + 1) * CH], start=(e == 0), stop=(e == D - 1))
                mm.then_inc(s_o, 1)

            def project(b):
                pe.wait_ge(s_oT, b + 1)
                wait_used(pe, s_add, b)
                for t in range(TB):
                    mm = pe.matmul(ps_y[t // CT][:, t % CT, :], oT[:, t * P:(t + 1) * P], g.wT[:, 7, :],
                                   start=True, stop=True)
                mm.then_inc(s_y, 1)

            def body(b):
                before = not (isinstance(b, int) and b == 0)
                for e in range(D):
                    spread_k(b, e)
                    if e >= 2:
                        sum_o(b, e - 2)
                    elif before:
                        sum_o(b - 1, D - 2 + e)
                    if e == 2 and before:
                        project(b - 1)
            repeat(pe, B, body)
            sum_o(B - 1, D - 2)
            sum_o(B - 1, D - 1)
            project(B - 1)

        @block.vector
        def _(dve):
            dve.wait_ge(s_bo, 1)
            dve.tensor_copy(bo[:, :], ps_y[0][:, 0, :]).then_inc(s_bias, 1)
            dve.wait_ge(s_bias, 1)
            dve.tensor_tensor(g.x[:, :, :], g.x[:, :, :], bo[:, :].unsqueeze(1).to_broadcast([P, NT, P]), ALU.add)
            dve.wait_ge(s_same, 4)
            dve.tensor_reduce(rowsel[:, :], g.ident[:, :].rearrange("p (h e) -> p e h", h=H), AX.X,
                              ALU.add).then_inc(s_sel, 1)
            dve.wait_ge(s_sel, 1)
            for e in range(D):
                dve.tensor_scalar(spread[:, e, :], same[:, :, :].rearrange("p h d -> p (h d)"),
                                  rowsel[:, e:e + 1], None, ALU.mult).then_inc(s_sel, 1)
                dve.tensor_copy(gather[:, e, :, e], same[:, :, e]).then_inc(s_sel, 1)
            for b in range(B):
                dve.wait_ge(s_in[b], 16)

            def spread_u(b, e):
                n = D * b + e
                dve.wait_ge(s_k, n + 1)
                dve.tensor_tensor(kd[:, e % 2, :], u[:, bass.ds(b * S, S)], ps_k[e % 2][:, :],
                                  ALU.mult).then_inc(s_kd, 1)

            def add(b):
                dve.wait_ge(s_y, b + 1)
                for t in range(TB):
                    xt = g.x[:, bass.ds(b * TB + t, 1), :].rearrange("p o c -> p (o c)")
                    ins = dve.scalar_tensor_tensor(out=xt, in0=ps_y[t // CT][:, t % CT, :],
                                                   scalar=q_scale[:, bass.ds(b * TB + t, 1)], in1=xt,
                                                   op0=ALU.mult, op1=ALU.add)
                ins.then_inc(s_add, 1)
                dve.wait_ge(s_add, b + 1)
                for t in range(TB):
                    bn_stats_of(nc, g, b * TB + t)

            def body(b):
                tok = bass.ds(b * S, S)
                spread_u(b, 0)
                for e in range(D):
                    n = D * b + e
                    dve.wait_ge(s_kd, n + 1)
                    dve.tensor_tensor_scan(St[:, e % 2, :], a[:, tok], kd[:, e % 2, :], 0.0, ALU.mult,
                                           ALU.add).then_inc(s_S, 1)
                    if e < D - 1:
                        spread_u(b, e + 1)
                    dve.wait_ge(s_S, n + 1)
                    wait_used(dve, s_o, n - 1)
                    dve.tensor_tensor(qS[:, e % 2, :], q[:, tok], St[:, e % 2, :], ALU.mult).then_inc(s_qS, 1)
                    if e == 3 and not (isinstance(b, int) and b == 0):
                        add(b - 1)
            repeat(dve, B, body)
            add(B - 1)

        @block.scalar
        def _(act):
            def body(b):
                act.wait_ge(s_o, D * (b + 1))
                wait_used(act, s_y, b)
                for i in range(2):
                    ins = act.activation(oT[:, i * CH:(i + 1) * CH], ps_o[:, i * CH:(i + 1) * CH], ACT.Copy)
                ins.then_inc(s_oT, 1)
            repeat(act, B, body)


class Shared:
    pass


def store(nc, out, x, name):
    with nc.semaphore(name) as s_out, nc.Block() as block:
        @block.sync
        def _(sp):
            sp.dma_start(out.rearrange("b (t p) c -> p (b t) c", p=P), x[:, :, :]).then_inc(s_out, 16)
            sp.wait_ge(s_out, 16)


def build(nc, ins, out, stop=None):
    g, scr = Shared(), Shared()
    scr.terms = [nc.dram_tensor(f"terms_{w}", (NPART, K1, H, N), BF16, kind="Internal").ap() for w in "qk"]
    scr.qkv = [nc.dram_tensor(f"delta_{w}", (P, N), F32, kind="Internal").ap() for w in "qkv"]
    scr.ab = nc.dram_tensor("delta_ab", (2, H, N), F32, kind="Internal").ap()
    scr.k_scale = nc.dram_tensor("delta_k_scale", (N,), F32, kind="Internal").ap()
    scr.k = nc.dram_tensor("delta_k_normed", (P, N), F32, kind="Internal").ap()
    scr.u = nc.dram_tensor("delta_u", (P, N), F32, kind="Internal").ap()
    with ExitStack() as ctx:
        m = Mem(nc, ctx, "all")
        g.x = m.sb("x", [P, NT, P])
        g.ident = m.sb("ident", [P, P])
        g.ones = m.sb("ones", [P, P])
        g.varsel = m.sb("varsel", [P, 2, 48])
        g.wT = m.sb("wT", [P, 8, P])
        g.gatesT = m.sb("gatesT", [P, 48])
        g.bias_qkv = m.sb("bias_qkv", [P, 3])
        g.conv = m.sb("conv", [P, 3, K])
        g.bias_ab = m.sb("bias_ab", [48, 1])
        g.bo_row = m.sb("bo_row", [1, P])
        g.gate_w = m.sb("gate_w", [P, E])
        g.w1 = m.sb("w1", [P, E, F])
        g.w3 = m.sb("w3", [P, E, F])
        g.w2 = m.sb("w2", [P, E, MF, P])
        g.s_experts = m.sem("experts_loaded")
        g.stats = m.sb("stats", [P, NT, 6])
        g.rstd = m.sb("rstd", [P, NT])
        g.nmr = m.sb("nmr", [P, NT])
        load_and_turn_weights(nc, g, ins)
        layer_norm_scales(nc, g, "ln_a")
        with ExitStack() as actx:
            ma = Mem(nc, actx, "a")
            g.o = ma.sb("o", [P, NT, P])
            with ExitStack() as vctx:
                mv = Mem(nc, vctx, "av")
                g.v1 = mv.sb("v1", [P, NT, H, VW])
                g.q_op = [mv.sb(f"q_op{s}", [P, GH, S], BF16) for s in range(NQ)]
                g.k_op = [mv.sb(f"k_op{s}", [P, GH, S], BF16) for s in range(NQ)]
                project_qkv(nc, g, scr)
                attend(nc, g, scr)
            if stop == "o":
                return store(nc, out, g.o, "dbg")
            project_out_a(nc, g, ins)
        if stop == "x1":
            return store(nc, out, g.x, "dbg")
        moe_layer(nc, g, ins, "moe1", True)
        if stop == "x2":
            return store(nc, out, g.x, "dbg")
        with ExitStack() as bctx:
            mb = Mem(nc, bctx, "b")
            q_scale = mb.sb("q_scale", [P, NT])
            sumsq = mb.sb("sumsq", [P, 2, NT])
            layer_norm_scales(nc, g, "ln_b")
            project_conv(nc, g, scr, sumsq)
            q = mb.sb("q", [P, N])
            k = mb.sb("k", [P, N])
            a = mb.sb("a", [P, N])
            solve_and_scan(nc, g, scr, sumsq, q_scale, q, k, a)
            delta_out(nc, g, scr, q_scale, q, k, a)
        if stop == "x3":
            return store(nc, out, g.x, "dbg")
        moe_layer(nc, g, ins, "moe2", False)
        store(nc, out, g.x, "stored_out")


_INS = ["a_x", "a_Wq", "a_Wk", "a_Wv", "a_Wo", "b_Wq", "b_bq", "b_Wk", "b_bk", "b_Wv", "b_bv", "b_Wa", "b_ba",
        "b_Wb", "b_bb", "b_conv_q", "b_conv_k", "b_conv_v", "b_Wo", "b_bo", "f_gate_w", "f_w1", "f_w2", "f_w3"]
_LAYERS = {"a": "L0_attn_a_", "b": "L0_attn_b_", "f": "L0_ffn_"}


def kernel(**inputs):
    import numpy as np
    import concourse.bacc as bacc
    from concourse.bass_utils import run_bass_kernel_spmd

    nc = bacc.Bacc("TRN2", target_bir_lowering=False, num_devices=1)
    arrays, ins = {}, {}
    for name in _INS:
        a = np.ascontiguousarray(inputs[_LAYERS[name[0]] + name[2:]])
        arrays[f"in_{name}"] = a
        ins[name] = nc.dram_tensor(f"in_{name}", a.shape, mybir.dt.from_np(a.dtype), kind="ExternalInput").ap()
    out = nc.dram_tensor("out_x", (B, S, P), F32, kind="ExternalOutput").ap()
    build(nc, ins, out)
    r = run_bass_kernel_spmd(nc, [arrays], core_ids=[0])
    return r.results[0]["out_x"]
```
